# Optimizing a Trainium2 kernel written in Bass

```python
import numpy as np
import jax
import jax.numpy as jnp

def _softmax(x, axis=-1):
    return jax.nn.softmax(x, axis=axis)

def _gelu(x):
    return jax.nn.gelu(x, approximate=True)

def _silu(x):
    return jax.nn.silu(x)

def _sigmoid(x):
    return jax.nn.sigmoid(x)

def _layernorm(x, axis=-1, eps=1e-05):
    m = jnp.mean(x, axis=axis, keepdims=True)
    v = jnp.var(x, axis=axis, keepdims=True)
    return (x - m) / jnp.sqrt(v + eps)

def _scatter_add(tgt, idx, src, axis=0):
    return tgt.at[idx].add(src)

def _segment_sum(src, seg, n):
    return jax.ops.segment_sum(src, seg, n)
kernel_name = 'mk_adaln_ffn_d2_seqx_r4_1f9117'

def setup_inputs(seed: int=0):
    np.random.seed(seed)
    _w = jnp.asarray

    def _rec_inputs():
        import jax
        import jax.numpy as jnp
        _rk = jax.random.key(seed)
        x = -0.000125 + 0.9999 * jax.random.normal(jax.random.fold_in(_rk, 1), (4, 512, 512), jnp.float32)
        _lenS = 512 - jax.random.randint(jax.random.fold_in(_rk, 7), (4,), 0, max(1, 512 // 4) + 1, jnp.int32)
        _lenS2 = 512 - jax.random.randint(jax.random.fold_in(_rk, 8), (4,), 0, max(1, 512 // 4) + 1, jnp.int32)
        fside_BxSxS_0 = -1.52775e-05 + 0.999936 * jax.random.normal(jax.random.fold_in(_rk, 11), (4, 512, 512), jnp.float32)
        cond_512 = -5.03954e-05 + 1.00559 * jax.random.normal(jax.random.fold_in(_rk, 12), (4, 128), jnp.float32)
        return (x, fside_BxSxS_0, cond_512)
    x, fside_BxSxS_0, cond_512 = _rec_inputs()

    def _L0_cond_setup():
        import jax, jax.numpy as jnp
        from jax import lax
        import numpy as np
        B, T, C, TD = (8, 512, 512, 128)

        def _bi_wkv(r, k, v, w, u, time_emb):
            tf = jax.nn.sigmoid(jnp.sum(time_emb, axis=-1))[:, None, None]
            decay = jnp.exp(-jnp.exp(w.astype(jnp.float32)))[None, :] * (0.5 + 0.5 * tf[:, :, 0])
            kf = k.astype(jnp.float32)
            vf = v.astype(jnp.float32)
            ek = jnp.exp(jnp.minimum(kf, 30.0))
            ekv = ek * vf

            def step(carry, x):
                a, b = carry
                ekv_t, ek_t = x
                a = a * decay + ekv_t
                b = b * decay + ek_t
                return ((a, b), (a, b))
            ekv_t = jnp.swapaxes(ekv, 0, 1)
            ek_t = jnp.swapaxes(ek, 0, 1)
            init = (jnp.zeros_like(decay), jnp.zeros_like(decay))
            _, (nf, df) = lax.scan(step, init, (ekv_t, ek_t))
            _, (nb, db) = lax.scan(step, init, (ekv_t, ek_t), reverse=True)
            nf = jnp.swapaxes(nf, 0, 1)
            df = jnp.swapaxes(df, 0, 1)
            nb = jnp.swapaxes(nb, 0, 1)
            db = jnp.swapaxes(db, 0, 1)
            euk = jnp.exp(jnp.minimum(u.astype(jnp.float32)[None, None, :] + kf, 30.0))
            num = nf + nb - ekv + euk * vf
            den = df + db - ek + euk
            base = jax.nn.sigmoid(r.astype(jnp.float32)) * (num / jnp.maximum(den, 1e-08))
            out = base * (0.8 + 0.2 * tf)
            return out.astype(r.dtype)
        key = jax.random.key(seed)
        ks = jax.random.split(key, 6)
        return {'r': jax.random.normal(ks[0], (B, T, C), dtype=jnp.float32), 'k': jax.random.normal(ks[1], (B, T, C), dtype=jnp.float32), 'v': jax.random.normal(ks[2], (B, T, C), dtype=jnp.float32), 'w': jax.random.normal(ks[3], (C,), dtype=jnp.float32), 'u': jax.random.normal(ks[4], (C,), dtype=jnp.float32), 'time_emb': jax.random.normal(ks[5], (B, TD), dtype=jnp.float32)}
    _L0_cond_all = _L0_cond_setup()
    _L0_cond_in = {k: v for k, v in _L0_cond_all.items() if k in ('w', 'u')}
    del _L0_cond_all

    def _L0_ffn_setup():
        import jax, jax.numpy as jnp
        import numpy as np
        _FP4_LUT = jnp.array([0.0, 0.5, 1.0, 1.5, 2.0, 3.0, 4.0, 6.0, -0.0, -0.5, -1.0, -1.5, -2.0, -3.0, -4.0, -6.0], dtype=jnp.float32)
        GROUP_SIZE = 128
        EPS = 1e-06

        def _dequant_fp4(packed_i32, scales_f16, group_size):
            out_f, in_p = packed_i32.shape
            w = packed_i32.astype(jnp.uint32)
            shifts = jnp.arange(8, dtype=jnp.uint32) * 4
            nib = w[:, :, None] >> shifts & jnp.uint32(15)
            vals = _FP4_LUT[nib.astype(jnp.int32)].reshape(out_f, in_p * 8)
            s = scales_f16.astype(jnp.float32).T
            s_full = jnp.repeat(s, group_size, axis=1)
            return vals * s_full
        key = jax.random.key(seed)
        k1, k2, k3, k4, k5 = jax.random.split(key, 5)
        B, S, H, I = (4, 512, 512, 1408)
        x = jax.random.normal(k1, (B, S, H), dtype=jnp.float32)
        gate_up_packed = jax.random.randint(k2, (2 * I, H // 8), 0, 2147483647, dtype=jnp.int32)
        gate_up_scales = jax.random.uniform(k3, (H // GROUP_SIZE, 2 * I), dtype=jnp.float32).astype(jnp.float16)
        down_packed = jax.random.randint(k4, (H, I // 8), 0, 2147483647, dtype=jnp.int32)
        down_scales = jax.random.uniform(k5, (I // GROUP_SIZE, H), dtype=jnp.float32).astype(jnp.float16)
        return {'x': x, 'gate_up_packed': gate_up_packed, 'gate_up_scales': gate_up_scales, 'down_packed': down_packed, 'down_scales': down_scales}
    _L0_ffn_all = _L0_ffn_setup()
    _L0_ffn_in = {k: v for k, v in _L0_ffn_all.items() if k in ('gate_up_packed', 'gate_up_scales', 'down_packed', 'down_scales')}
    del _L0_ffn_all

    def _L1_cond_setup():
        import jax, jax.numpy as jnp
        from jax import lax
        import numpy as np
        B, T, C, TD = (8, 512, 512, 128)

        def _bi_wkv(r, k, v, w, u, time_emb):
            tf = jax.nn.sigmoid(jnp.sum(time_emb, axis=-1))[:, None, None]
            decay = jnp.exp(-jnp.exp(w.astype(jnp.float32)))[None, :] * (0.5 + 0.5 * tf[:, :, 0])
            kf = k.astype(jnp.float32)
            vf = v.astype(jnp.float32)
            ek = jnp.exp(jnp.minimum(kf, 30.0))
            ekv = ek * vf

            def step(carry, x):
                a, b = carry
                ekv_t, ek_t = x
                a = a * decay + ekv_t
                b = b * decay + ek_t
                return ((a, b), (a, b))
            ekv_t = jnp.swapaxes(ekv, 0, 1)
            ek_t = jnp.swapaxes(ek, 0, 1)
            init = (jnp.zeros_like(decay), jnp.zeros_like(decay))
            _, (nf, df) = lax.scan(step, init, (ekv_t, ek_t))
            _, (nb, db) = lax.scan(step, init, (ekv_t, ek_t), reverse=True)
            nf = jnp.swapaxes(nf, 0, 1)
            df = jnp.swapaxes(df, 0, 1)
            nb = jnp.swapaxes(nb, 0, 1)
            db = jnp.swapaxes(db, 0, 1)
            euk = jnp.exp(jnp.minimum(u.astype(jnp.float32)[None, None, :] + kf, 30.0))
            num = nf + nb - ekv + euk * vf
            den = df + db - ek + euk
            base = jax.nn.sigmoid(r.astype(jnp.float32)) * (num / jnp.maximum(den, 1e-08))
            out = base * (0.8 + 0.2 * tf)
            return out.astype(r.dtype)
        key = jax.random.key(seed)
        ks = jax.random.split(key, 6)
        return {'r': jax.random.normal(ks[0], (B, T, C), dtype=jnp.float32), 'k': jax.random.normal(ks[1], (B, T, C), dtype=jnp.float32), 'v': jax.random.normal(ks[2], (B, T, C), dtype=jnp.float32), 'w': jax.random.normal(ks[3], (C,), dtype=jnp.float32), 'u': jax.random.normal(ks[4], (C,), dtype=jnp.float32), 'time_emb': jax.random.normal(ks[5], (B, TD), dtype=jnp.float32)}
    _L1_cond_all = _L1_cond_setup()
    _L1_cond_in = {k: v for k, v in _L1_cond_all.items() if k in ('w', 'u')}
    del _L1_cond_all

    def _L1_ffn_setup():
        import jax, jax.numpy as jnp
        import numpy as np
        D_MODEL = 512
        NUM_TILES = 64
        D_SLICE = D_MODEL // NUM_TILES
        TILES_PER_CLUSTER = 8
        NUM_CLUSTERS = NUM_TILES // TILES_PER_CLUSTER
        GRID = 16
        LN_EPS = 1e-05
        DIMS = (np.arange(NUM_TILES)[:, None] * D_SLICE + np.arange(D_SLICE)[None, :]) % D_MODEL
        DIMS = jnp.asarray(DIMS, dtype=jnp.int32)

        def _forward(x, ln_gamma, ln_beta, spline_bases, spline_slopes, output_scale):
            B, S, D = x.shape
            N = B * S
            mu = jnp.mean(x, axis=-1, keepdims=True)
            var = jnp.mean(jnp.square(x - mu), axis=-1, keepdims=True)
            xn = (x - mu) * jax.lax.rsqrt(var + LN_EPS) * ln_gamma + ln_beta
            xf = xn.reshape(N, D)
            slope_sign = jnp.sign(jnp.mean(spline_slopes, axis=-1))
            tile_sigs = jnp.zeros((NUM_TILES, D), dtype=x.dtype)
            tile_sigs = tile_sigs.at[jnp.arange(NUM_TILES)[:, None], DIMS].set(slope_sign)
            cluster_sigs = jnp.sign(tile_sigs.reshape(NUM_CLUSTERS, TILES_PER_CLUSTER, D).mean(axis=1))
            cluster_assign = jnp.arange(NUM_TILES, dtype=jnp.int32) // TILES_PER_CLUSTER
            input_sigs = jnp.sign(xf)
            cluster_scores = input_sigs @ cluster_sigs.T
            best_cluster = jnp.argmax(cluster_scores, axis=-1)
            tile_scores = input_sigs @ tile_sigs.T
            in_cluster = cluster_assign[None, :] == best_cluster[:, None]
            tile_idx = jnp.argmax(jnp.where(in_cluster, tile_scores, -jnp.inf), axis=-1)
            tok_dims = DIMS[tile_idx]
            x_slice = jnp.take_along_axis(xf, tok_dims, axis=1)
            tok_min = x_slice.min(axis=1)
            tok_max = x_slice.max(axis=1)
            onehot = tile_idx[None, :] == jnp.arange(NUM_TILES)[:, None]
            tile_min = jnp.where(onehot, tok_min[None, :], jnp.inf).min(axis=1)
            tile_max = jnp.where(onehot, tok_max[None, :], -jnp.inf).max(axis=1)
            mn = tile_min[tile_idx][:, None]
            mx = tile_max[tile_idx][:, None]
            u = jnp.clip((x_slice - mn) / (mx - mn + 1e-08), 0.0, 1.0 - 1e-06)
            gi = jnp.clip((u * GRID).astype(jnp.int32), 0, GRID - 1)
            j = jnp.arange(D_SLICE)[None, :]
            b = spline_bases[tile_idx[:, None], j, gi]
            s = spline_slopes[tile_idx[:, None], j, gi]
            x_local = (u - gi.astype(u.dtype) / GRID) * GRID
            delta = (b + s * x_local) * output_scale[tile_idx][:, None]
            out = jnp.zeros_like(xf).at[jnp.arange(N)[:, None], tok_dims].set(delta)
            return x + out.reshape(B, S, D)
        key = jax.random.key(seed)
        k1, k2, k3, k4, k5, k6 = jax.random.split(key, 6)
        x = jax.random.normal(k1, (4, 1024, D_MODEL), dtype=jnp.float32)
        ln_gamma = 1.0 + 0.1 * jax.random.normal(k2, (D_MODEL,), dtype=jnp.float32)
        ln_beta = 0.1 * jax.random.normal(k3, (D_MODEL,), dtype=jnp.float32)
        spline_bases = 0.1 * jax.random.normal(k4, (NUM_TILES, D_SLICE, GRID), dtype=jnp.float32)
        spline_slopes = 0.1 + 0.1 * jax.random.normal(k5, (NUM_TILES, D_SLICE, GRID), dtype=jnp.float32)
        output_scale = 1.0 + 0.1 * jax.random.normal(k6, (NUM_TILES,), dtype=jnp.float32)
        return {'x': x, 'ln_gamma': ln_gamma, 'ln_beta': ln_beta, 'spline_bases': spline_bases, 'spline_slopes': spline_slopes, 'output_scale': output_scale}
    _L1_ffn_all = _L1_ffn_setup()
    _L1_ffn_in = {k: v for k, v in _L1_ffn_all.items() if k in ('ln_gamma', 'ln_beta', 'spline_bases', 'spline_slopes', 'output_scale')}
    del _L1_ffn_all
    return {'x': x, 'fside_BxSxS_0': fside_BxSxS_0, 'cond_512': cond_512, 'L0_cond_w': _L0_cond_in['w'], 'L0_cond_u': _L0_cond_in['u'], 'L0_ffn_gate_up_packed': _L0_ffn_in['gate_up_packed'], 'L0_ffn_gate_up_scales': _L0_ffn_in['gate_up_scales'], 'L0_ffn_down_packed': _L0_ffn_in['down_packed'], 'L0_ffn_down_scales': _L0_ffn_in['down_scales'], 'L1_cond_w': _L1_cond_in['w'], 'L1_cond_u': _L1_cond_in['u'], 'L1_ffn_ln_gamma': _L1_ffn_in['ln_gamma'], 'L1_ffn_ln_beta': _L1_ffn_in['ln_beta'], 'L1_ffn_spline_bases': _L1_ffn_in['spline_bases'], 'L1_ffn_spline_slopes': _L1_ffn_in['spline_slopes'], 'L1_ffn_output_scale': _L1_ffn_in['output_scale']}

def reference(x, fside_BxSxS_0, cond_512, L0_cond_w, L0_cond_u, L0_ffn_gate_up_packed, L0_ffn_gate_up_scales, L0_ffn_down_packed, L0_ffn_down_scales, L1_cond_w, L1_cond_u, L1_ffn_ln_gamma, L1_ffn_ln_beta, L1_ffn_spline_bases, L1_ffn_spline_slopes, L1_ffn_output_scale):
    import jax
    import jax.numpy as jnp

    def _L0_cond_ref(r, k, v, w, u, time_emb):
        import jax, jax.numpy as jnp
        from jax import lax
        import numpy as np
        B, T, C, TD = (8, 512, 512, 128)

        def _bi_wkv(r, k, v, w, u, time_emb):
            tf = jax.nn.sigmoid(jnp.sum(time_emb, axis=-1))[:, None, None]
            decay = jnp.exp(-jnp.exp(w.astype(jnp.float32)))[None, :] * (0.5 + 0.5 * tf[:, :, 0])
            kf = k.astype(jnp.float32)
            vf = v.astype(jnp.float32)
            ek = jnp.exp(jnp.minimum(kf, 30.0))
            ekv = ek * vf

            def step(carry, x):
                a, b = carry
                ekv_t, ek_t = x
                a = a * decay + ekv_t
                b = b * decay + ek_t
                return ((a, b), (a, b))
            ekv_t = jnp.swapaxes(ekv, 0, 1)
            ek_t = jnp.swapaxes(ek, 0, 1)
            init = (jnp.zeros_like(decay), jnp.zeros_like(decay))
            _, (nf, df) = lax.scan(step, init, (ekv_t, ek_t))
            _, (nb, db) = lax.scan(step, init, (ekv_t, ek_t), reverse=True)
            nf = jnp.swapaxes(nf, 0, 1)
            df = jnp.swapaxes(df, 0, 1)
            nb = jnp.swapaxes(nb, 0, 1)
            db = jnp.swapaxes(db, 0, 1)
            euk = jnp.exp(jnp.minimum(u.astype(jnp.float32)[None, None, :] + kf, 30.0))
            num = nf + nb - ekv + euk * vf
            den = df + db - ek + euk
            base = jax.nn.sigmoid(r.astype(jnp.float32)) * (num / jnp.maximum(den, 1e-08))
            out = base * (0.8 + 0.2 * tf)
            return out.astype(r.dtype)
        return _bi_wkv(r, k, v, w, u, time_emb)

    def _L0_ffn_ref(x, gate_up_packed, gate_up_scales, down_packed, down_scales):
        import jax, jax.numpy as jnp
        import numpy as np
        _FP4_LUT = jnp.array([0.0, 0.5, 1.0, 1.5, 2.0, 3.0, 4.0, 6.0, -0.0, -0.5, -1.0, -1.5, -2.0, -3.0, -4.0, -6.0], dtype=jnp.float32)
        GROUP_SIZE = 128
        EPS = 1e-06

        def _dequant_fp4(packed_i32, scales_f16, group_size):
            out_f, in_p = packed_i32.shape
            w = packed_i32.astype(jnp.uint32)
            shifts = jnp.arange(8, dtype=jnp.uint32) * 4
            nib = w[:, :, None] >> shifts & jnp.uint32(15)
            vals = _FP4_LUT[nib.astype(jnp.int32)].reshape(out_f, in_p * 8)
            s = scales_f16.astype(jnp.float32).T
            s_full = jnp.repeat(s, group_size, axis=1)
            return vals * s_full
        I = gate_up_packed.shape[0] // 2
        w_gu = _dequant_fp4(gate_up_packed, gate_up_scales, GROUP_SIZE)
        w_down = _dequant_fp4(down_packed, down_scales, GROUP_SIZE)
        gate_up = jnp.einsum('bsh,oh->bso', x, w_gu)
        gate, up = (gate_up[..., :I], gate_up[..., I:])
        h = jax.nn.silu(gate) * up
        y = jnp.einsum('bsi,hi->bsh', h, w_down)
        rms = jnp.sqrt(jnp.mean(y * y, axis=-1, keepdims=True) + EPS)
        return y / rms

    def _L1_cond_ref(r, k, v, w, u, time_emb):
        import jax, jax.numpy as jnp
        from jax import lax
        import numpy as np
        B, T, C, TD = (8, 512, 512, 128)

        def _bi_wkv(r, k, v, w, u, time_emb):
            tf = jax.nn.sigmoid(jnp.sum(time_emb, axis=-1))[:, None, None]
            decay = jnp.exp(-jnp.exp(w.astype(jnp.float32)))[None, :] * (0.5 + 0.5 * tf[:, :, 0])
            kf = k.astype(jnp.float32)
            vf = v.astype(jnp.float32)
            ek = jnp.exp(jnp.minimum(kf, 30.0))
            ekv = ek * vf

            def step(carry, x):
                a, b = carry
                ekv_t, ek_t = x
                a = a * decay + ekv_t
                b = b * decay + ek_t
                return ((a, b), (a, b))
            ekv_t = jnp.swapaxes(ekv, 0, 1)
            ek_t = jnp.swapaxes(ek, 0, 1)
            init = (jnp.zeros_like(decay), jnp.zeros_like(decay))
            _, (nf, df) = lax.scan(step, init, (ekv_t, ek_t))
            _, (nb, db) = lax.scan(step, init, (ekv_t, ek_t), reverse=True)
            nf = jnp.swapaxes(nf, 0, 1)
            df = jnp.swapaxes(df, 0, 1)
            nb = jnp.swapaxes(nb, 0, 1)
            db = jnp.swapaxes(db, 0, 1)
            euk = jnp.exp(jnp.minimum(u.astype(jnp.float32)[None, None, :] + kf, 30.0))
            num = nf + nb - ekv + euk * vf
            den = df + db - ek + euk
            base = jax.nn.sigmoid(r.astype(jnp.float32)) * (num / jnp.maximum(den, 1e-08))
            out = base * (0.8 + 0.2 * tf)
            return out.astype(r.dtype)
        return _bi_wkv(r, k, v, w, u, time_emb)

    def _L1_ffn_ref(x, ln_gamma, ln_beta, spline_bases, spline_slopes, output_scale):
        import jax, jax.numpy as jnp
        import numpy as np
        D_MODEL = 512
        NUM_TILES = 64
        D_SLICE = D_MODEL // NUM_TILES
        TILES_PER_CLUSTER = 8
        NUM_CLUSTERS = NUM_TILES // TILES_PER_CLUSTER
        GRID = 16
        LN_EPS = 1e-05
        DIMS = (np.arange(NUM_TILES)[:, None] * D_SLICE + np.arange(D_SLICE)[None, :]) % D_MODEL
        DIMS = jnp.asarray(DIMS, dtype=jnp.int32)

        def _forward(x, ln_gamma, ln_beta, spline_bases, spline_slopes, output_scale):
            B, S, D = x.shape
            N = B * S
            mu = jnp.mean(x, axis=-1, keepdims=True)
            var = jnp.mean(jnp.square(x - mu), axis=-1, keepdims=True)
            xn = (x - mu) * jax.lax.rsqrt(var + LN_EPS) * ln_gamma + ln_beta
            xf = xn.reshape(N, D)
            slope_sign = jnp.sign(jnp.mean(spline_slopes, axis=-1))
            tile_sigs = jnp.zeros((NUM_TILES, D), dtype=x.dtype)
            tile_sigs = tile_sigs.at[jnp.arange(NUM_TILES)[:, None], DIMS].set(slope_sign)
            cluster_sigs = jnp.sign(tile_sigs.reshape(NUM_CLUSTERS, TILES_PER_CLUSTER, D).mean(axis=1))
            cluster_assign = jnp.arange(NUM_TILES, dtype=jnp.int32) // TILES_PER_CLUSTER
            input_sigs = jnp.sign(xf)
            cluster_scores = input_sigs @ cluster_sigs.T
            best_cluster = jnp.argmax(cluster_scores, axis=-1)
            tile_scores = input_sigs @ tile_sigs.T
            in_cluster = cluster_assign[None, :] == best_cluster[:, None]
            tile_idx = jnp.argmax(jnp.where(in_cluster, tile_scores, -jnp.inf), axis=-1)
            tok_dims = DIMS[tile_idx]
            x_slice = jnp.take_along_axis(xf, tok_dims, axis=1)
            tok_min = x_slice.min(axis=1)
            tok_max = x_slice.max(axis=1)
            onehot = tile_idx[None, :] == jnp.arange(NUM_TILES)[:, None]
            tile_min = jnp.where(onehot, tok_min[None, :], jnp.inf).min(axis=1)
            tile_max = jnp.where(onehot, tok_max[None, :], -jnp.inf).max(axis=1)
            mn = tile_min[tile_idx][:, None]
            mx = tile_max[tile_idx][:, None]
            u = jnp.clip((x_slice - mn) / (mx - mn + 1e-08), 0.0, 1.0 - 1e-06)
            gi = jnp.clip((u * GRID).astype(jnp.int32), 0, GRID - 1)
            j = jnp.arange(D_SLICE)[None, :]
            b = spline_bases[tile_idx[:, None], j, gi]
            s = spline_slopes[tile_idx[:, None], j, gi]
            x_local = (u - gi.astype(u.dtype) / GRID) * GRID
            delta = (b + s * x_local) * output_scale[tile_idx][:, None]
            out = jnp.zeros_like(xf).at[jnp.arange(N)[:, None], tok_dims].set(delta)
            return x + out.reshape(B, S, D)
        return _forward(x, ln_gamma, ln_beta, spline_bases, spline_slopes, output_scale)
    x = x + _L0_ffn_ref(_L0_cond_ref(x, fside_BxSxS_0, fside_BxSxS_0, L0_cond_w, L0_cond_u, cond_512), L0_ffn_gate_up_packed, L0_ffn_gate_up_scales, L0_ffn_down_packed, L0_ffn_down_scales)
    x = x + _L1_ffn_ref(_L1_cond_ref(x, fside_BxSxS_0, fside_BxSxS_0, L1_cond_w, L1_cond_u, cond_512), L1_ffn_ln_gamma, L1_ffn_ln_beta, L1_ffn_spline_bases, L1_ffn_spline_slopes, L1_ffn_output_scale)
    return x

_drawn_inputs = setup_inputs


def setup_inputs(seed=0):
    import zlib

    import numpy as np

    out = dict(_drawn_inputs(seed))
    spreads = {}
    factors = {'L1_ffn_ln_gamma': 8.0,
     'L1_ffn_ln_beta': 6.665,
     'L1_ffn_spline_bases': 7.652,
     'L1_ffn_spline_slopes': 8.0,
     'L1_ffn_output_scale': 8.0}
    for name, (base, spread) in spreads.items():
        noise = np.random.default_rng([zlib.crc32(name.encode()), seed]).standard_normal(out[name].shape)
        drawn = base * np.exp(spread * noise) if base else spread * noise
        out[name] = jnp.asarray(drawn.astype(out[name].dtype))
    for name, factor in factors.items():
        out[name] = (out[name] * factor).astype(out[name].dtype)
    return out
```

```python
from contextlib import ExitStack

import concourse.bass as bass
import numpy as np
from concourse import mybir

B, T, C = 4, 512, 512
P = 128
CT = C // P
TC = T // P
NCH = B * TC
INNER = 1408
PAIRS = INNER // P
TD = 128
TILES, SLICE, GRID = 64, 8, 16
CLUSTERS = TILES // 8
FULL = 2
REST = PAIRS - 4 * FULL
BIG = float(2.0 ** 126)
SEED = float(0x7EF311C3)
E30 = float(np.exp(np.float64(30.0)))
ROUND = float(2 ** 23)


def build_program(nc, xT, kT, x, cond, w0, w1, u0, u1, gu_pack, gu_scale, dn_pack, dn_scale,
                  gamma, beta, bases, slopes, oscale, out):
    f32, f16, bf16 = mybir.dt.float32, mybir.dt.float16, mybir.dt.bfloat16
    i32, u16 = mybir.dt.int32, mybir.dt.uint16
    ALU, ACT, AX = mybir.AluOpType, mybir.ActivationFunctionType, mybir.AxisListType.X

    ctx = ExitStack()
    with ctx:
        def sb(name, shape, dt):
            return ctx.enter_context(nc.sbuf_tensor(name, shape, dt))

        def sem(name):
            return ctx.enter_context(nc.semaphore(name))

        wg_hi = sb("wg_hi", [P, CT, 2 * INNER], f16)
        wg_lo = sb("wg_lo", [P, CT, 2 * INNER], bf16)
        wd_hi = sb("wd_hi", [P, PAIRS, C], f16)
        wd_lo = sb("wd_lo", [P, PAIRS, C], bf16)
        z = sb("z", [P, NCH, C], f32)
        q1 = sb("q1", [P, CT, T], f32)
        base_hi = sb("base_hi", [P, CT, T], f16)
        base_lo = sb("base_lo", [P, CT, T], f16)
        h_hi = sb("h_hi", [P, PAIRS, T], f16)
        h_lo = sb("h_lo", [P, PAIRS, T], f16)
        kbuf = sb("kbuf", [P, 2, T], f32)
        xTb = sb("xTb", [P, CT, T], f32)
        xf = sb("xf", [P, TC, C], f32)
        E = sb("E", [P, T + 1], f32)
        vs = sb("vs", [P, 2, T], f32)
        ekv = sb("ekv", [P, T + 1], f32)
        EU = sb("EU", [P, 2, T], f32)
        Fd = sb("Fd", [P, 2, T], f32)
        Bd = sb("Bd", [P, 2, T], f32)
        Fn = sb("Fn", [P, 2, T], f32)
        Bn = sb("Bn", [P, 2, T], f32)
        Tg = sb("Tg", [P, 2, T], f32)
        gam = sb("gam", [P, C], f32)
        bet = sb("bet", [P, C], f32)
        sig = sb("sig", [P, C], bf16)
        sgn = sb("sgn", [P, C], bf16)
        onehot = sb("onehot", [P, NCH, TILES], bf16)
        ts = sb("ts", [P, TC, TILES], f32)
        comp = sb("comp", [P, TC, TILES], f32)
        cs = sb("cs", [P, TC, CLUSTERS], f32)
        rank = sb("rank", [P, TC, TILES], f32)
        best = sb("best", [P, TC], f32)
        xs = sb("xs", [P, NCH, SLICE], f32)
        tmn = sb("tmn", [P, 2, TC], f32)
        mkv = sb("mkv", [P, 2, TILES], f32)
        run = sb("run", [P, 2, TILES], f32)
        ident = sb("ident", [P, P], f32)
        identh = sb("identh", [P, P], bf16)
        decay = sb("decay", [P, 2, CT, B], f32)
        wl = sb("wl", [P, 2, CT], f32)
        ul = sb("ul", [P, 2, CT], f32)
        tf = sb("tf", [P, 3, B], f32)
        sc = sb("sc", [P, B], f32)
        half = sb("half", [P, 1], f32)
        stat = sb("stat", [P, 9, TC], f32)
        shq = sb("shq", [P, 3], i32)
        junk = sb("junk", [P, C], bf16)
        ones = sb("ones", [TILES, P], bf16)
        iota16 = sb("iota16", [P, GRID], f32)
        osc = sb("osc", [P, NCH], f32)
        lk = sb("lk", [P, NCH, 2], f32)
        rng = sb("rng", [P, NCH], f32)
        lookt = sb("lookt", [TILES, 2], f32)
        gi = sb("gi", [P, NCH, SLICE], f32)
        gt = sb("gt", [P, NCH, SLICE], f32)
        bs = sb("bs", [P, 2, NCH * SLICE], f32)

        z_i = z[:, 4:NCH, :].rearrange("p a b -> p (a b)").bitcast(i32)
        gp_i = z_i[:, 0:2 * INNER]
        dp_i = z_i[:, 2 * INNER:2 * INNER + (FULL + REST) * C]
        hh = h_hi[:, :, :].rearrange("p a b -> p (a b)")
        hl = h_lo[:, :, :].rearrange("p a b -> p (a b)")
        gs_h = hh[:, 0:2 * INNER]
        ds_h = hh[:, 2 * INNER:2 * INNER + (FULL + REST) * C]
        gu_u = hl[:, 0:2 * INNER].bitcast(u16)
        dn_u = hl[:, 2 * INNER:2 * INNER + (FULL + REST) * C].bitcast(u16)
        V = base_hi[:, :, :].rearrange("p a b -> p (a b)").bitcast(u16)
        S = base_lo[:, :, :].rearrange("p a b -> p (a b)").bitcast(u16)
        w32 = xf[:, :, :].rearrange("p a b -> p (a b)")
        xTf = xTb[:, :, :].rearrange("p a b -> p (a b)")
        hf = h_hi[:, :, :].rearrange("p a b -> p (a b)").bitcast(f32)
        lf = h_lo[:, :, :].rearrange("p a b -> p (a b)").bitcast(f32)
        ohT = hf[0:TILES, 0:NCH * P]
        tab = lf[0:TILES, 0:2 * SLICE * GRID + 1]
        looked = q1[:, :, :].rearrange("p a b -> p (a b)")
        looked_s = xTf
        oneh16 = xf[:, :, :].rearrange("p a b -> p (a b)")

        ps = ctx.enter_context(nc.psum_tensor("ps", [P, 8, 512], f32))
        Y0, TR0 = 4, 6

        names = ("ld_k0 ld_k1 ld_z0 ld_x ld_z ld_pack ld_scale ld_small ld_tab st_out "
                 "iota_done half_set tf_sum tf_tanh tf_scale tf_decay w_exp w_exp2 dec_done sc_done "
                 "shift_set shift_set2 halves compact dmag dsgn dval dprod whi wlo "
                 "slope_sum slope_sgn sig_mask sig_rhs sig_bc sig_done rank_done run_init ident_done "
                 "km ex vsc ekvd eu sd sn d1 n1 euv den denm num seed pd wq e2 e4 fa fb fq tx based bhi blo "
                 "gu tg ag hd hhi hlo tr q1t yd ssq msq rs x1 t1 mix zadd nmean varr varm rstd nbias xn gamd xfd "
                 "sgnd ssd tsd csd cmp1 cmp2 bestd ohd prodd xsd tmnd tmxd mk1 mk2 mk3 rund rund2 "
                 "ohtr ohtc tabm tabc rtr rred lk lkc g1 g2 g3 g4 g5 g6 g7 g8 g9 g10 g11 fin1 fin2 bnz ones tabl").split()
        s = {n: sem(n) for n in names}

        SSQ, RS, SUM, NMEAN, VAR, RSTD, VAREPS, SSQEPS, NBIAS = range(9)

        def rev(ap):
            return ap[:, ::-1]

        block = ctx.enter_context(nc.Block())
        xT_v = xT
        kT_v = kT

        @block.sync
        def _(sp):
            sp.dma_start(gp_i, gu_pack).then_inc(s["ld_pack"], 16)
            sp.dma_start(gs_h, gu_scale).then_inc(s["ld_scale"], 16)
            sp.dma_start(dp_i, dn_pack).then_inc(s["ld_pack"], 16)

            def load_k(n, b, m):
                if not (isinstance(n, int) and n < 2):
                    sp.wait_ge(s["eu"], 2 * n - 2)
                    sp.wait_ge(s["vsc"], n - 1)
                    sp.wait_ge(s["km"], n - 1)
                sp.dma_start(kbuf[:, m % 2, :], kT_v[m, :, b, :]).then_inc(s["ld_k%d" % (m % 2)], 16)

            def load_x(b):
                if not (isinstance(b, int) and b == 0):
                    sp.wait_ge(s["blo"], 4 * b)
                sp.dma_start(xTb[:, :, :], xT_v[:, :, b, :].rearrange("m p t -> p m t")).then_inc(s["ld_x"], 16)

            load_k(0, 0, 0)
            load_k(1, 0, 1)
            load_x(0)
            sp.dma_start(z[:, 0:TC, :], x[0].rearrange("(c p) n -> p c n", p=P)).then_inc(s["ld_z0"], 16)
            for m in range(2, CT):
                load_k(m, 0, m)
            load_k(4, 1, 0)
            load_k(5, 1, 1)
            sp.wait_ge(s["halves"], 3)
            sp.wait_ge(s["compact"], 2)
            for b in range(1, B):
                sp.dma_start(z[:, TC * b:TC * (b + 1), :],
                             x[b].rearrange("(c p) n -> p c n", p=P)).then_inc(s["ld_z"], 16)
            load_x(1)
            for b in range(B - 1):
                for m in range(2, CT):
                    load_k(4 * (b + 1) + m, b + 1, m)
                if b < B - 2:
                    load_k(4 * (b + 2), b + 2, 0)
                    load_k(4 * (b + 2) + 1, b + 2, 1)
                    load_x(b + 2)
            sp.wait_ge(s["yd"], NCH)
            sp.dma_start(tab[:, 0:SLICE * GRID], bases.rearrange("t j g -> t (j g)")).then_inc(s["ld_tab"], 16)
            sp.dma_start(tab[:, SLICE * GRID:2 * SLICE * GRID], slopes.rearrange("t j g -> t (j g)")).then_inc(s["ld_tab"], 16)
            sp.dma_start(tab[:, 2 * SLICE * GRID:], oscale.rearrange("(t a) -> t a", a=1)).then_inc(s["ld_tab"], 16)
            for c in range(NCH):
                sp.wait_ge(s["fin2"], c + 1)
                sp.dma_start(out[c // TC, (c % TC) * P:(c % TC + 1) * P, :], z[:, c, :]).then_inc(s["st_out"], 16)
            sp.wait_ge(s["st_out"], 16 * NCH)

        @block.gpsimd
        def _(g):
            g.memset(ident[:, :], 0.0).then_inc(s["ident_done"], 1)
            g.wait_ge(s["ident_done"], 1)
            g.affine_select(out=ident[:, :], in_=ident[:, :], compare_op=ALU.not_equal, fill=1.0, base=0,
                            pattern=[[-1, P]], channel_multiplier=1).then_inc(s["ident_done"], 1)
            g.wait_ge(s["ident_done"], 2)
            g.tensor_copy(identh[:, :], ident[:, :]).then_inc(s["ident_done"], 1)
            g.iota(shq[:, 0:1], pattern=[[0, 1]], base=0, channel_multiplier=1).then_inc(s["iota_done"], 1)
            g.iota(comp[:, :, :].bitcast(i32), pattern=[[0, TC], [-256, CLUSTERS], [-1, 8]], base=0, channel_multiplier=0).then_inc(s["iota_done"], 1)
            g.wait_ge(s["iota_done"], 2)
            g.tensor_copy(rank[:, :, :], comp[:, :, :].bitcast(i32)).then_inc(s["rank_done"], 1)
            g.iota(cs[:, 0:2, :].bitcast(i32), pattern=[[1, GRID]], base=0, channel_multiplier=0).then_inc(s["iota_done"], 1)
            g.wait_ge(s["iota_done"], 3)
            g.tensor_copy(iota16[:, :], cs[:, 0:2, :].rearrange("p a b -> p (a b)").bitcast(i32)).then_inc(s["rank_done"], 1)
            g.memset(ones[:, :], 1.0).then_inc(s["ones"], 1)
            g.memset(half[:, :], -0.5).then_inc(s["half_set"], 1)
            g.memset(run[:, 0, :], BIG).then_inc(s["run_init"], 1)
            g.memset(run[:, 1, :], -BIG).then_inc(s["run_init"], 1)
            g.memset(E[:, T:T + 1], 0.0).then_inc(s["bnz"], 1)
            g.memset(ekv[:, T:T + 1], 0.0).then_inc(s["bnz"], 1)
            g.wait_ge(s["slope_sgn"], 1)
            g.affine_select(out=sgn[0:TILES, :].rearrange("p (t j) -> p t j", j=SLICE),
                            in_=ts[0:TILES, 1, 0:SLICE].unsqueeze(1).broadcast_to([TILES, TILES, SLICE]),
                            compare_op=ALU.is_equal, fill=0.0, base=0,
                            pattern=[[-1, TILES], [0, SLICE]], channel_multiplier=1).then_inc(s["sig_rhs"], 1)

            def w_lo(i, dst, src, hi):
                g.wait_ge(s["whi"], i + 1)
                g.tensor_tensor(dst, src, hi, ALU.subtract).then_inc(s["wlo"], 1)

            def shared(n, m):
                g.wait_ge(s["ex"], n + 1)
                g.wait_ge(s["vsc"], n + 1)
                if not (isinstance(n, int) and n == 0):
                    g.wait_ge(s["sn"], 4 * n)
                g.tensor_tensor(ekv[:, 0:T], E[:, 0:T], vs[:, m % 2, :], ALU.mult).then_inc(s["ekvd"], 1)

            def ratio_a(k, l):
                g.wait_ge(s["seed"], k + 1)
                g.tensor_tensor(EU[:, l, :], Fd[:, l, :], Bd[:, l, :], ALU.mult).then_inc(s["pd"], 1)
                g.wait_ge(s["num"], k + 1)
                g.tensor_tensor(Fn[:, l, :], Fn[:, l, :], Bd[:, l, :], ALU.mult).then_inc(s["wq"], 1)

            def sums(k, l):
                g.wait_ge(s["sd"], 2 * k + 2)
                g.tensor_tensor(Fd[:, l, :], Fd[:, l, :], Bd[:, l, :], ALU.add).then_inc(s["d1"], 1)
                g.wait_ge(s["sn"], 2 * k + 2)
                g.tensor_tensor(Fn[:, l, :], Fn[:, l, :], Bn[:, l, :], ALU.add).then_inc(s["n1"], 1)

            def numer(k, l):
                g.wait_ge(s["euv"], k + 1)
                g.wait_ge(s["n1"], k + 1)
                g.tensor_tensor(Fn[:, l, :], Fn[:, l, :], Bn[:, l, :], ALU.add).then_inc(s["num"], 1)

            def half_step(b, i):
                k, l, m = 8 * b + i, i % 2, i // 2
                if i > 0:
                    ratio_a(k - 1, 1 - l)
                sums(k, l)
                numer(k, l)
                if l == 1 and m + 1 < CT:
                    shared(4 * b + m + 1, m + 1)

            def split_base(b):
                for m in range(CT):
                    g.wait_ge(s["bhi"], 4 * b + m + 1)
                    g.tensor_tensor(base_lo[:, m, :], xTb[:, m, :], base_hi[:, m, :], ALU.subtract).then_inc(s["blo"], 1)

            chunks = [(wg_lo[:, :, 2 * P * j:2 * P * (j + 1)],
                       w32[:, 1024 * (j % 2):1024 * (j % 2) + CT * 2 * P].rearrange("p (m n) -> p m n", m=CT),
                       wg_hi[:, :, 2 * P * j:2 * P * (j + 1)]) for j in range(PAIRS)]
            for i, (dst, src, hi) in enumerate(chunks):
                w_lo(i, dst, src, hi)
            for i in range(FULL + 1):
                nt = CT if i < FULL else REST
                w_lo(PAIRS + i, wd_lo[:, CT * i:CT * i + nt, :],
                     w32[:, 0:nt * C].rearrange("p (m n) -> p m n", m=nt), wd_hi[:, CT * i:CT * i + nt, :])
            shared(0, 0)
            for i in range(2 * CT):
                half_step(0, i)
            ratio_a(7, 1)
            split_base(0)

            def stage1(t, c):
                g.wait_ge(s["msq"], t + 1)
                g.tensor_tensor(stat[:, RS, c:c + 1], stat[:, SSQEPS, c:c + 1], half[:, :], ALU.pow).then_inc(s["rs"], 1)
                g.wait_ge(s["mix"], t + 1)
                g.tensor_tensor(z[:, t, :], z[:, t, :], xf[:, c, :], ALU.add).then_inc(s["zadd"], 1)
                g.wait_ge(s["varm"], t + 1)
                g.tensor_tensor(stat[:, RSTD, c:c + 1], stat[:, VAREPS, c:c + 1], half[:, :], ALU.pow).then_inc(s["rstd"], 1)

            def stage2(t, c):
                g.wait_ge(s["xn"], t + 1)
                g.tensor_tensor(xf[:, c, :], xf[:, c, :], gam[:, :], ALU.mult).then_inc(s["gamd"], 1)

            def select_slice(b):
                g.wait_ge(s["ohd"], b + 1)
                g.wait_ge(s["xfd"], TC * (b + 1))
                g.tensor_tensor(xf[:, :, :].rearrange("p c (t j) -> p (c t) j", j=SLICE),
                                xf[:, :, :].rearrange("p c (t j) -> p (c t) j", j=SLICE),
                                onehot[:, TC * b:TC * (b + 1), :].rearrange("p c t -> p (c t)").unsqueeze(2)
                                .broadcast_to([P, TC * TILES, SLICE]), ALU.mult).then_inc(s["prodd"], 1)

            def iteration(b, last):
                for j in range(PAIRS):
                    e = PAIRS * b + j
                    g.wait_ge(s["hhi"], e + 1)
                    g.tensor_tensor(h_lo[:, j, :], Tg[:, j % 2, :], h_hi[:, j, :], ALU.subtract).then_inc(s["hlo"], 1)
                    if b > 0 and j == 0:
                        stage2(TC * b - 1, TC - 1)
                    if b > 0 and j == 1:
                        select_slice(b - 1)
                    if not last:
                        if j == 1:
                            shared(4 * (b + 1), 0)
                        if 2 <= j < 10:
                            half_step(b + 1, j - 2)
                        if j == 10:
                            ratio_a(8 * (b + 1) + 7, 1)
                            split_base(b + 1)
                for c in range(TC):
                    stage1(TC * b + c, c)
                    if c > 0:
                        stage2(TC * b + c - 1, c - 1)

            g.wait_ge(s["ld_small"], 16 * 8)
            for b in range(B):
                iteration(b, b == B - 1)
            stage2(NCH - 1, TC - 1)
            select_slice(B - 1)


        @block.scalar
        def _(a):
            for l, (wv, uv) in enumerate(((w0, u0), (w1, u1))):
                a.dma_start(wl[:, l, :], wv).then_inc(s["ld_small"], 16)
                a.dma_start(ul[:, l, :], uv).then_inc(s["ld_small"], 16)
            a.dma_start(Tg[:, 1, :], cond.rearrange("(o b) t -> o (b t)", o=1).broadcast_to([P, B * TD])).then_inc(s["ld_small"], 16)
            a.dma_start(gam[:, :], gamma.rearrange("(o n) -> o n", o=1).broadcast_to([P, C])).then_inc(s["ld_small"], 16)
            a.dma_start(bet[:, :], beta.rearrange("(o n) -> o n", o=1).broadcast_to([P, C])).then_inc(s["ld_small"], 16)
            a.dma_start(Tg[0:TILES, 0, 0:SLICE * GRID], slopes.rearrange("t j g -> t (j g)")).then_inc(s["ld_small"], 16)
            a.dma_start(ds_h, dn_scale).then_inc(s["ld_scale"], 16)
            a.wait_ge(s["ld_small"], 16 * 8)
            a.activation(wl[:, :, :], wl[:, :, :], ACT.Exp).then_inc(s["w_exp"], 1)
            a.wait_ge(s["w_exp"], 1)
            a.activation(wl[:, :, :], wl[:, :, :], ACT.Exp, scale=-1.0).then_inc(s["w_exp"], 1)
            a.wait_ge(s["tf_sum"], 1)
            a.activation(tf[:, 1, :], tf[:, 0, :], ACT.Tanh, scale=0.5).then_inc(s["tf_tanh"], 1)
            a.wait_ge(s["slope_sum"], 1)
            a.activation(ts[0:TILES, 1, 0:SLICE], ts[0:TILES, 0, 0:SLICE], ACT.Sign).then_inc(s["slope_sgn"], 1)
            for n, (dst, src) in enumerate(((gu_u, gp_i), (dn_u, dp_i))):
                a.wait_ge(s["halves"], (1, 3)[n])
                a.activation(dst, src.bitcast(u16)[:, ::2], ACT.Copy).then_inc(s["compact"], 1)
            for j in range(PAIRS):
                a.wait_ge(s["dprod"], j + 1)
                a.activation(wg_hi[:, :, 2 * P * j:2 * P * (j + 1)],
                             w32[:, 1024 * (j % 2):1024 * (j % 2) + CT * 2 * P].rearrange("p (m n) -> p m n", m=CT),
                             ACT.Copy).then_inc(s["whi"], 1)
            for i in range(FULL + 1):
                nt = CT if i < FULL else REST
                a.wait_ge(s["dprod"], PAIRS + i + 1)
                a.activation(wd_hi[:, CT * i:CT * i + nt, :], w32[:, 0:nt * C].rearrange("p (m n) -> p m n", m=nt),
                             ACT.Copy).then_inc(s["whi"], 1)

            def shared(b, m):
                n = 4 * b + m
                a.wait_ge(s["km"], n + 1)
                a.activation(E[:, 0:T], E[:, 0:T], ACT.Exp).then_inc(s["ex"], 1)
                if n >= 2:
                    a.wait_ge(s["euv"], 2 * n - 2)
                a.activation(vs[:, m % 2, :], kbuf[:, m % 2, :], ACT.Copy, scale=sc[:, b:b + 1]).then_inc(s["vsc"], 1)

            def powers(k, l):
                a.wait_ge(s["pd"], k + 1)
                a.wait_ge(s["wq"], k + 1)
                a.activation(Bn[:, l, :], EU[:, l, :], ACT.Square, scale=-1.0, bias=1.0).then_inc(s["e2"], 1)
                a.wait_ge(s["e2"], k + 1)
                a.activation(Bd[:, l, :], Bn[:, l, :], ACT.Square).then_inc(s["e4"], 1)

            def half_step(b, i):
                k, l, m = 8 * b + i, i % 2, i // 2
                if k >= 2:
                    a.wait_ge(s["fa"], k - 1)
                a.activation(EU[:, l, :], kbuf[:, m % 2, :], ACT.Exp, bias=ul[:, l, m:m + 1]).then_inc(s["eu"], 1)
                if i > 0:
                    powers(k - 1, 1 - l)
                if l == 0:
                    if m == 0:
                        a.wait_ge(s["ld_x"], 16 * (b + 1))
                    a.activation(xTb[:, m, :], xTb[:, m, :], ACT.Tanh, scale=0.5).then_inc(s["tx"], 1)
                a.wait_ge(s["denm"], k + 1)
                a.activation(Bd[:, l, :].bitcast(i32), Fd[:, l, :].bitcast(i32), ACT.Copy, scale=-1.0, bias=SEED).then_inc(s["seed"], 1)
                if l == 1 and m + 1 < CT:
                    shared(b, m + 1)

            def split_base(b):
                for m in range(CT):
                    a.wait_ge(s["based"], 4 * b + m + 1)
                    if b > 0:
                        a.wait_ge(s["gu"], PAIRS * b)
                    else:
                        a.wait_ge(s["dprod"], PAIRS + FULL + 1)
                    a.activation(base_hi[:, m, :], xTb[:, m, :], ACT.Copy).then_inc(s["bhi"], 1)

            a.wait_ge(s["sc_done"], 2)
            shared(0, 0)
            for i in range(2 * CT):
                half_step(0, i)
            powers(7, 1)
            split_base(0)

            def stage1(t, c):
                a.wait_ge(s["yd"], t + 1)
                a.activation(junk[:, :], ps[:, Y0 + c % 2, :], ACT.Square, accum_out=stat[:, SSQ, c:c + 1]).then_inc(s["ssq"], 1)
                a.wait_ge(s["x1"], t + 1)
                a.activation(Tg[:, c % 2, :], z[:, t, :], ACT.Tanh, scale=0.5).then_inc(s["t1"], 1)
                a.wait_ge(s["mix"], t + 1)
                a.activation(stat[:, NMEAN, c:c + 1], stat[:, SUM, c:c + 1], ACT.Copy, scale=-1.0 / C).then_inc(s["nmean"], 1)
                a.wait_ge(s["nmean"], t + 1)
                a.activation(junk[:, :], xf[:, c, :], ACT.Square, bias=stat[:, NMEAN, c:c + 1],
                             accum_out=stat[:, VAR, c:c + 1]).then_inc(s["varr"], 1)
                a.wait_ge(s["rstd"], t + 1)
                a.activation(stat[:, NBIAS, c:c + 1], stat[:, NMEAN, c:c + 1], ACT.Copy, scale=stat[:, RSTD, c:c + 1]).then_inc(s["nbias"], 1)
                a.wait_ge(s["nbias"], t + 1)
                a.wait_ge(s["zadd"], t + 1)
                a.activation(xf[:, c, :], xf[:, c, :], ACT.Identity, scale=stat[:, RSTD, c:c + 1],
                             bias=stat[:, NBIAS, c:c + 1]).then_inc(s["xn"], 1)

            def stage2(t, c):
                a.wait_ge(s["xfd"], t + 1)
                if t > 0:
                    a.wait_ge(s["tsd"], t)
                a.activation(sgn[:, :], xf[:, c, :], ACT.Sign).then_inc(s["sgnd"], 1)

            def q1_rows(b):
                for c in range(TC):
                    t = TC * b + c
                    a.wait_ge(s["tr"], t + 1)
                    if b > 0:
                        a.wait_ge(s["xsd"], b)
                    a.activation(xf[:, c, :].rearrange("p (r q m) -> p m q r", q=2, m=CT),
                                 ps[:, TR0 + c % 2, :].rearrange("p (m q r) -> p m q r", m=CT, q=2),
                                 ACT.Copy).then_inc(s["q1t"], 1)

            for b in range(B):
                for j in range(PAIRS):
                    e = PAIRS * b + j
                    a.wait_ge(s["gu"], e + 1)
                    if j >= 2:
                        a.wait_ge(s["hlo"], e - 1)
                    elif b > 0:
                        a.wait_ge(s["hlo"], PAIRS * b)
                        a.wait_ge(s["mix"], TC * b)
                    a.activation(Tg[:, j % 2, :], ps[:, 2 * (j % 2), :], ACT.Tanh, scale=4.0).then_inc(s["tg"], 1)
                    a.wait_ge(s["hd"], e + 1)
                    a.activation(h_hi[:, j, :], Tg[:, j % 2, :], ACT.Copy).then_inc(s["hhi"], 1)
                    if b > 0 and j == 0:
                        stage2(TC * b - 1, TC - 1)
                    if j == 1:
                        q1_rows(b)
                    if b + 1 < B:
                        if j == 1:
                            shared(b + 1, 0)
                        if 2 <= j < 10:
                            half_step(b + 1, j - 2)
                        if j == 10:
                            powers(8 * (b + 1) + 7, 1)
                if b + 1 < B:
                    split_base(b + 1)
                for c in range(TC):
                    stage1(TC * b + c, c)
                    if c > 0:
                        stage2(TC * b + c - 1, c - 1)
            stage2(NCH - 1, TC - 1)
            for c in range(NCH):
                a.wait_ge(s["ohtr"], c + 1)
                a.activation(ohT[:, c * P:(c + 1) * P], ps[0:TILES, TR0 + c % 2, 0:TILES].bitcast(bf16), ACT.Copy).then_inc(s["ohtc"], 1)
            for c in range(NCH):
                a.wait_ge(s["tabm"], c + 1)
                half_w = SLICE * GRID
                a.activation(looked[:, c * half_w:(c + 1) * half_w], ps[:, c % 4, 0:half_w], ACT.Copy)
                a.activation(looked_s[:, c * half_w:(c + 1) * half_w], ps[:, c % 4, half_w:2 * half_w], ACT.Copy)
                a.activation(osc[:, c:c + 1], ps[:, c % 4, 2 * half_w:2 * half_w + 1], ACT.Copy).then_inc(s["tabc"], 1)

        @block.tensor
        def _(pe):
            pe.wait_ge(s["sig_rhs"], 1)
            pe.wait_ge(s["ones"], 1)
            nc.tensor.matmul(ps[:, TR0, :], ones[:, :], sgn[0:TILES, :], start=True, stop=True).then_inc(s["sig_bc"], 1)
            pe.wait_ge(s["ident_done"], 3)
            for b in range(B):
                pe.wait_ge(s["blo"], 4 * (b + 1))
                for j in range(PAIRS):
                    e = PAIRS * b + j
                    if b == 0:
                        pe.wait_ge(s["wlo"], j + 1)
                    if j >= 2:
                        pe.wait_ge(s["hd"], e - 1)
                    elif b > 0:
                        pe.wait_ge(s["hd"], PAIRS * b)
                    for part in range(2):
                        cols = slice(2 * P * j + P * part, 2 * P * j + P * (part + 1))
                        dst = ps[:, 2 * (j % 2) + part, :]
                        for m in range(CT):
                            nc.tensor.matmul(dst, wg_hi[:, m, cols], base_hi[:, m, :], start=(m == 0), stop=False)
                            nc.tensor.matmul(dst, wg_hi[:, m, cols], base_lo[:, m, :], start=False, stop=False)
                            last = nc.tensor.matmul(dst, wg_lo[:, m, cols], base_hi[:, m, :], start=False, stop=(m == CT - 1))
                    last.then_inc(s["gu"], 1)
                    if j == 1:
                        pe.wait_ge(s["fq"], 8 * (b + 1))
                        for c in range(TC):
                            if c >= 2:
                                pe.wait_ge(s["q1t"], TC * b + c - 1)
                            elif b == 0:
                                pe.wait_ge(s["sig_done"], 1)
                            for m in range(CT):
                                last = nc.tensor.transpose(ps[:, TR0 + c % 2, P * m:P * (m + 1)],
                                                           q1[:, m, P * c:P * (c + 1)], ident[:, :])
                            last.then_inc(s["tr"], 1)
                pe.wait_ge(s["hlo"], PAIRS * (b + 1))
                if b == 0:
                    pe.wait_ge(s["wlo"], PAIRS + FULL + 1)
                for c in range(TC):
                    t = TC * b + c
                    if t >= 2:
                        pe.wait_ge(s["x1"], t - 1)
                    dst = ps[:, Y0 + c % 2, :]
                    for j in range(PAIRS):
                        rows = slice(P * c, P * (c + 1))
                        nc.tensor.matmul(dst, h_hi[:, j, rows], wd_hi[:, j, :], start=(j == 0), stop=False)
                        nc.tensor.matmul(dst, h_hi[:, j, rows], wd_lo[:, j, :], start=False, stop=False)
                        last = nc.tensor.matmul(dst, h_lo[:, j, rows], wd_hi[:, j, :], start=False, stop=(j == PAIRS - 1))
                    last.then_inc(s["yd"], 1)
            for c in range(NCH):
                pe.wait_ge(s["ohd"], c // TC + 1)
                if c >= 2:
                    pe.wait_ge(s["ohtc"], c - 1)
                nc.tensor.transpose(ps[0:TILES, TR0 + c % 2, 0:TILES].bitcast(bf16), onehot[:, c, :], identh[:, :]).then_inc(s["ohtr"], 1)
            pe.wait_ge(s["ld_tab"], 48)
            for c in range(NCH):
                pe.wait_ge(s["ohtc"], c + 1)
                if c >= 4:
                    pe.wait_ge(s["tabc"], c - 3)
                nc.tensor.matmul(ps[:, c % 4, 0:2 * SLICE * GRID + 1], ohT[:, c * P:(c + 1) * P], tab, start=True, stop=True).then_inc(s["tabm"], 1)
            pe.wait_ge(s["rund"], 2 * B)
            for i in range(2):
                nc.tensor.transpose(ps[0:TILES, Y0, P * i:P * (i + 1)], run[:, i, :], ident[:, :]).then_inc(s["rtr"], 1)
            pe.wait_ge(s["rred"], 2)
            for c in range(NCH):
                last = nc.tensor.matmul(ps[:, Y0 + 1, 2 * c:2 * c + 2], ohT[:, c * P:(c + 1) * P], lookt[:, :], start=True, stop=True)
            last.then_inc(s["lk"], 1)

        @block.vector
        def _(v):
            chain = [0]

            def link(ins):
                chain[0] += 1
                ins.then_inc(s["bestd"], 1)
                v.wait_ge(s["bestd"], chain[0])

            v.wait_ge(s["ld_small"], 16 * 8)
            nc.vector.tensor_reduce(tf[:, 0, :], Tg[:, 1, :].rearrange("p (b t) -> p b t", b=B), axis=AX, op=ALU.add).then_inc(s["tf_sum"], 1)
            nc.vector.tensor_reduce(ts[0:TILES, 0, 0:SLICE], Tg[0:TILES, 0, 0:SLICE * GRID].rearrange("p (j g) -> p j g", g=GRID),
                                    axis=AX, op=ALU.add).then_inc(s["slope_sum"], 1)
            v.wait_ge(s["iota_done"], 1)
            nc.vector.tensor_scalar(shq[:, 1:2], shq[:, 0:1], 6, 4, ALU.logical_shift_right, ALU.logical_shift_left).then_inc(s["shift_set"], 1)
            nc.vector.tensor_scalar(shq[:, 2:3], shq[:, 0:1], 4, 2, ALU.logical_shift_right, ALU.logical_shift_left).then_inc(s["shift_set"], 1)
            v.wait_ge(s["shift_set"], 2)
            v.wait_ge(s["ld_pack"], 32)
            v.wait_ge(s["ld_scale"], 32)
            nc.vector.tensor_scalar(gp_i, gp_i, shq[:, 1:2], None, ALU.logical_shift_right).then_inc(s["halves"], 1)
            nc.vector.tensor_scalar(dp_i[:, 0:FULL * C], dp_i[:, 0:FULL * C], shq[:, 1:2], None, ALU.logical_shift_right).then_inc(s["halves"], 1)
            nc.vector.tensor_scalar(dp_i[:, FULL * C:], dp_i[:, FULL * C:], shq[:, 2:3], None, ALU.logical_shift_right).then_inc(s["halves"], 1)
            v.wait_ge(s["tf_tanh"], 1)
            v.wait_ge(s["w_exp"], 2)
            nc.vector.tensor_scalar(tf[:, 2, :], tf[:, 1, :], 0.25, 0.75, ALU.mult, ALU.add).then_inc(s["tf_scale"], 1)
            nc.vector.tensor_scalar(sc[:, :], tf[:, 1, :], 0.05, 0.45, ALU.mult, ALU.add).then_inc(s["sc_done"], 1)
            v.wait_ge(s["tf_scale"], 1)
            nc.vector.tensor_tensor(decay[:, :, :, :].rearrange("p l m b -> p (l m) b"),
                                    wl[:, :, :].rearrange("p l m -> p (l m)").unsqueeze(2).broadcast_to([P, 2 * CT, B]),
                                    tf[:, 2, :].unsqueeze(1).broadcast_to([P, 2 * CT, B]), ALU.mult).then_inc(s["sc_done"], 1)
            v.wait_ge(s["sig_bc"], 1)
            nc.vector.tensor_copy(sig[:, :], ps[:, TR0, :]).then_inc(s["sig_done"], 1)

            def decode(i, words, nt, n, scale, dst, shifts):
                if i > 0:
                    v.wait_ge(s["dprod"], i)
                for m in range(nt):
                    left = 9 - shifts[m]
                    nc.vector.tensor_scalar(V[:, m * n:(m + 1) * n], words[m], abs(left), 0x0E00,
                                            ALU.logical_shift_left if left > 0 else ALU.logical_shift_right,
                                            ALU.bitwise_and).then_inc(s["dmag"], 1)
                    nc.vector.tensor_scalar(S[:, m * n:(m + 1) * n], words[m], 12 - shifts[m], 0x8000,
                                            ALU.logical_shift_left, ALU.bitwise_and).then_inc(s["dsgn"], 1)
                dcount[0] += nt
                v.wait_ge(s["dmag"], dcount[0])
                v.wait_ge(s["dsgn"], dcount[0])
                nc.vector.tensor_tensor(V[:, 0:nt * n], V[:, 0:nt * n], S[:, 0:nt * n], ALU.bitwise_or).then_inc(s["dval"], 1)
                v.wait_ge(s["dval"], i + 1)
                nc.vector.scalar_tensor_tensor(dst, V[:, 0:nt * n].bitcast(f16).rearrange("p (m n) -> p m n", m=nt), 2048.0,
                                               scale, ALU.mult, ALU.mult).then_inc(s["dprod"], 1)

            dcount = [0]
            v.wait_ge(s["compact"], 1)
            for j in range(PAIRS):
                if j >= 2:
                    v.wait_ge(s["wlo"], j - 1)
                word = gu_u[:, 2 * P * j:2 * P * (j + 1)]
                decode(j, [word] * CT, CT, 2 * P,
                       gs_h[:, 2 * P * j:2 * P * (j + 1)].unsqueeze(1).broadcast_to([P, CT, 2 * P]),
                       w32[:, 1024 * (j % 2):1024 * (j % 2) + 1024].rearrange("p (m n) -> p m n", m=CT),
                       [0, 4, 8, 12])
            v.wait_ge(s["compact"], 2)
            for i in range(FULL + 1):
                v.wait_ge(s["wlo"], PAIRS + i)
                if i < FULL:
                    decode(PAIRS + i, [dn_u[:, C * i:C * (i + 1)]] * CT, CT, C,
                           ds_h[:, C * i:C * (i + 1)].unsqueeze(1).broadcast_to([P, CT, C]),
                           w32[:, 0:CT * C].rearrange("p (m n) -> p m n", m=CT), [0, 4, 8, 12])
                else:
                    decode(PAIRS + i, [dn_u[:, C * (FULL + r):C * (FULL + r + 1)] for r in range(REST)], REST, C,
                           ds_h[:, C * FULL:].rearrange("p (m n) -> p m n", m=REST),
                           w32[:, 0:REST * C].rearrange("p (m n) -> p m n", m=REST), [0] * REST)

            def shared(b, m):
                n = 4 * b + m
                v.wait_ge(s["ld_k%d" % (m % 2)], 16 * (2 * b + m // 2 + 1))
                if n > 0:
                    v.wait_ge(s["ekvd"], n)
                nc.vector.tensor_scalar(E[:, 0:T], kbuf[:, m % 2, :], 30.0, None, ALU.min).then_inc(s["km"], 1)

            def scans(b, i):
                k, l, m = 8 * b + i, i % 2, i // 2
                n = 4 * b + m
                d = decay[:, l, m, b:b + 1]

                def fwd(dst, src):
                    return nc.vector.tensor_tensor_scan(dst[:, l, :], d.broadcast_to([P, T]), src, 0.0, ALU.mult, ALU.add)

                def bwd(dst, src):
                    return nc.vector.tensor_tensor_scan(rev(dst[:, l, :]), rev(src[:, 1:T + 1]), d.broadcast_to([P, T]),
                                                        0.0, ALU.add, ALU.mult)
                v.wait_ge(s["ex"], n + 1)
                fwd(Fd, E[:, 0:T]).then_inc(s["sd"], 1)
                bwd(Bd, E).then_inc(s["sd"], 1)
                v.wait_ge(s["ekvd"], n + 1)
                fwd(Fn, ekv[:, 0:T]).then_inc(s["sn"], 1)
                bwd(Bn, ekv).then_inc(s["sn"], 1)

            def weigh(b, i):
                k, l, m = 8 * b + i, i % 2, i // 2
                v.wait_ge(s["eu"], k + 1)
                v.wait_ge(s["n1"], k + 1)
                nc.vector.scalar_tensor_tensor(Bn[:, l, :], EU[:, l, :], E30, vs[:, m % 2, :], ALU.min, ALU.mult).then_inc(s["euv"], 1)
                nc.vector.scalar_tensor_tensor(Fd[:, l, :], EU[:, l, :], E30, Fd[:, l, :], ALU.min, ALU.add).then_inc(s["den"], 1)
                v.wait_ge(s["den"], k + 1)
                nc.vector.tensor_scalar(Fd[:, l, :], Fd[:, l, :], 1e-8, None, ALU.max).then_inc(s["denm"], 1)

            def ratio(b, i):
                k, l, m = 8 * b + i, i % 2, i // 2
                v.wait_ge(s["wq"], k + 1)
                v.wait_ge(s["e2"], k + 1)
                nc.vector.scalar_tensor_tensor(Fn[:, l, :], EU[:, l, :], 2.0, Fn[:, l, :], ALU.subtract, ALU.mult, reverse0=True).then_inc(s["fa"], 1)
                v.wait_ge(s["fa"], k + 1)
                nc.vector.scalar_tensor_tensor(Fn[:, l, :], Bn[:, l, :], 1.0, Fn[:, l, :], ALU.add, ALU.mult).then_inc(s["fb"], 1)
                v.wait_ge(s["fb"], k + 1)
                v.wait_ge(s["e4"], k + 1)
                if l == 1 and b > 0:
                    v.wait_ge(s["tr"], TC * b)
                nc.vector.scalar_tensor_tensor(q1[:, m, :] if l else Fn[:, l, :], Bd[:, l, :], 1.0, Fn[:, l, :], ALU.add, ALU.mult).then_inc(s["fq"], 1)
                if l == 0:
                    v.wait_ge(s["fq"], k + 1)
                    v.wait_ge(s["tx"], 4 * b + m + 1)
                    nc.vector.scalar_tensor_tensor(xTb[:, m, :], xTb[:, m, :], 1.0, Fn[:, l, :], ALU.add, ALU.mult).then_inc(s["based"], 1)

            def half_step(b, i):
                scans(b, i)
                if i > 0:
                    ratio(b, i - 1)
                weigh(b, i)
                if i % 2 == 1 and i // 2 + 1 < CT:
                    shared(b, i // 2 + 1)

            v.wait_ge(s["bnz"], 2)
            v.wait_ge(s["sc_done"], 2)
            shared(0, 0)
            for i in range(2 * CT):
                half_step(0, i)
            ratio(0, 7)

            def stage1(t, c):
                v.wait_ge(s["ssq"], t + 1)
                nc.vector.tensor_scalar(stat[:, SSQEPS, c:c + 1], stat[:, SSQ, c:c + 1], 1.0 / C, 1e-6 / 65536.0,
                                        ALU.mult, ALU.add).then_inc(s["msq"], 1)
                v.wait_ge(s["rs"], t + 1)
                v.wait_ge(s["ld_z0" if t < TC else "ld_z"], 16 if t < TC else 16 * (B - 1))
                nc.vector.scalar_tensor_tensor(z[:, t, :], ps[:, Y0 + c % 2, :], stat[:, RS, c:c + 1], z[:, t, :],
                                               ALU.mult, ALU.add).then_inc(s["x1"], 1)
                v.wait_ge(s["t1"], t + 1)
                v.wait_ge(s["q1t"], t + 1)
                nc.vector.scalar_tensor_tensor(xf[:, c, :], Tg[:, c % 2, :], 1.0, xf[:, c, :], ALU.add, ALU.mult,
                                               accum_out=stat[:, SUM, c:c + 1]).then_inc(s["mix"], 1)
                v.wait_ge(s["varr"], t + 1)
                nc.vector.tensor_scalar(stat[:, VAREPS, c:c + 1], stat[:, VAR, c:c + 1], 1.0 / C, 1e-5,
                                        ALU.mult, ALU.add).then_inc(s["varm"], 1)

            def stage2(t, c):
                v.wait_ge(s["gamd"], t + 1)
                nc.vector.tensor_tensor(xf[:, c, :], xf[:, c, :], bet[:, :], ALU.add).then_inc(s["xfd"], 1)
                v.wait_ge(s["sgnd"], t + 1)
                nc.vector.tensor_tensor(sgn[:, :], sgn[:, :], sig[:, :], ALU.mult).then_inc(s["ssd"], 1)
                v.wait_ge(s["ssd"], t + 1)
                nc.vector.tensor_reduce(ts[:, c, :], sgn[:, :].rearrange("p (t j) -> p t j", j=SLICE), axis=AX, op=ALU.add).then_inc(s["tsd"], 1)

            def choose(b):
                oh = onehot[:, TC * b:TC * (b + 1), :]
                tsv = ts[:, :, :].rearrange("p c (k i) -> p (c k) i", i=8)
                cmv = comp[:, :, :].rearrange("p c (k i) -> p (c k) i", i=8)
                csv = cs[:, :, :].rearrange("p c k -> p (c k)")
                v.wait_ge(s["tsd"], TC * (b + 1))
                link(nc.vector.tensor_reduce(csv, tsv, axis=AX, op=ALU.add))
                link(nc.vector.scalar_tensor_tensor(cmv, csv.unsqueeze(2).broadcast_to([P, TC * CLUSTERS, 8]), 2048.0,
                                                    rank[:, :, :].rearrange("p c (k i) -> p (c k) i", i=8), ALU.mult, ALU.add))
                link(nc.vector.scalar_tensor_tensor(comp[:, :, :], ts[:, :, :], 8.0, comp[:, :, :], ALU.mult, ALU.add))
                link(nc.vector.tensor_reduce(best[:, :], comp[:, :, :], axis=AX, op=ALU.max))
                nc.vector.tensor_tensor(oh, comp[:, :, :], best[:, :].unsqueeze(2).broadcast_to([P, TC, TILES]), ALU.is_equal).then_inc(s["ohd"], 1)

            def gather(b):
                oh = onehot[:, TC * b:TC * (b + 1), :]
                v.wait_ge(s["ohd"], b + 1)
                link(nc.vector.tensor_scalar(ts[:, :, :], oh, -BIG, BIG, ALU.mult, ALU.add))
                v.wait_ge(s["prodd"], b + 1)
                nc.vector.tensor_reduce(xs[:, TC * b:TC * (b + 1), :], xf[:, :, :].rearrange("p c (t j) -> p c j t", j=SLICE),
                                        axis=AX, op=ALU.add).then_inc(s["xsd"], 1)
                v.wait_ge(s["xsd"], b + 1)
                for i, op in enumerate((ALU.min, ALU.max)):
                    link(nc.vector.tensor_reduce(tmn[:, i, :], xs[:, TC * b:TC * (b + 1), :], axis=AX, op=op))
                    link(nc.vector.tensor_tensor(comp[:, :, :], oh, tmn[:, i, :].unsqueeze(2).broadcast_to([P, TC, TILES]), ALU.mult))
                    link(nc.vector.tensor_tensor(comp[:, :, :], comp[:, :, :], ts[:, :, :], (ALU.add, ALU.subtract)[i]))
                    link(nc.vector.tensor_reduce(mkv[:, i, :], comp[:, :, :].rearrange("p c t -> p t c"), axis=AX, op=op))
                    nc.vector.tensor_tensor(run[:, i, :], run[:, i, :], mkv[:, i, :], op).then_inc(s["rund"], 1)
                v.wait_ge(s["rund"], 2 * (b + 1))

            v.wait_ge(s["rank_done"], 2)
            v.wait_ge(s["run_init"], 2)
            for b in range(B):
                for j in range(PAIRS):
                    e = PAIRS * b + j
                    v.wait_ge(s["tg"], e + 1)
                    nc.vector.scalar_tensor_tensor(Tg[:, j % 2, :], Tg[:, j % 2, :], 1.0, ps[:, 2 * (j % 2), :], ALU.add, ALU.mult).then_inc(s["ag"], 1)
                    v.wait_ge(s["ag"], e + 1)
                    nc.vector.tensor_tensor(Tg[:, j % 2, :], Tg[:, j % 2, :], ps[:, 2 * (j % 2) + 1, :], ALU.mult).then_inc(s["hd"], 1)
                    if b > 0 and j == 0:
                        stage2(TC * b - 1, TC - 1)
                        choose(b - 1)
                    if b > 0 and j == 1:
                        gather(b - 1)
                    if b + 1 < B:
                        if j == 1:
                            shared(b + 1, 0)
                        if 2 <= j < 10:
                            half_step(b + 1, j - 2)
                        if j == 10:
                            ratio(b + 1, 7)
                for c in range(TC):
                    stage1(TC * b + c, c)
                    if c > 0:
                        stage2(TC * b + c - 1, c - 1)
            stage2(NCH - 1, TC - 1)
            choose(B - 1)
            gather(B - 1)
            v.wait_ge(s["rtr"], 2)
            nc.vector.tensor_reduce(lookt[:, 0:1], ps[0:TILES, Y0, 0:P], axis=AX, op=ALU.min).then_inc(s["rred"], 1)
            nc.vector.tensor_reduce(lookt[:, 1:2], ps[0:TILES, Y0, P:2 * P], axis=AX, op=ALU.max).then_inc(s["rred"], 1)
            v.wait_ge(s["lk"], 1)
            link(nc.vector.tensor_copy(lk[:, :, :].rearrange("p c i -> p (c i)"), ps[:, Y0 + 1, 0:2 * NCH]))
            link(nc.vector.tensor_tensor(rng[:, :], lk[:, :, 1], lk[:, :, 0], ALU.subtract))
            link(nc.vector.tensor_scalar(rng[:, :], rng[:, :], 1e-8, None, ALU.add))
            link(nc.vector.reciprocal(rng[:, :], rng[:, :]))
            wide = [P, NCH, SLICE]
            link(nc.vector.tensor_tensor(xs[:, :, :], xs[:, :, :], lk[:, :, 0].unsqueeze(2).broadcast_to(wide), ALU.subtract))
            link(nc.vector.tensor_tensor(xs[:, :, :], xs[:, :, :], rng[:, :].unsqueeze(2).broadcast_to(wide), ALU.mult))
            link(nc.vector.tensor_scalar(xs[:, :, :], xs[:, :, :], 0.0, 1.0 - 1e-6, ALU.max, ALU.min))
            link(nc.vector.tensor_scalar(xs[:, :, :], xs[:, :, :], float(GRID), None, ALU.mult))
            link(nc.vector.tensor_scalar(gi[:, :, :], xs[:, :, :], ROUND, -ROUND, ALU.add, ALU.add))
            link(nc.vector.tensor_tensor(gt[:, :, :], gi[:, :, :], xs[:, :, :], ALU.is_gt))
            link(nc.vector.tensor_tensor(gi[:, :, :], gi[:, :, :], gt[:, :, :], ALU.subtract))
            link(nc.vector.tensor_scalar(gi[:, :, :], gi[:, :, :], 0.0, float(GRID - 1), ALU.max, ALU.min))
            link(nc.vector.tensor_tensor(xs[:, :, :], xs[:, :, :], gi[:, :, :], ALU.subtract))
            n16 = NCH * SLICE
            g3 = [P, n16, GRID]
            link(nc.vector.tensor_tensor(oneh16.rearrange("p (n g) -> p n g", g=GRID),
                                         gi[:, :, :].rearrange("p c j -> p (c j)").unsqueeze(2).broadcast_to(g3),
                                         iota16[:, :].unsqueeze(1).broadcast_to(g3), ALU.is_equal))
            v.wait_ge(s["tabc"], NCH)
            for i, tbl in enumerate((looked, looked_s)):
                link(nc.vector.tensor_tensor(tbl, tbl, oneh16, ALU.mult))
                link(nc.vector.tensor_reduce(bs[:, i, :], tbl.rearrange("p (n g) -> p n g", g=GRID), axis=AX, op=ALU.add))
            xsf = xs[:, :, :].rearrange("p c j -> p (c j)")
            link(nc.vector.tensor_tensor(xsf, xsf, bs[:, 1, :], ALU.mult))
            link(nc.vector.tensor_tensor(xsf, xsf, bs[:, 0, :], ALU.add))
            link(nc.vector.tensor_tensor(xs[:, :, :], xs[:, :, :], osc[:, :].unsqueeze(2).broadcast_to(wide), ALU.mult))
            for c in range(NCH):
                o3 = [P, TILES, SLICE]
                link(nc.vector.tensor_tensor(Tg[:, c % 2, :].rearrange("p (t j) -> p t j", j=SLICE),
                                             onehot[:, c, :].unsqueeze(2).broadcast_to(o3),
                                             xs[:, c, :].unsqueeze(1).broadcast_to(o3), ALU.mult))
                nc.vector.tensor_tensor(z[:, c, :], z[:, c, :], Tg[:, c % 2, :], ALU.add).then_inc(s["fin2"], 1)


def kernel(x, fside_BxSxS_0, cond_512, L0_cond_w, L0_cond_u, L0_ffn_gate_up_packed, L0_ffn_gate_up_scales,
           L0_ffn_down_packed, L0_ffn_down_scales, L1_cond_w, L1_cond_u, L1_ffn_ln_gamma, L1_ffn_ln_beta,
           L1_ffn_spline_bases, L1_ffn_spline_slopes, L1_ffn_output_scale):
    import concourse.bacc as bacc
    from concourse.bass_utils import run_bass_kernel_spmd

    p = np.arange(P)
    q, r = p // 64, p % 64
    chan = np.stack([8 * r + 4 * q + m for m in range(CT)], 1)
    inner = [512 * (j // 4) + 8 * r + 4 * q + j % 4 for j in range(4 * FULL)]
    inner += [8 * (64 * FULL + 16 * t + p % 16) + p // 16 for t in range(REST)]
    order = np.concatenate([np.concatenate([i, i + INNER]) for i in inner])

    x = np.asarray(x)
    side = np.asarray(fside_BxSxS_0)
    gp = np.asarray(L0_ffn_gate_up_packed)
    gs = np.asarray(L0_ffn_gate_up_scales)
    dp = np.asarray(L0_ffn_down_packed)
    ds = np.asarray(L0_ffn_down_scales)
    xc = x.transpose(2, 0, 1)
    kc = side.transpose(2, 0, 1)
    arrays = {
        "xT": np.stack([xc[chan[:, m]] for m in range(CT)]),
        "kT": np.stack([kc[chan[:, m]] for m in range(CT)]),
        "x": x,
        "cond": np.asarray(cond_512),
        "w0": np.asarray(L0_cond_w)[chan], "w1": np.asarray(L1_cond_w)[chan],
        "u0": np.asarray(L0_cond_u)[chan], "u1": np.asarray(L1_cond_u)[chan],
        "gu_pack": gp[order].T[r],
        "gu_scale": gs[:, order][r // 16],
        "dn_pack": np.concatenate([dp.T[64 * b + r] for b in range(FULL)]
                                  + [dp.T[64 * FULL + 16 * t + p % 16] for t in range(REST)], 1),
        "dn_scale": np.concatenate([ds[4 * b + r // 16] for b in range(FULL)]
                                   + [ds[4 * FULL + t + 0 * p] for t in range(REST)], 1),
        "gamma": np.asarray(L1_ffn_ln_gamma), "beta": np.asarray(L1_ffn_ln_beta),
        "bases": np.asarray(L1_ffn_spline_bases), "slopes": np.asarray(L1_ffn_spline_slopes),
        "oscale": np.asarray(L1_ffn_output_scale),
    }
    nc = bacc.Bacc("TRN2", target_bir_lowering=False, num_devices=1)
    feed, args = {}, []
    for name, a in arrays.items():
        a = np.ascontiguousarray(a)
        feed[f"in_{name}"] = a
        args.append(nc.dram_tensor(f"in_{name}", a.shape, mybir.dt.from_np(a.dtype), kind="ExternalInput").ap())
    args.append(nc.dram_tensor("out_0", (B, T, C), mybir.dt.float32, kind="ExternalOutput").ap())
    build_program(nc, *args)
    res = run_bass_kernel_spmd(nc, [feed], core_ids=[0])
    return res.results[0]["out_0"]
```

```python
from contextlib import ExitStack

import concourse.bass as bass
import numpy as np
from concourse import mybir

B, T, C = 4, 512, 512
P = 128
CT = C // P
TC = T // P
NCH = B * TC
INNER = 1408
PAIRS = INNER // P
TD = 128
TILES, SLICE, GRID = 64, 8, 16
CLUSTERS = TILES // 8
FULL = 2
REST = PAIRS - 4 * FULL
BIG = float(2.0 ** 126)
SEED = float(0x7EF311C3)
E30 = float(np.exp(np.float64(30.0)))
UNPACK = (3, 3, 1, 1, 1, 1, 1, 1, 0, 0, 0)
JG = 3
N_POOL = 9
PLACES0 = (1, 2, 3, 4, 5, 6, 8, 9, 10, 11, 12)
PLACES = (1, 2, 4, 5, 7, 8, 10, 11, 12, 13)
ROUND = float(2 ** 23)
SEED_E = 0.0506


def reciprocal_factors():
    cheb = np.polynomial.chebyshev.Chebyshev([0, 0, 0, 0, 0, 1]).convert(kind=np.polynomial.Polynomial)
    top = float(cheb(1 / SEED_E))
    num = np.array([1.0 if i == 0 else 0.0 for i in range(6)]) - cheb.coef / top / SEED_E ** np.arange(6)
    quot, _ = np.polynomial.polynomial.polydiv(num, np.array([1.0, -1.0]))
    roots = np.polynomial.polynomial.polyroots(quot)
    roots = [r for r in roots if r.imag > 0]
    lead = np.sqrt(quot[4])
    return [(float(np.sqrt(lead)), float(-np.sqrt(lead) * r.real), float(lead * r.imag ** 2)) for r in roots]


def build_program(nc, xT, kT, x, cond, w0, w1, u0, u1, gu_pack, gu_scale, dn_pack, dn_scale,
                  gamma, beta, bases, slopes, oscale, out):
    f32, f16, bf16 = mybir.dt.float32, mybir.dt.float16, mybir.dt.bfloat16
    i32, u16 = mybir.dt.int32, mybir.dt.uint16
    ALU, ACT, AX = mybir.AluOpType, mybir.ActivationFunctionType, mybir.AxisListType.X

    steps = [(0, m, 0) for m in range(CT)] + [(0, m, 1) for m in range(CT)]
    steps += [(b, m, l) for b in range(1, B) for m in range(CT) for l in range(2)]
    shares = []
    for k, (b, m, l) in enumerate(steps):
        shares.append((shares[-1] if k and steps[k - 1][:2] == (b, m) else shares[-1] + 1) if k else 0)
    fresh = [k == 0 or shares[k] != shares[k - 1] for k in range(len(steps))]
    last_of = {n: k for k, n in enumerate(shares)}
    first_of = {n: k for k, n in reversed(list(enumerate(shares)))}
    based_at = {(b, m): i for i, (b, m) in enumerate((b, m) for b, m, l in steps if l == 0)}
    factors = reciprocal_factors()

    ctx = ExitStack()
    with ctx:
        def sb(name, shape, dt):
            return ctx.enter_context(nc.sbuf_tensor(name, shape, dt))

        def sem(name):
            return ctx.enter_context(nc.semaphore(name))

        wg_hi = sb("wg_hi", [P, CT, 2 * INNER], f16)
        wg_lo = sb("wg_lo", [P, CT, 2 * INNER], bf16)
        wd_hi = sb("wd_hi", [P, PAIRS, C], f16)
        wd_lo = sb("wd_lo", [P, PAIRS, C], bf16)
        z = sb("z", [P, NCH, C], f32)
        q1 = sb("q1", [P, CT, T], f32)
        base_hi = sb("base_hi", [P, CT, T], f16)
        base_lo = sb("base_lo", [P, CT, T], f16)
        h_hi = sb("h_hi", [P, PAIRS, T], f16)
        h_lo = sb("h_lo", [P, PAIRS, T], f16)
        kbuf = sb("kbuf", [P, 2, T], f32)
        xTb = sb("xTb", [P, CT, T], f32)
        xf = sb("xf", [P, TC, C], f32)
        E = sb("E", [P, T], f32)
        vs = sb("vs", [P, 2, T], f32)
        ekv = sb("ekv", [P, T], f32)
        EU = sb("EU", [P, 2, T], f32)
        F = sb("F", [P, 2, 2, T], f32)
        G = sb("G", [P, 2, 2, T], f32)
        Tg = sb("Tg", [P, 2, T], f32)
        gam = sb("gam", [P, C], f32)
        bet = sb("bet", [P, C], f32)
        sig = sb("sig", [P, C], bf16)
        sgn = sb("sgn", [P, C], bf16)
        onehot = sb("onehot", [P, NCH, TILES], bf16)
        ts = sb("ts", [P, TC, TILES], f32)
        comp = sb("comp", [P, TC, TILES], f32)
        cand = sb("cand", [P, TC, TILES], f32)
        cs = sb("cs", [P, TC, CLUSTERS], f32)
        rank = sb("rank", [P, TC, TILES], f32)
        best = sb("best", [P, TC], f32)
        xs = sb("xs", [P, NCH, SLICE], f32)
        tmn = sb("tmn", [P, 2, TC], f32)
        mkv = sb("mkv", [P, 2, TILES], f32)
        run = sb("run", [P, 2, TILES], f32)
        ident = sb("ident", [P, P], f32)
        identh = sb("identh", [P, P], bf16)
        decay = sb("decay", [P, 2, CT, B], f32)
        kappa = sb("kappa", [P, 2, CT, B], f32)
        cap = sb("cap", [P, 2, CT, B], f32)
        floor = sb("floor", [P, 2, CT, B], f32)
        wl = sb("wl", [P, 2, CT], f32)
        ul = sb("ul", [P, 2, CT], f32)
        tf = sb("tf", [P, 3, B], f32)
        sc = sb("sc", [P, B], f32)
        half = sb("half", [P, 1], f32)
        stat = sb("stat", [P, 9, TC], f32)
        shq = sb("shq", [P, 3], i32)
        junk = sb("junk", [P, 2, C], bf16)
        ones = sb("ones", [TILES, P], bf16)
        iota16 = sb("iota16", [P, GRID], bf16)
        lk = sb("lk", [P, NCH, 3], f32)
        knot = sb("knot", [P, NCH * SLICE], bf16)
        rng = sb("rng", [P, NCH], f32)
        lookt = sb("lookt", [TILES, 3], f32)
        lookr = sb("lookr", [TILES, 3], f32)
        look_part = sb("look_part", [TILES, 3, 3], bf16)

        z_w = z[:, TC:NCH, :].rearrange("p a b -> p (a b)")
        z_i, z_u = z_w.bitcast(i32), z_w.bitcast(u16)
        DN = (FULL + REST) * C
        gp_i = z_i[:, 0:2 * INNER]
        dp_i = z_i[:, 2 * INNER:2 * INNER + DN]
        PIECE, GP, NBUF = 1024, 4 * INNER, 3
        code = [z_u[:, o:o + PIECE] for o in (0, PIECE, 2 * PIECE + DN)]
        dn_u = z_u[:, 2 * PIECE:2 * PIECE + DN]
        dn_a = z_u[:, GP:GP + DN].bitcast(bf16)
        dn_b = z_u[:, GP + DN:GP + 2 * DN].bitcast(bf16)
        hh = h_hi[:, :, :].rearrange("p a b -> p (a b)")
        hl = h_lo[:, :, :].rearrange("p a b -> p (a b)")
        gu_u = hl[:, DN:DN + 2 * INNER].bitcast(u16)
        gu_a = hh[:, DN:DN + 2 * INNER].bitcast(bf16)
        gs_h = xf[:, :, :].rearrange("p a b -> p (a b)").bitcast(f16)[:, 0:2 * INNER]
        gu_b = gs_h.bitcast(bf16)
        ds_h = hh[:, 0:DN]
        xTf = xTb[:, :, :].rearrange("p a b -> p (a b)")
        KNOTS = SLICE * GRID
        Gf = G[:, :, :, :].rearrange("p a b c -> p (a b c)").bitcast(bf16)
        ohT = Gf[0:TILES, 0:NCH * P]
        tab = vs[:, :, :].rearrange("p a b -> p (a b)")[0:TILES, 0:2 * KNOTS]
        tab_rest = EU[:, :, :].rearrange("p a b -> p (a b)")[0:TILES, 0:2 * KNOTS]
        tab_part = ekv[:, :].bitcast(bf16)[0:TILES, 0:6 * KNOTS].rearrange("p (a b) -> p a b", a=3)
        looked = xTb[:, :, :].rearrange("p a b -> p (a b)")
        looked_s = F[:, :, :, :].rearrange("p a b c -> p (a b c)")
        gi = E[:, 0:NCH * SLICE].rearrange("p (c j) -> p c j", j=SLICE)
        gt = E[:, NCH * SLICE:2 * NCH * SLICE].rearrange("p (c j) -> p c j", j=SLICE)
        bs = E[:, 2 * NCH * SLICE:4 * NCH * SLICE].rearrange("p (i n) -> p i n", i=2)
        knot_hot = kbuf[:, :, :].rearrange("p a b -> p (a b)").bitcast(bf16)[:, 0:NCH * KNOTS]

        ps = ctx.enter_context(nc.psum_tensor("ps", [P, 8, 512], f32))
        Y0, TR0 = 4, 6

        names = ("ld_k0 ld_k1 ld_z0 ld_x ld_z ld_pack0 ld_pack1 ld_scale0 ld_scale1 ld_small ld_late ld_tab st_out "
                 "iota_done half_set kap sclA sclB dor dhi dlo tf_sum tf_tanh tf_scale tf_decay w_exp w_exp2 dec_done sc_done "
                 "shift_set shift_set2 halves compact dmag dsgn dval dprod whi wlo "
                 "slope_sum slope_sgn sig_mask sig_rhs sig_bc sig_done rank_done run_init ident_done "
                 "km ex vsc ekvd eu euk edge sf sg euv den denm num seed pd wq e2 e4 fa fq tx based bhi blo "
                 "gu tg ag hd hhi hlo tr q1t yd ssq msq rs x1 t1 mix zadd nmean varr varm rstd nbias xn gamd xfd "
                 "sgnd ssd tsd csd cmp1 cmp2 bestd range_step ohd prodd xsd tmnd tmxd mk1 mk2 mk3 rund rund2 "
                 "ohtr ohtc tabm tabc rtr rred lk lkc g1 g2 g3 g4 g5 g6 g7 g8 g9 g10 g11 look_split tabsp spl pact ppool fin_pool fin_dve bnz ones tabl").split()
        s = {n: sem(n) for n in names}

        SSQ, RS, SUM, NMEAN, VAR, RSTD, VAREPS, SSQEPS, NBIAS = range(9)

        def rev(ap):
            return ap[:, ::-1]

        unpack = []
        for j in range(PAIRS):
            cols = slice(2 * P * j, 2 * P * (j + 1))
            unpack.append(([(gu_u[:, cols], 4 * m) for m in range(CT)], CT, 2 * P, (gu_a, gu_b, cols),
                           (wg_hi[:, :, cols], wg_lo[:, :, cols])))
        for i in range(FULL):
            for m in (0, 2):
                cols, tiles = slice(C * i, C * (i + 1)), slice(CT * i + m, CT * i + m + 2)
                unpack.append(([(dn_u[:, cols], 4 * m), (dn_u[:, cols], 4 * m + 4)], 2, C, (dn_a, dn_b, cols),
                               (wd_hi[:, tiles, :], wd_lo[:, tiles, :])))
        for t, n in ((0, 2), (2, 1)):
            cols = slice(C * (FULL + t), C * (FULL + t + n))
            tiles = slice(CT * FULL + t, CT * FULL + t + n)
            unpack.append(([(dn_u[:, C * (FULL + t + i):C * (FULL + t + i + 1)], 0) for i in range(n)], n, C,
                           (dn_a, dn_b, cols), (wd_hi[:, tiles, :], wd_lo[:, tiles, :])))
        done = 0
        for i, u in enumerate(unpack):
            done += u[1]
            unpack[i] = (*u, done)

        def value(i):
            return code[i % NBUF][:, 0:unpack[i][1] * unpack[i][2]].bitcast(f16).rearrange("p (m n) -> p m n", m=unpack[i][1])

        def factor(i, scales):
            _, nt, n, (_, _, cols), _, _ = unpack[i]
            if i >= PAIRS + 4:
                return scales[:, cols].rearrange("p (m n) -> p m n", m=nt)
            return scales[:, cols].unsqueeze(1).broadcast_to([P, nt, n])

        def unpack_with(j):
            return list(range(5, PAIRS + 6))[sum(UNPACK[:j]):sum(UNPACK[:j + 1])]

        places = [PLACES0] + [PLACES] * (B - 2) + [()]

        def mixing(b, i):
            if i not in places[b]:
                return None, None, None
            start = 7 if b == 0 else 8 * (b + 1)
            end = 8 * (b + 2)
            k = start + places[b].index(i)
            return (k if k < end else None, k - 1 if (b == 0 or k > start) and k <= end else None,
                    k - 2 if b == 0 or k > start + 1 else None)

        def splits(b, i):
            if i < PAIRS or b == B - 1:
                return []
            ready = {m: max(PAIRS, places[b][steps.index((b + 1, m, 0)) - (7 if b == 0 else 8 * (b + 1)) + 2])
                     for m in range(CT)}
            return [m for m in range(CT) if ready[m] == i]

        by_pool = list(range(N_POOL))
        by_dve = list(range(N_POOL, NCH))
        by_act = by_pool[1::2]

        def chosen_bank(b):
            half_bank = ps[0:TILES, (4, 4, 5, 0)[b], :].bitcast(bf16)
            return half_bank[:, (b == 1) * TC * P:((b == 1) + 1) * TC * P]

        def table_bank(i):
            return (6, 7, 4, 5, 6, 7, 1, 2)[i]

        block = ctx.enter_context(nc.Block())
        xT_v = xT
        kT_v = kT

        @block.sync
        def _(sp):
            def load_k(n):
                b, m, _ = steps[first_of[n]]
                if n >= 2:
                    sp.wait_ge(s["eu"], last_of[n - 2] + 1)
                    sp.wait_ge(s["vsc"], n - 1)
                    sp.wait_ge(s["km"], n - 1)
                sp.dma_start(kbuf[:, n % 2, :], kT[m, :, b, :]).then_inc(s["ld_k%d" % (n % 2)], 16)

            def load_x(b):
                if b > 0:
                    sp.wait_ge(s["blo"], 4 * b)
                sp.dma_start(xTb[:, :, :], xT[:, :, b, :].rearrange("m p t -> p m t")).then_inc(s["ld_x"], 16)

            load_k(0)
            for l, (wv, uv) in enumerate(((w0, u0), (w1, u1))):
                sp.dma_start(wl[:, l, :], wv).then_inc(s["ld_small"], 16)
                sp.dma_start(ul[:, l, :], uv).then_inc(s["ld_small"], 16)
            sp.dma_start(Tg[:, 1, :], cond.rearrange("(o b) t -> o (b t)", o=1).broadcast_to([P, B * TD])).then_inc(s["ld_small"], 16)
            sp.dma_start(gp_i, gu_pack).then_inc(s["ld_pack0"], 16)
            sp.dma_start(gs_h, gu_scale).then_inc(s["ld_scale0"], 16)
            load_k(1)
            load_x(0)
            sp.dma_start(dp_i, dn_pack).then_inc(s["ld_pack1"], 16)
            sp.dma_start(ds_h, dn_scale).then_inc(s["ld_scale1"], 16)
            sp.dma_start(Tg[0:TILES, 0, 0:SLICE * GRID], slopes.rearrange("t j g -> t (j g)")).then_inc(s["ld_late"], 16)
            sp.dma_start(gam[:, :], gamma.rearrange("(o n) -> o n", o=1).broadcast_to([P, C])).then_inc(s["ld_late"], 16)
            sp.dma_start(bet[:, :], beta.rearrange("(o n) -> o n", o=1).broadcast_to([P, C])).then_inc(s["ld_late"], 16)
            sp.dma_start(z[:, 0:TC, :], x[0].rearrange("(c p) n -> p c n", p=P)).then_inc(s["ld_z0"], 16)
            for n in range(2, 10):
                load_k(n)
            load_x(1)
            for n in range(10, 12):
                load_k(n)
            sp.wait_ge(s["dlo"], PAIRS + 6)
            sp.wait_ge(s["dhi"], PAIRS + 6)
            for b in range(1, B):
                sp.dma_start(z[:, TC * b:TC * (b + 1), :],
                             x[b].rearrange("(c p) n -> p c n", p=P)).then_inc(s["ld_z"], 16)
            for n in range(12, 14):
                load_k(n)
            load_x(2)
            for n in range(14, 18):
                load_k(n)
            load_x(3)
            for n in range(18, 20):
                load_k(n)
            sp.wait_ge(s["fq"], len(steps))
            sp.dma_start(tab[:, 0:KNOTS], bases.rearrange("t j g -> t (j g)")).then_inc(s["ld_tab"], 16)
            sp.dma_start(tab[:, KNOTS:], slopes.rearrange("t j g -> t (j g)")).then_inc(s["ld_tab"], 16)
            sp.dma_start(lookt[:, 2:3], oscale.rearrange("(t a) -> t a", a=1)).then_inc(s["ld_tab"], 16)
            order = sorted([(i / len(by_pool), "fin_pool", i + 1, c) for i, c in enumerate(by_pool)]
                           + [((i + len(by_dve)) / 2 / len(by_dve), "fin_dve", i + 1, c) for i, c in enumerate(by_dve)])
            for _, name, n, c in order:
                sp.wait_ge(s[name], n)
                sp.dma_start(out[c // TC, (c % TC) * P:(c % TC + 1) * P, :], z[:, c, :]).then_inc(s["st_out"], 16)
            sp.wait_ge(s["st_out"], 16 * NCH)

        @block.gpsimd
        def _(g):
            g.memset(ident[:, :], 0.0).then_inc(s["ident_done"], 1)
            g.wait_ge(s["ident_done"], 1)
            g.affine_select(out=ident[:, :], in_=ident[:, :], compare_op=ALU.not_equal, fill=1.0, base=0,
                            pattern=[[-1, P]], channel_multiplier=1).then_inc(s["ident_done"], 1)
            g.wait_ge(s["ident_done"], 2)
            g.tensor_copy(identh[:, :], ident[:, :]).then_inc(s["ident_done"], 1)
            g.iota(shq[:, 0:1], pattern=[[0, 1]], base=0, channel_multiplier=1).then_inc(s["iota_done"], 1)
            g.iota(comp[:, :, :].bitcast(i32), pattern=[[0, TC], [-256, CLUSTERS], [-1, 8]], base=0, channel_multiplier=0).then_inc(s["iota_done"], 1)
            g.wait_ge(s["iota_done"], 2)
            g.tensor_copy(rank[:, :, :], comp[:, :, :].bitcast(i32)).then_inc(s["rank_done"], 1)
            g.iota(cs[:, 0:2, :].bitcast(i32), pattern=[[1, GRID]], base=0, channel_multiplier=0).then_inc(s["iota_done"], 1)
            g.wait_ge(s["iota_done"], 3)
            g.tensor_copy(iota16[:, :], cs[:, 0:2, :].rearrange("p a b -> p (a b)").bitcast(i32)).then_inc(s["rank_done"], 1)
            g.memset(ones[:, :], 1.0).then_inc(s["ones"], 1)
            g.memset(half[:, :], -0.5).then_inc(s["half_set"], 1)
            g.memset(run[:, 0, :], BIG).then_inc(s["run_init"], 1)
            g.memset(run[:, 1, :], -BIG).then_inc(s["run_init"], 1)
            def exponentials(n):
                g.wait_ge(s["ex"], n + 1)
                g.wait_ge(s["vsc"], n + 1)
                if n > 0:
                    g.wait_ge(s["sf"], 2 * last_of[n - 1] + 2)
                g.tensor_tensor(ekv[:, :], E[:, :], vs[:, n % 2, :], ALU.mult).then_inc(s["ekvd"], 1)

            def seeded(k):
                i = k % 2
                g.wait_ge(s["euv"], k + 1)
                g.wait_ge(s["sg"], 2 * k + 2)
                g.tensor_tensor(G[:, i, 1, :], G[:, i, 1, :], F[:, i, 1, :], ALU.add).then_inc(s["num"], 1)
                g.wait_ge(s["seed"], k + 1)
                g.tensor_tensor(EU[:, i, :], G[:, i, 0, :], F[:, i, 0, :], ALU.mult).then_inc(s["pd"], 1)
                g.wait_ge(s["num"], k + 1)
                g.tensor_tensor(G[:, i, 1, :], G[:, i, 1, :], F[:, i, 0, :], ALU.mult).then_inc(s["wq"], 1)

            def slot(k):
                if k < len(steps) and fresh[k]:
                    exponentials(shares[k])
                seeded(k - 1)

            def split_base(b, ms=range(CT)):
                for m in ms:
                    g.wait_ge(s["bhi"], 4 * b + m + 1)
                    g.tensor_tensor(base_lo[:, m, :], xTb[:, m, :], base_hi[:, m, :], ALU.subtract).then_inc(s["blo"], 1)

            def slope_signs():
                g.wait_ge(s["slope_sgn"], 1)
                g.affine_select(out=sgn[0:TILES, :].rearrange("p (t j) -> p t j", j=SLICE),
                                in_=ts[0:TILES, 1, 0:SLICE].unsqueeze(1).broadcast_to([TILES, TILES, SLICE]),
                                compare_op=ALU.is_equal, fill=0.0, base=0,
                                pattern=[[-1, TILES], [0, SLICE]], channel_multiplier=1).then_inc(s["sig_rhs"], 1)

            def low_product(i):
                _, nt, n, (_, sb_, cols), (_, lo), _ = unpack[i]
                g.wait_ge(s["dval"], i + 1)
                g.wait_ge(s["sclB"], 1 if i < PAIRS else 2)
                g.tensor_tensor(lo, value(i), factor(i, sb_), ALU.mult).then_inc(s["dlo"], 1)

            exponentials(0)
            for k in range(1, 7):
                slot(k)
                if k >= 2:
                    low_product(k - 2)
                if k == 3:
                    slope_signs()
                if k == 5:
                    split_base(0)

            def rows(t, first=True, second=True, scan=None):
                c, c1 = t % TC, (t - 1) % TC
                if second:
                    g.wait_ge(s["varm"], t)
                    g.tensor_tensor(stat[:, RSTD, c1:c1 + 1], stat[:, VAREPS, c1:c1 + 1], half[:, :], ALU.pow).then_inc(s["rstd"], 1)
                if first:
                    g.wait_ge(s["msq"], t + 1)
                    g.tensor_tensor(stat[:, RS, c:c + 1], stat[:, SSQEPS, c:c + 1], half[:, :], ALU.pow).then_inc(s["rs"], 1)
                if scan is not None and fresh[scan]:
                    exponentials(shares[scan])
                if second:
                    g.wait_ge(s["xn"], t)
                    g.tensor_tensor(xf[:, c1, :], xf[:, c1, :], gam[:, :], ALU.mult).then_inc(s["gamd"], 1)
                if first:
                    g.wait_ge(s["mix"], t + 1)
                    g.tensor_tensor(z[:, t, :], z[:, t, :], xf[:, c, :], ALU.add).then_inc(s["zadd"], 1)

            def select_slice(b, n=TC):
                g.wait_ge(s["ohd"], b + 1)
                g.wait_ge(s["xfd"], TC * b + n)
                g.tensor_tensor(xf[:, 0:n, :].rearrange("p c (t j) -> p (c t) j", j=SLICE),
                                xf[:, 0:n, :].rearrange("p c (t j) -> p (c t) j", j=SLICE),
                                onehot[:, TC * b:TC * b + n, :].rearrange("p c t -> p (c t)").unsqueeze(2)
                                .broadcast_to([P, n * TILES, SLICE]), ALU.mult).then_inc(s["prodd"], 1)

            def mix(b, i):
                scan, weigh, _ = mixing(b, i)
                if scan is not None and fresh[scan] and i < PAIRS:
                    exponentials(shares[scan])
                if weigh is not None:
                    seeded(weigh)

            def iteration(b, last):
                for j in range(PAIRS):
                    e = PAIRS * b + j
                    g.wait_ge(s["hhi"], e + 1)
                    g.tensor_tensor(h_lo[:, j, :], Tg[:, j % 2, :], h_hi[:, j, :], ALU.subtract).then_inc(s["hlo"], 1)
                    if b > 0 and j == 0:
                        rows(TC * b, first=False)
                    if b > 0 and j == 2:
                        select_slice(b - 1)
                    if b == 0:
                        for i in unpack_with(j):
                            low_product(i)
                    mix(b, j)
                for c in range(TC):
                    rows(TC * b + c, second=c > 0, scan=mixing(b, PAIRS + c)[0])
                    mix(b, PAIRS + c)
                    split_base(b + 1, splits(b, PAIRS + c))

            g.wait_ge(s["ld_late"], 16 * 3)
            for b in range(B):
                iteration(b, b == B - 1)
            rows(NCH, first=False)
            select_slice(B - 1, TC - 1)
            for n, c in enumerate(by_pool):
                g.wait_ge(s["spl"], c // TC + 1)
                if c in by_act:
                    i = by_act.index(c)
                    g.wait_ge(s["pact"], i + 1)
                    add = Tg[:, i % 2, :]
                else:
                    add = xf[:, c % TC, :]
                    g.tensor_tensor(add.rearrange("p (t j) -> p t j", j=SLICE),
                                    onehot[:, c, :].unsqueeze(2).broadcast_to([P, TILES, SLICE]),
                                    xs[:, c, :].unsqueeze(1).broadcast_to([P, TILES, SLICE]), ALU.mult).then_inc(s["ppool"], 1)
                    g.wait_ge(s["ppool"], n - sum(a < c for a in by_act) + 1)
                g.tensor_tensor(z[:, c, :], z[:, c, :], add, ALU.add).then_inc(s["fin_pool"], 1)

        @block.scalar
        def _(a):
            a.wait_ge(s["ld_small"], 16 * 5)
            a.activation(wl[:, :, :], wl[:, :, :], ACT.Exp).then_inc(s["w_exp"], 1)
            a.wait_ge(s["w_exp"], 1)
            a.activation(wl[:, :, :], wl[:, :, :], ACT.Exp, scale=-1.0).then_inc(s["w_exp"], 1)
            a.wait_ge(s["tf_sum"], 1)
            a.activation(tf[:, 1, :], tf[:, 0, :], ACT.Tanh, scale=0.5).then_inc(s["tf_tanh"], 1)
            def compact(n, dst, src, waits):
                a.wait_ge(s["halves"], waits)
                if n == 1:
                    a.wait_ge(s["compact"], 1)
                a.activation(dst, src.bitcast(u16)[:, ::2], ACT.Copy).then_inc(s["compact"], 1)

            def sign_carry(i):
                n = unpack[i][1] * unpack[i][2]
                a.wait_ge(s["dmag"], unpack[i][5])
                a.activation(code[i % NBUF][:, 0:n], code[i % NBUF][:, 0:n], ACT.Copy, bias=float(0x7000)).then_inc(s["dsgn"], 1)

            def exponentials(n):
                b, m, _ = steps[first_of[n]]
                a.wait_ge(s["km"], n + 1)
                a.activation(E[:, :], E[:, :], ACT.Exp).then_inc(s["ex"], 1)
                if n >= 2:
                    a.wait_ge(s["euv"], last_of[n - 2] + 1)
                    a.wait_ge(s["ekvd"], n - 1)
                a.activation(vs[:, n % 2, :], kbuf[:, n % 2, :], ACT.Copy, scale=sc[:, b:b + 1]).then_inc(s["vsc"], 1)

            def own_exp(k):
                b, m, l = steps[k]
                i = k % 2
                if not fresh[k]:
                    a.wait_ge(s["km"], shares[k] + 1)
                if k >= 2:
                    a.wait_ge(s["e2"], 2 * k - 2)
                a.activation(EU[:, i, :], kbuf[:, shares[k] % 2, :], ACT.Exp, bias=ul[:, l, m:m + 1]).then_inc(s["eu"], 1)
                a.wait_ge(s["eu"], k + 1)
                a.activation(EU[:, i, :], EU[:, i, :], ACT.Copy, scale=kappa[:, l, m, b:b + 1]).then_inc(s["euk"], 1)

            def seed(k):
                i = k % 2
                a.wait_ge(s["denm"], k + 1)
                a.activation(F[:, i, 0, :].bitcast(i32), G[:, i, 0, :].bitcast(i32), ACT.Copy, scale=-1.0, bias=SEED).then_inc(s["seed"], 1)

            def squares(k):
                i = k % 2
                a.wait_ge(s["wq"], k + 1)
                for (sl, tt, _), dst in zip(factors, (F[:, i, 1, :], F[:, i, 0, :])):
                    a.activation(dst, EU[:, i, :], ACT.Square, scale=-sl, bias=sl + tt).then_inc(s["e2"], 1)

            def tanh_x(b, m):
                if m == 0:
                    a.wait_ge(s["ld_x"], 16 * (b + 1))
                a.activation(xTb[:, m, :], xTb[:, m, :], ACT.Tanh, scale=0.5).then_inc(s["tx"], 1)

            def slot(k):
                if k >= 2:
                    squares(k - 2)
                if fresh[k]:
                    exponentials(shares[k])
                own_exp(k)
                if k >= 1:
                    seed(k - 1)
                if steps[k][2] == 0:
                    tanh_x(steps[k][0], steps[k][1])

            def split_base(b, ms=range(CT)):
                for m in ms:
                    a.wait_ge(s["based"], 4 * b + m + 1)
                    if b > 0:
                        a.wait_ge(s["gu"], PAIRS * b)
                    a.activation(base_hi[:, m, :], xTb[:, m, :], ACT.Copy).then_inc(s["bhi"], 1)

            a.wait_ge(s["sc_done"], 3)
            slot(0)
            compact(0, gu_u, gp_i, 1)
            a.wait_ge(s["ld_scale0"], 16)
            a.activation(gu_a, gs_h, ACT.Copy, scale=4096.0).then_inc(s["sclA"], 1)
            sign_carry(0)
            slot(1)
            for k in range(2, 7):
                if fresh[k]:
                    exponentials(shares[k])
                sign_carry(k - 1)
                squares(k - 2)
                own_exp(k)
                seed(k - 1)
                if steps[k][2] == 0:
                    tanh_x(steps[k][0], steps[k][1])
                if k == 2:
                    compact(1, dn_u, dp_i, 3)
                if k == 3:
                    a.wait_ge(s["compact"], 2)
                    a.wait_ge(s["ld_scale1"], 16)
                    a.activation(dn_a, ds_h, ACT.Copy, scale=16384.0).then_inc(s["sclA"], 1)
                    a.wait_ge(s["slope_sum"], 1)
                    a.activation(ts[0:TILES, 1, 0:SLICE], ts[0:TILES, 0, 0:SLICE], ACT.Sign).then_inc(s["slope_sgn"], 1)
                if k == 5:
                    split_base(0)

            def rows(t, first=True, second=True, third=True, mixes=(None, None, None)):
                c, c1, c2 = t % TC, (t - 1) % TC, (t - 2) % TC
                if second:
                    a.wait_ge(s["nmean"], t)
                    a.activation(junk[:, 1, :], xf[:, c1, :], ACT.Square, bias=stat[:, NMEAN, c1:c1 + 1],
                                 accum_out=stat[:, VAR, c1:c1 + 1]).then_inc(s["varr"], 1)
                if first:
                    a.wait_ge(s["yd"], t + 1)
                    a.activation(junk[:, 0, :], ps[:, Y0 + c, :], ACT.Square, accum_out=stat[:, SSQ, c:c + 1]).then_inc(s["ssq"], 1)
                if first and mixes[2] is not None:
                    squares(mixes[2])
                if third:
                    a.wait_ge(s["xfd"], t - 1)
                    if t > 2:
                        a.wait_ge(s["tsd"], t - 2)
                    a.activation(sgn[:, :], xf[:, c2, :], ACT.Sign).then_inc(s["sgnd"], 1)
                if second:
                    a.wait_ge(s["rstd"], t)
                    a.activation(stat[:, NBIAS, c1:c1 + 1], stat[:, NMEAN, c1:c1 + 1], ACT.Copy, scale=stat[:, RSTD, c1:c1 + 1]).then_inc(s["nbias"], 1)
                    a.wait_ge(s["nbias"], t)
                    a.wait_ge(s["zadd"], t)
                    a.activation(xf[:, c1, :], xf[:, c1, :], ACT.Identity, scale=stat[:, RSTD, c1:c1 + 1],
                                 bias=stat[:, NBIAS, c1:c1 + 1]).then_inc(s["xn"], 1)
                if first and mixes[0] is not None and fresh[mixes[0]]:
                    exponentials(shares[mixes[0]])
                if first:
                    a.wait_ge(s["x1"], t + 1)
                    a.activation(Tg[:, c % 2, :], z[:, t, :], ACT.Tanh, scale=0.5).then_inc(s["t1"], 1)
                    a.wait_ge(s["mix"], t + 1)
                    a.activation(stat[:, NMEAN, c:c + 1], stat[:, SUM, c:c + 1], ACT.Copy, scale=-1.0 / C).then_inc(s["nmean"], 1)

            def q1_rows(b):
                for c in range(TC):
                    t = TC * b + c
                    a.wait_ge(s["tr"], t + 1)
                    if b > 0:
                        a.wait_ge(s["xsd"], b)
                    a.activation(xf[:, c, :].rearrange("p (r q m) -> p m q r", q=2, m=CT),
                                 ps[:, Y0 + c, :].rearrange("p (m q r) -> p m q r", m=CT, q=2),
                                 ACT.Copy).then_inc(s["q1t"], 1)

            def copy_chosen(b):
                a.wait_ge(s["ohtr"], TC * (b + 1))
                if b == 0:
                    a.wait_ge(s["fq"], len(steps))
                a.activation(ohT[:, TC * P * b:TC * P * (b + 1)], chosen_bank(b), ACT.Copy).then_inc(s["ohtc"], 1)

            def copy_tables(pairs):
                for i in pairs:
                    a.wait_ge(s["tabm"], i + 1)
                    a.wait_ge(s["blo"], B * CT)
                    both = ps[:, table_bank(i), :].rearrange("p (c k) -> p c k", c=2)
                    for dst, cols in ((looked, slice(0, KNOTS)), (looked_s, slice(KNOTS, 2 * KNOTS))):
                        a.activation(dst[:, 2 * KNOTS * i:2 * KNOTS * (i + 1)].rearrange("p (c k) -> p c k", c=2),
                                     both[:, :, cols], ACT.Copy).then_inc(s["tabc"], 1)

            def mix(b, i):
                scan, weigh, _ = mixing(b, i)
                if scan is not None:
                    if fresh[scan] and i < PAIRS:
                        exponentials(shares[scan])
                    own_exp(scan)
                if weigh is not None:
                    seed(weigh)
                if scan is not None and steps[scan][2] == 0:
                    tanh_x(*steps[scan][:2])

            for b in range(B):
                for j in range(PAIRS):
                    e = PAIRS * b + j
                    a.wait_ge(s["gu"], e + 1)
                    if j >= 2:
                        a.wait_ge(s["hlo"], e - 1)
                    elif b > 0:
                        a.wait_ge(s["hlo"], PAIRS * b)
                        a.wait_ge(s["mix"], TC * b)
                    a.activation(Tg[:, j % 2, :], ps[:, 2 * (j % 2), :], ACT.Tanh, scale=2.0).then_inc(s["tg"], 1)

                    def high_part():
                        a.wait_ge(s["hd"], e + 1)
                        a.activation(h_hi[:, j, :], Tg[:, j % 2, :], ACT.Copy).then_inc(s["hhi"], 1)
                    if mixing(b, j)[2] is not None:
                        squares(mixing(b, j)[2])
                    high_part()
                    if b == 0:
                        for i in unpack_with(j):
                            if i + 1 < len(unpack):
                                sign_carry(i + 1)
                    if b > 0 and j < 2:
                        rows(TC * b + j, first=False, second=j == 0)
                    mix(b, j)
                    if j == (4 if b == 0 else JG):
                        q1_rows(b)
                    if b == B - 1 and j == 6:
                        for i in range(B - 1):
                            copy_chosen(i)
                    if b == B - 1 and j == 8:
                        copy_tables(range(4))
                    if b == B - 1 and j == 10:
                        copy_tables(range(4, 6))
                for c in range(TC):
                    rows(TC * b + c, second=c > 0, third=c > 1, mixes=mixing(b, PAIRS + c))
                    mix(b, PAIRS + c)
                    split_base(b + 1, splits(b, PAIRS + c))
            rows(NCH, first=False)
            rows(NCH + 1, first=False, second=False)
            copy_chosen(B - 1)
            copy_tables([2 * (B - 1), 2 * B - 1])
            for i, c in enumerate(by_act):
                a.wait_ge(s["spl"], c // TC + 1)
                if i >= 2:
                    a.wait_ge(s["fin_pool"], by_act[i - 2] + 1)
                for j in range(SLICE):
                    last = a.activation(Tg[:, i % 2, j::SLICE], onehot[:, c, :], ACT.Copy, scale=xs[:, c, j:j + 1])
                last.then_inc(s["pact"], 1)

        @block.tensor
        def _(pe):
            pe.wait_ge(s["sig_rhs"], 1)
            pe.wait_ge(s["ones"], 1)
            nc.tensor.matmul(ps[:, TR0, :], ones[:, :], sgn[0:TILES, :], start=True, stop=True).then_inc(s["sig_bc"], 1)
            pe.wait_ge(s["ident_done"], 3)
            def product(j, part, m):
                cols = slice(2 * P * j + P * part, 2 * P * j + P * (part + 1))
                dst = ps[:, 2 * (j % 2) + part, :]
                nc.tensor.matmul(dst, wg_hi[:, m, cols], base_hi[:, m, :], start=(m == 0), stop=False)
                nc.tensor.matmul(dst, wg_hi[:, m, cols], base_lo[:, m, :], start=False, stop=False)
                return nc.tensor.matmul(dst, wg_lo[:, m, cols], base_hi[:, m, :], start=False, stop=(m == CT - 1))

            def turn_chosen(b):
                pe.wait_ge(s["ohd"], b + 1 + (b == B - 1))
                for c in range(TC):
                    nc.tensor.transpose(chosen_bank(b)[:, c * P:(c + 1) * P], onehot[:, TC * b + c, :], identh[:, :]).then_inc(s["ohtr"], 1)

            def look_up(pairs):
                for i in pairs:
                    pe.wait_ge(s["ohtc"], i // 2 + 1)
                    for c in range(2 * i, 2 * i + 2):
                        for part in range(3):
                            last = nc.tensor.matmul(ps[:, table_bank(i), 2 * KNOTS * (c % 2):2 * KNOTS * (c % 2 + 1)],
                                                    ohT[:, c * P:(c + 1) * P], tab_part[:, part, :], start=(part == 0), stop=(part == 2))
                    last.then_inc(s["tabm"], 1)

            for b in range(B):
                for j in range(PAIRS):
                    e = PAIRS * b + j
                    if b == 0:
                        pe.wait_ge(s["dlo"], j + 1)
                        pe.wait_ge(s["dhi"], j + 1)
                    if j >= 2:
                        pe.wait_ge(s["hd"], e - 1)
                    elif b > 0:
                        pe.wait_ge(s["hd"], PAIRS * b)
                    if j == 0 and b > 0:
                        for m in range(CT):
                            pe.wait_ge(s["blo"], CT * b + m + 1)
                            for jj in range(2):
                                for part in range(2):
                                    last = product(jj, part, m)
                                if m == CT - 1:
                                    last.then_inc(s["gu"], 1)
                    elif j > 1 or b == 0:
                        for part in range(2):
                            for m in range(CT):
                                if b == j == part == 0:
                                    pe.wait_ge(s["blo"], m + 1)
                                last = product(j, part, m)
                        last.then_inc(s["gu"], 1)
                    if j == (4 if b == 0 else 1):
                        pe.wait_ge(s["fq"], 8 * (b + 1))
                        for c in range(TC):
                            if b == 0:
                                pe.wait_ge(s["sig_done"], 1)
                            else:
                                pe.wait_ge(s["x1"], TC * (b - 1) + c + 1)
                            for m in range(CT):
                                last = nc.tensor.transpose(ps[:, Y0 + c, P * m:P * (m + 1)],
                                                           q1[:, m, P * c:P * (c + 1)], ident[:, :])
                            last.then_inc(s["tr"], 1)
                    if b == B - 1 and j == 5:
                        pe.wait_ge(s["q1t"], NCH)
                        for i in range(B - 1):
                            turn_chosen(i)
                    if b == B - 1 and j == 8:
                        pe.wait_ge(s["tabsp"], 3)
                        pe.wait_ge(s["ohtc"], B - 1)
                        look_up(range(4))
                    if b == B - 1 and j == 10:
                        pe.wait_ge(s["tabc"], 4)
                        look_up(range(4, 6))
                if b == 0:
                    pe.wait_ge(s["dlo"], PAIRS + 6)
                    pe.wait_ge(s["dhi"], PAIRS + 6)
                for c in range(TC):
                    t = TC * b + c
                    pe.wait_ge(s["q1t"], t + 1)
                    if b == B - 1:
                        pe.wait_ge(s["tabc"], 8 if c < 2 else 12)
                    dst = ps[:, Y0 + c, :]
                    for j in range(PAIRS):
                        if c == 0:
                            pe.wait_ge(s["hlo"], PAIRS * b + j + 1)
                        rows = slice(P * c, P * (c + 1))
                        nc.tensor.matmul(dst, h_hi[:, j, rows], wd_hi[:, j, :], start=(j == 0), stop=False)
                        nc.tensor.matmul(dst, h_hi[:, j, rows], wd_lo[:, j, :], start=False, stop=False)
                        last = nc.tensor.matmul(dst, h_lo[:, j, rows], wd_hi[:, j, :], start=False, stop=(j == PAIRS - 1))
                    last.then_inc(s["yd"], 1)
            turn_chosen(B - 1)
            look_up([2 * (B - 1), 2 * B - 1])
            pe.wait_ge(s["rund"], 2 * B)
            for i in range(2):
                nc.tensor.transpose(ps[0:TILES, 3, P * i:P * (i + 1)], run[:, i, :], ident[:, :]).then_inc(s["rtr"], 1)
            pe.wait_ge(s["look_split"], 3)
            for c in range(NCH):
                last = nc.tensor.matmul(ps[:, Y0, 9 * c:9 * (c + 1)], ohT[:, c * P:(c + 1) * P],
                                        look_part[:, :, :].rearrange("p a b -> p (a b)"), start=True, stop=True)
            last.then_inc(s["lk"], 1)

        @block.vector
        def _(v):
            count = {}

            def await_step(sem, n):
                count[sem] = count.get(sem, 0) + n
                v.wait_ge(sem, count[sem])

            def link(ins, sem=s["bestd"]):
                ins.then_inc(sem, 1)
                await_step(sem, 1)

            def code_bits(i):
                tiles, nt, n, _, _, _ = unpack[i]
                if i >= PAIRS:
                    v.wait_ge(s["compact"], 2)
                if i >= NBUF:
                    v.wait_ge(s["dlo"], i - NBUF + 1)
                    v.wait_ge(s["dhi"], i - NBUF + 1)
                for m, (src, shift) in enumerate(tiles):
                    left = 9 - shift
                    nc.vector.tensor_scalar(code[i % NBUF][:, m * n:(m + 1) * n], src, abs(left), 0x1E00,
                                            ALU.logical_shift_left if left > 0 else ALU.logical_shift_right,
                                            ALU.bitwise_and).then_inc(s["dmag"], 1)

            def products(i):
                _, nt, n, (sa, _, _), (hi, _), _ = unpack[i]
                v.wait_ge(s["dsgn"], i + 1)
                bits = code[i % NBUF][:, 0:nt * n]
                nc.vector.tensor_scalar(bits, bits, 0x8FFF, None, ALU.bitwise_and).then_inc(s["dval"], 1)
                v.wait_ge(s["dval"], i + 1)
                v.wait_ge(s["sclB"], 1 if i < PAIRS else 2)
                nc.vector.tensor_tensor(hi, value(i), factor(i, sa), ALU.mult).then_inc(s["dhi"], 1)

            def exponentials(n):
                v.wait_ge(s["ld_k%d" % (n % 2)], 16 * (n // 2 + 1))
                if n > 0:
                    v.wait_ge(s["ekvd"], n)
                    v.wait_ge(s["sf"], 2 * last_of[n - 1] + 2)
                nc.vector.tensor_scalar(E[:, :], kbuf[:, n % 2, :], 30.0, None, ALU.min).then_inc(s["km"], 1)

            def scans(k):
                b, m, l = steps[k]
                i = k % 2
                d = decay[:, l, m, b:b + 1]
                v.wait_ge(s["ex"], shares[k] + 1)
                if k >= 2:
                    v.wait_ge(s["fq"], k - 1)
                for src, dst, ready in ((E, 0, None), (ekv, 1, "ekvd")):
                    if ready:
                        v.wait_ge(s[ready], shares[k] + 1)
                    nc.vector.tensor_tensor_scan(F[:, i, dst, :], d.broadcast_to([P, T]), src[:, :], 0.0,
                                                 ALU.mult, ALU.add).then_inc(s["sf"], 1)
                for dst in range(2):
                    v.wait_ge(s["sf"], 2 * k + dst + 1)
                    nc.vector.tensor_scalar(G[:, i, dst, T - 1:T], F[:, i, dst, T - 1:T], kappa[:, l, m, b:b + 1], None,
                                            ALU.mult).then_inc(s["edge"], 1)
                for dst in range(2):
                    v.wait_ge(s["edge"], 2 * k + dst + 1)
                    nc.vector.tensor_tensor_scan(rev(G[:, i, dst, 0:T - 1]), d.broadcast_to([P, T - 1]),
                                                 rev(F[:, i, dst, 0:T - 1]), G[:, i, dst, T - 1:T],
                                                 ALU.mult, ALU.add).then_inc(s["sg"], 1)

            def own_weight(k):
                b, m, l = steps[k]
                i = k % 2
                v.wait_ge(s["euk"], k + 1)
                v.wait_ge(s["sg"], 2 * k + 2)
                nc.vector.scalar_tensor_tensor(F[:, i, 1, :], EU[:, i, :], cap[:, l, m, b:b + 1], vs[:, shares[k] % 2, :],
                                               ALU.min, ALU.mult).then_inc(s["euv"], 1)

            def add_own(k):
                if k is not None:
                    b, m, l = steps[k]
                    i = k % 2
                    nc.vector.scalar_tensor_tensor(G[:, i, 0, :], EU[:, i, :], cap[:, l, m, b:b + 1], G[:, i, 0, :],
                                                   ALU.min, ALU.add).then_inc(s["den"], 1)

            def floor_under(k):
                if k is not None:
                    b, m, l = steps[k]
                    i = k % 2
                    v.wait_ge(s["den"], k + 1)
                    nc.vector.tensor_scalar(G[:, i, 0, :], G[:, i, 0, :], floor[:, l, m, b:b + 1], None, ALU.max).then_inc(s["denm"], 1)

            def first_factor(k):
                if k is not None:
                    i = k % 2
                    v.wait_ge(s["wq"], k + 1)
                    v.wait_ge(s["e2"], 2 * k + 1)
                    nc.vector.scalar_tensor_tensor(G[:, i, 1, :], F[:, i, 1, :], factors[0][2], G[:, i, 1, :],
                                                   ALU.add, ALU.mult).then_inc(s["fa"], 1)

            def second_factor(k):
                if k is not None:
                    b, m, l = steps[k]
                    i = k % 2
                    v.wait_ge(s["fa"], k + 1)
                    v.wait_ge(s["e2"], 2 * k + 2)
                    if l == 1 and b > 0:
                        v.wait_ge(s["tr"], TC * b)
                    nc.vector.scalar_tensor_tensor(q1[:, m, :] if l else G[:, i, 1, :], F[:, i, 0, :], factors[1][2],
                                                   G[:, i, 1, :], ALU.add, ALU.mult).then_inc(s["fq"], 1)

            def gate_input(k):
                if k is not None and steps[k][2] == 0:
                    b, m, _ = steps[k]
                    v.wait_ge(s["fq"], k + 1)
                    v.wait_ge(s["tx"], based_at[(b, m)] + 1)
                    nc.vector.scalar_tensor_tensor(xTb[:, m, :], xTb[:, m, :], 1.0, G[:, k % 2, 1, :], ALU.add, ALU.mult).then_inc(s["based"], 1)

            def weigh_and_divide(w, r):
                first_factor(r)
                add_own(w)
                second_factor(r)
                floor_under(w)
                gate_input(r)

            def slot(k):
                if fresh[k]:
                    exponentials(shares[k])
                if k >= 1:
                    own_weight(k - 1)
                weigh_and_divide(k - 1 if k >= 1 else None, k - 2 if k >= 2 else None)
                scans(k)

            v.wait_ge(s["iota_done"], 1)
            nc.vector.tensor_scalar(shq[:, 1:2], shq[:, 0:1], 6, 4, ALU.logical_shift_right, ALU.logical_shift_left).then_inc(s["shift_set"], 1)
            nc.vector.tensor_scalar(shq[:, 2:3], shq[:, 0:1], 4, 2, ALU.logical_shift_right, ALU.logical_shift_left).then_inc(s["shift_set"], 1)
            v.wait_ge(s["ld_small"], 16 * 5)
            nc.vector.tensor_reduce(tf[:, 0, :], Tg[:, 1, :].rearrange("p (b t) -> p b t", b=B), axis=AX, op=ALU.add).then_inc(s["tf_sum"], 1)
            v.wait_ge(s["tf_tanh"], 1)
            v.wait_ge(s["w_exp"], 2)
            nc.vector.tensor_scalar(tf[:, 2, :], tf[:, 1, :], 0.25, 0.75, ALU.mult, ALU.add).then_inc(s["tf_scale"], 1)
            nc.vector.tensor_scalar(sc[:, :], tf[:, 1, :], 0.05, 0.45, ALU.mult, ALU.add).then_inc(s["sc_done"], 1)
            v.wait_ge(s["tf_scale"], 1)
            flat = [t[:, :, :, :].rearrange("p l m b -> p (l m b)") for t in (decay, kappa, cap, floor)]
            link(nc.vector.tensor_tensor(decay[:, :, :, :].rearrange("p l m b -> p (l m) b"),
                                         wl[:, :, :].rearrange("p l m -> p (l m)").unsqueeze(2).broadcast_to([P, 2 * CT, B]),
                                         tf[:, 2, :].unsqueeze(1).broadcast_to([P, 2 * CT, B]), ALU.mult))
            link(nc.vector.tensor_scalar(flat[0], flat[0], 1.0 - 2.0 ** -24, None, ALU.min))
            link(nc.vector.tensor_scalar(flat[1], flat[0], -1.0, 1.0, ALU.mult, ALU.add))
            link(nc.vector.scalar_tensor_tensor(flat[1], flat[0], 1.0, flat[1], ALU.add, ALU.mult))
            link(nc.vector.reciprocal(flat[1], flat[1]))
            nc.vector.tensor_scalar(flat[2], flat[1], E30, None, ALU.mult).then_inc(s["sc_done"], 1)
            nc.vector.tensor_scalar(flat[3], flat[1], 1e-8, None, ALU.mult).then_inc(s["sc_done"], 1)
            v.wait_ge(s["sc_done"], 3)
            slot(0)
            v.wait_ge(s["shift_set"], 2)
            v.wait_ge(s["ld_pack0"], 16)
            nc.vector.tensor_scalar(gp_i, gp_i, shq[:, 1:2], None, ALU.logical_shift_right).then_inc(s["halves"], 1)
            exponentials(1)
            own_weight(0)
            v.wait_ge(s["compact"], 1)
            code_bits(0)
            weigh_and_divide(0, None)
            scans(1)
            v.wait_ge(s["ld_scale0"], 16)
            v.wait_ge(s["sclA"], 1)
            nc.vector.scalar_tensor_tensor(gu_b, gs_h, 4096.0, gu_a, ALU.mult, ALU.subtract).then_inc(s["sclB"], 1)
            v.wait_ge(s["ld_pack1"], 16)
            nc.vector.tensor_scalar(dp_i[:, 0:FULL * C], dp_i[:, 0:FULL * C], shq[:, 1:2], None, ALU.logical_shift_right).then_inc(s["halves"], 1)
            nc.vector.tensor_scalar(dp_i[:, FULL * C:], dp_i[:, FULL * C:], shq[:, 2:3], None, ALU.logical_shift_right).then_inc(s["halves"], 1)
            for k in range(2, 7):
                if fresh[k]:
                    exponentials(shares[k])
                code_bits(k - 1)
                own_weight(k - 1)
                products(k - 2)
                weigh_and_divide(k - 1, k - 2)
                scans(k)
                if k == 3:
                    v.wait_ge(s["ld_late"], 16 * 3)
                    nc.vector.tensor_reduce(ts[0:TILES, 0, 0:SLICE], Tg[0:TILES, 0, 0:SLICE * GRID].rearrange("p (j g) -> p j g", g=GRID),
                                            axis=AX, op=ALU.add).then_inc(s["slope_sum"], 1)
                if k == 4:
                    v.wait_ge(s["sig_bc"], 1)
                    nc.vector.tensor_copy(sig[:, :], ps[:, TR0, :]).then_inc(s["sig_done"], 1)
                if k == 5:
                    v.wait_ge(s["sclA"], 2)
                    nc.vector.scalar_tensor_tensor(dn_b, ds_h, 16384.0, dn_a, ALU.mult, ALU.subtract).then_inc(s["sclB"], 1)

            def rows(t, first=True, second=True, third=True, mixes=(None, None, None), start=None):
                c, c1, c2 = t % TC, (t - 1) % TC, (t - 2) % TC
                scan, w, r = mixes
                if second:
                    v.wait_ge(s["varr"], t)
                    nc.vector.tensor_scalar(stat[:, VAREPS, c1:c1 + 1], stat[:, VAR, c1:c1 + 1], 1.0 / C, 1e-5,
                                            ALU.mult, ALU.add).then_inc(s["varm"], 1)
                if third:
                    v.wait_ge(s["gamd"], t - 1)
                    nc.vector.tensor_tensor(xf[:, c2, :], xf[:, c2, :], bet[:, :], ALU.add).then_inc(s["xfd"], 1)
                if first:
                    v.wait_ge(s["ssq"], t + 1)
                    nc.vector.tensor_scalar(stat[:, SSQEPS, c:c + 1], stat[:, SSQ, c:c + 1], 1.0 / C, 1e-6 / 64.0,
                                            ALU.mult, ALU.add).then_inc(s["msq"], 1)
                if start:
                    start()
                if scan is not None and fresh[scan] and w is not None:
                    own_weight(w)
                first_factor(r)
                if third:
                    v.wait_ge(s["sgnd"], t - 1)
                    nc.vector.tensor_tensor(sgn[:, :], sgn[:, :], sig[:, :], ALU.mult).then_inc(s["ssd"], 1)
                add_own(w)
                if first:
                    v.wait_ge(s["rs"], t + 1)
                    v.wait_ge(s["ld_z0" if t < TC else "ld_z"], 16 if t < TC else 16 * (B - 1))
                    nc.vector.scalar_tensor_tensor(z[:, t, :], ps[:, Y0 + c, :], stat[:, RS, c:c + 1], z[:, t, :],
                                                   ALU.mult, ALU.add).then_inc(s["x1"], 1)
                if third:
                    v.wait_ge(s["ssd"], t - 1)
                    nc.vector.tensor_reduce(ts[:, c2, :], sgn[:, :].rearrange("p (t j) -> p t j", j=SLICE), axis=AX, op=ALU.add).then_inc(s["tsd"], 1)
                second_factor(r)
                if first:
                    v.wait_ge(s["t1"], t + 1)
                    v.wait_ge(s["q1t"], t + 1)
                    nc.vector.scalar_tensor_tensor(xf[:, c, :], Tg[:, c % 2, :], 1.0, xf[:, c, :], ALU.add, ALU.mult,
                                                   accum_out=stat[:, SUM, c:c + 1]).then_inc(s["mix"], 1)
                floor_under(w)
                gate_input(r)
                if scan is not None:
                    scans(scan)

            def choose(b, lo=0, hi=TC):
                n = hi - lo
                oh = onehot[:, TC * b + lo:TC * b + hi, :]
                tsv = ts[:, lo:hi, :].rearrange("p c (k i) -> p (c k) i", i=8)
                cmv = comp[:, lo:hi, :].rearrange("p c (k i) -> p (c k) i", i=8)
                csv = cs[:, lo:hi, :].rearrange("p c k -> p (c k)")
                v.wait_ge(s["tsd"], TC * b + hi)
                link(nc.vector.tensor_reduce(csv, tsv, axis=AX, op=ALU.add))
                link(nc.vector.scalar_tensor_tensor(cmv, csv.unsqueeze(2).broadcast_to([P, n * CLUSTERS, 8]), 2048.0,
                                                    rank[:, lo:hi, :].rearrange("p c (k i) -> p (c k) i", i=8), ALU.mult, ALU.add))
                link(nc.vector.scalar_tensor_tensor(comp[:, lo:hi, :], ts[:, lo:hi, :], 8.0, comp[:, lo:hi, :], ALU.mult, ALU.add))
                link(nc.vector.tensor_reduce(best[:, lo:hi], comp[:, lo:hi, :], axis=AX, op=ALU.max))
                link(nc.vector.tensor_tensor(oh, comp[:, lo:hi, :], best[:, lo:hi].unsqueeze(2).broadcast_to([P, n, TILES]), ALU.is_equal), s["ohd"])

            def gather(b, lo=TC):
                oh = onehot[:, TC * b:TC * (b + 1), :]
                xb = xs[:, TC * b:TC * (b + 1), :]
                link(nc.vector.tensor_scalar(ts[:, :, :], oh, -BIG, BIG, ALU.mult, ALU.add))
                if lo < TC:
                    sel = xf[:, lo:TC, :].rearrange("p c (t j) -> p (c t) j", j=SLICE)
                    link(nc.vector.tensor_tensor(sel, sel, oh[:, lo:TC, :].rearrange("p c t -> p (c t)").unsqueeze(2)
                                                 .broadcast_to([P, (TC - lo) * TILES, SLICE]), ALU.mult))
                v.wait_ge(s["prodd"], b + 1)
                nc.vector.tensor_reduce(xb, xf[:, :, :].rearrange("p c (t j) -> p c j t", j=SLICE),
                                        axis=AX, op=ALU.add).then_inc(s["xsd"], 1)
                v.wait_ge(s["xsd"], b + 1)
                ops = (ALU.min, ALU.max)
                for i, op in enumerate(ops):
                    nc.vector.tensor_reduce(tmn[:, i, :], xb, axis=AX, op=op).then_inc(s["range_step"], 1)
                await_step(s["range_step"], 2)
                for i, buf in enumerate((comp, cand)):
                    nc.vector.tensor_tensor(buf[:, :, :], oh, tmn[:, i, :].unsqueeze(2).broadcast_to([P, TC, TILES]), ALU.mult).then_inc(s["range_step"], 1)
                await_step(s["range_step"], 2)
                for i, buf in enumerate((comp, cand)):
                    nc.vector.tensor_tensor(buf[:, :, :], buf[:, :, :], ts[:, :, :], (ALU.add, ALU.subtract)[i]).then_inc(s["range_step"], 1)
                await_step(s["range_step"], 2)
                for i, buf in enumerate((comp, cand)):
                    nc.vector.tensor_reduce(mkv[:, i, :], buf[:, :, :].rearrange("p c t -> p t c"), axis=AX, op=ops[i]).then_inc(s["range_step"], 1)
                await_step(s["range_step"], 2)
                for i in range(2):
                    nc.vector.tensor_tensor(run[:, i, :], run[:, i, :], mkv[:, i, :], ops[i]).then_inc(s["rund"], 1)
                v.wait_ge(s["rund"], 2 * (b + 1))

            def mix(b, i):
                scan, weighs, divides = mixing(b, i)
                if weighs is not None and scan is not None and fresh[scan]:
                    own_weight(weighs)
                weigh_and_divide(weighs, divides)
                if scan is not None:
                    scans(scan)

            def mix_first(b, i):
                scan, weighs, _ = mixing(b, i)
                if scan is not None and fresh[scan]:
                    exponentials(shares[scan])
                elif weighs is not None:
                    own_weight(weighs)

            def three_parts(full, rest, parts, sem):
                src = full
                for i in range(3):
                    nc.vector.tensor_copy(parts[:, i, :], src).then_inc(sem, 1)
                    if i < 2:
                        await_step(sem, 1)
                        link(nc.vector.tensor_tensor(rest, src, parts[:, i, :], ALU.subtract))
                        src = rest

            v.wait_ge(s["rank_done"], 2)
            v.wait_ge(s["run_init"], 2)
            for b in range(B):
                for j in range(PAIRS):
                    e = PAIRS * b + j
                    v.wait_ge(s["tg"], e + 1)
                    nc.vector.scalar_tensor_tensor(Tg[:, j % 2, :], Tg[:, j % 2, :], 1.0, ps[:, 2 * (j % 2), :], ALU.add, ALU.mult).then_inc(s["ag"], 1)
                    mix_first(b, j)
                    v.wait_ge(s["ag"], e + 1)
                    nc.vector.tensor_tensor(Tg[:, j % 2, :], Tg[:, j % 2, :], ps[:, 2 * (j % 2) + 1, :], ALU.mult).then_inc(s["hd"], 1)
                    if b > 0 and j < 2:
                        rows(TC * b + j, first=False, second=j == 0, mixes=mixing(b, j))
                    if b > 0 and j == 1:
                        choose(b - 1)
                    if b > 0 and j == JG:
                        gather(b - 1)
                    if b == B - 1 and j == 4:
                        v.wait_ge(s["ld_tab"], 48)
                        three_parts(tab, tab_rest, tab_part, s["tabsp"])
                    if b == 0:
                        for i in unpack_with(j):
                            if i + 1 < len(unpack):
                                code_bits(i + 1)
                            products(i)
                    if b == 0 or j >= 2:
                        mix(b, j)
                for c in range(TC):
                    rows(TC * b + c, second=c > 0, third=c > 1, mixes=mixing(b, PAIRS + c),
                         start=lambda: mix_first(b, PAIRS + c))
            rows(NCH, first=False)
            choose(B - 1, 0, TC - 1)
            rows(NCH + 1, first=False, second=False)
            choose(B - 1, TC - 1, TC)
            gather(B - 1, TC - 1)

            v.wait_ge(s["rtr"], 2)
            nc.vector.tensor_reduce(lookt[:, 0:1], ps[0:TILES, 3, 0:P], axis=AX, op=ALU.min).then_inc(s["rred"], 1)
            nc.vector.tensor_reduce(lookt[:, 1:2], ps[0:TILES, 3, P:2 * P], axis=AX, op=ALU.max).then_inc(s["rred"], 1)
            v.wait_ge(s["rred"], 2)
            three_parts(lookt[:, :], lookr[:, :], look_part, s["look_split"])
            v.wait_ge(s["lk"], 1)
            lkp = ps[:, Y0, 0:9 * NCH].rearrange("p (c q i) -> p c q i", q=3, i=3)
            link(nc.vector.tensor_copy(lk[:, :, :], lkp[:, :, 0, :]))
            link(nc.vector.tensor_tensor(lk[:, :, :], lk[:, :, :], lkp[:, :, 1, :], ALU.add))
            link(nc.vector.tensor_tensor(lk[:, :, :], lk[:, :, :], lkp[:, :, 2, :], ALU.add))
            wide = [P, NCH, SLICE]
            nc.vector.tensor_tensor(xs[:, :, :], xs[:, :, :], lk[:, :, 0].unsqueeze(2).broadcast_to(wide), ALU.subtract).then_inc(s["g1"], 1)
            link(nc.vector.tensor_tensor(rng[:, :], lk[:, :, 1], lk[:, :, 0], ALU.subtract))
            link(nc.vector.tensor_scalar(rng[:, :], rng[:, :], 1e-8, None, ALU.add))
            link(nc.vector.reciprocal(rng[:, :], rng[:, :]))
            v.wait_ge(s["g1"], 1)
            link(nc.vector.tensor_tensor(xs[:, :, :], xs[:, :, :], rng[:, :].unsqueeze(2).broadcast_to(wide), ALU.mult))
            link(nc.vector.tensor_scalar(xs[:, :, :], xs[:, :, :], 0.0, 1.0 - 1e-6, ALU.max, ALU.min))
            link(nc.vector.tensor_scalar(xs[:, :, :], xs[:, :, :], float(GRID), None, ALU.mult))
            link(nc.vector.tensor_scalar(gi[:, :, :], xs[:, :, :], ROUND, -ROUND, ALU.add, ALU.add))
            link(nc.vector.tensor_tensor(gt[:, :, :], gi[:, :, :], xs[:, :, :], ALU.is_gt))
            link(nc.vector.tensor_tensor(gi[:, :, :], gi[:, :, :], gt[:, :, :], ALU.subtract))
            link(nc.vector.tensor_scalar(gi[:, :, :], gi[:, :, :], 0.0, float(GRID - 1), ALU.max, ALU.min))
            nc.vector.tensor_copy(knot[:, :], gi[:, :, :].rearrange("p c j -> p (c j)")).then_inc(s["g2"], 1)
            link(nc.vector.tensor_tensor(xs[:, :, :], xs[:, :, :], gi[:, :, :], ALU.subtract))
            v.wait_ge(s["g2"], 1)
            v.wait_ge(s["tabc"], 2 * NCH // 2)
            for q in range(B):
                n = slice(TC * SLICE * q, TC * SLICE * (q + 1))
                cols = slice(TC * KNOTS * q, TC * KNOTS * (q + 1))
                g3 = [P, TC * SLICE, GRID]
                link(nc.vector.tensor_tensor(knot_hot[:, cols].rearrange("p (n g) -> p n g", g=GRID),
                                             knot[:, n].unsqueeze(2).broadcast_to(g3),
                                             iota16[:, :].unsqueeze(1).broadcast_to(g3), ALU.is_equal))
                for i, tbl in enumerate((looked_s, looked)):
                    nc.vector.tensor_tensor(tbl[:, cols], tbl[:, cols], knot_hot[:, cols], ALU.mult).then_inc(s["g3"], 1)
                await_step(s["g3"], 2)
                for i, tbl in enumerate((looked_s, looked)):
                    nc.vector.tensor_reduce(bs[:, i, n], tbl[:, cols].rearrange("p (n g) -> p n g", g=GRID), axis=AX, op=ALU.add).then_inc(s["g4"], 1)
                await_step(s["g4"], 2)
                xsf = xs[:, TC * q:TC * (q + 1), :]
                link(nc.vector.tensor_tensor(xsf, xsf, bs[:, 0, n].rearrange("p (c j) -> p c j", j=SLICE), ALU.mult))
                link(nc.vector.tensor_tensor(xsf, xsf, bs[:, 1, n].rearrange("p (c j) -> p c j", j=SLICE), ALU.add))
                nc.vector.tensor_tensor(xsf, xsf, lk[:, TC * q:TC * (q + 1), 2].unsqueeze(2).broadcast_to([P, TC, SLICE]), ALU.mult).then_inc(s["spl"], 1)
            v.wait_ge(s["spl"], B)
            for c in by_dve:
                for j in range(SLICE):
                    last = nc.vector.scalar_tensor_tensor(z[:, c, j::SLICE], onehot[:, c, :], xs[:, c, j:j + 1],
                                                          z[:, c, j::SLICE], ALU.mult, ALU.add)
                last.then_inc(s["fin_dve"], 1)


def kernel(x, fside_BxSxS_0, cond_512, L0_cond_w, L0_cond_u, L0_ffn_gate_up_packed, L0_ffn_gate_up_scales,
           L0_ffn_down_packed, L0_ffn_down_scales, L1_cond_w, L1_cond_u, L1_ffn_ln_gamma, L1_ffn_ln_beta,
           L1_ffn_spline_bases, L1_ffn_spline_slopes, L1_ffn_output_scale):
    import concourse.bacc as bacc
    from concourse.bass_utils import run_bass_kernel_spmd

    p = np.arange(P)
    q, r = p // 64, p % 64
    chan = np.stack([8 * r + 4 * q + m for m in range(CT)], 1)
    inner = [512 * (j // 4) + 8 * r + 4 * q + j % 4 for j in range(4 * FULL)]
    inner += [8 * (64 * FULL + 16 * t + p % 16) + p // 16 for t in range(REST)]
    order = np.concatenate([np.concatenate([i, i + INNER]) for i in inner])

    x = np.asarray(x)
    side = np.asarray(fside_BxSxS_0)
    gp = np.asarray(L0_ffn_gate_up_packed)
    gs = np.asarray(L0_ffn_gate_up_scales)
    dp = np.asarray(L0_ffn_down_packed)
    ds = np.asarray(L0_ffn_down_scales)
    xc = x.transpose(2, 0, 1)
    kc = side.transpose(2, 0, 1)
    arrays = {
        "xT": np.stack([xc[chan[:, m]] for m in range(CT)]),
        "kT": np.stack([kc[chan[:, m]] for m in range(CT)]),
        "x": x,
        "cond": np.asarray(cond_512),
        "w0": np.asarray(L0_cond_w)[chan], "w1": np.asarray(L1_cond_w)[chan],
        "u0": np.asarray(L0_cond_u)[chan], "u1": np.asarray(L1_cond_u)[chan],
        "gu_pack": gp[order].T[r],
        "gu_scale": gs[:, order][r // 16],
        "dn_pack": np.concatenate([dp.T[64 * b + r] for b in range(FULL)]
                                  + [dp.T[64 * FULL + 16 * t + p % 16] for t in range(REST)], 1),
        "dn_scale": np.concatenate([ds[4 * b + r // 16] for b in range(FULL)]
                                   + [ds[4 * FULL + t + 0 * p] for t in range(REST)], 1),
        "gamma": np.asarray(L1_ffn_ln_gamma), "beta": np.asarray(L1_ffn_ln_beta),
        "bases": np.asarray(L1_ffn_spline_bases), "slopes": np.asarray(L1_ffn_spline_slopes),
        "oscale": np.asarray(L1_ffn_output_scale),
    }
    nc = bacc.Bacc("TRN2", target_bir_lowering=False, num_devices=1)
    feed, args = {}, []
    for name, a in arrays.items():
        a = np.ascontiguousarray(a)
        feed[f"in_{name}"] = a
        args.append(nc.dram_tensor(f"in_{name}", a.shape, mybir.dt.from_np(a.dtype), kind="ExternalInput").ap())
    args.append(nc.dram_tensor("out_0", (B, T, C), mybir.dt.float32, kind="ExternalOutput").ap())
    build_program(nc, *args)
    res = run_bass_kernel_spmd(nc, [feed], core_ids=[0])
    return res.results[0]["out_0"]
```

```python
from contextlib import ExitStack

import concourse.bass as bass
import numpy as np
from concourse import mybir

B, T, C = 4, 512, 512
P = 128
CT = C // P
TC = T // P
NCH = B * TC
INNER = 1408
PAIRS = INNER // P
TD = 128
TILES, SLICE, GRID = 64, 8, 16
CLUSTERS = TILES // 8
FULL = 2
REST = PAIRS - 4 * FULL
BIG = float(2.0 ** 126)
SEED = float(0x7EF311C3)
E30 = float(np.exp(np.float64(30.0)))
SELECT_AT = 2
UNPACK = (2, 2, 1, 1, 1, 1, 1, 1, 1, 1, 0)
GATHER_AT = 3
N_POOL = 11
PLACES0 = (0, 2, 3, 4, 6, 8, 9, 10, 11, 12, 14)
PLACES = (-1, 2, 4, 5, 7, 8, 10, 11, 12, 13)
ROUND = float(2 ** 23)
SEED_E = 0.0506


def reciprocal_factors():
    cheb = np.polynomial.chebyshev.Chebyshev([0, 0, 0, 0, 0, 1]).convert(kind=np.polynomial.Polynomial)
    top = float(cheb(1 / SEED_E))
    num = np.array([1.0 if i == 0 else 0.0 for i in range(6)]) - cheb.coef / top / SEED_E ** np.arange(6)
    quot, _ = np.polynomial.polynomial.polydiv(num, np.array([1.0, -1.0]))
    roots = np.polynomial.polynomial.polyroots(quot)
    roots = [r for r in roots if r.imag > 0]
    lead = np.sqrt(quot[4])
    return [(float(np.sqrt(lead)), float(-np.sqrt(lead) * r.real), float(lead * r.imag ** 2)) for r in roots]


def build_program(nc, xT, kT, x, cond, w0, w1, u0, u1, gu_pack, gu_scale, dn_pack, dn_scale,
                  gamma, beta, bases, slopes, oscale, out):
    f32, f16, bf16 = mybir.dt.float32, mybir.dt.float16, mybir.dt.bfloat16
    i32, u16 = mybir.dt.int32, mybir.dt.uint16
    ALU, ACT, AX = mybir.AluOpType, mybir.ActivationFunctionType, mybir.AxisListType.X

    steps = [(0, m, 0) for m in range(CT)] + [(0, m, 1) for m in range(CT)]
    steps += [(b, m, l) for b in range(1, B) for m in range(CT) for l in range(2)]
    shares = []
    for k, (b, m, l) in enumerate(steps):
        shares.append((shares[-1] if k and steps[k - 1][:2] == (b, m) else shares[-1] + 1) if k else 0)
    fresh = [k == 0 or shares[k] != shares[k - 1] for k in range(len(steps))]
    last_of = {n: k for k, n in enumerate(shares)}
    first_of = {n: k for k, n in reversed(list(enumerate(shares)))}
    based_at = {(b, m): i for i, (b, m) in enumerate((b, m) for b, m, l in steps if l == 0)}
    factors = reciprocal_factors()

    ctx = ExitStack()
    with ctx:
        def sb(name, shape, dt):
            return ctx.enter_context(nc.sbuf_tensor(name, shape, dt))

        def sem(name):
            return ctx.enter_context(nc.semaphore(name))

        wg_hi = sb("wg_hi", [P, CT, 2 * INNER], f16)
        wg_lo = sb("wg_lo", [P, CT, 2 * INNER], bf16)
        wd_hi = sb("wd_hi", [P, PAIRS, C], f16)
        wd_lo = sb("wd_lo", [P, PAIRS, C], bf16)
        z = sb("z", [P, NCH, C], f32)
        q1 = sb("q1", [P, CT, T], f32)
        base_hi = sb("base_hi", [P, CT, T], f16)
        base_lo = sb("base_lo", [P, CT, T], f16)
        h_hi = sb("h_hi", [P, PAIRS, T], f16)
        h_lo = sb("h_lo", [P, PAIRS, T], f16)
        kbuf = sb("kbuf", [P, 2, T], f32)
        xTb = sb("xTb", [P, CT, T], f32)
        xf = sb("xf", [P, TC, C], f32)
        E = sb("E", [P, T], f32)
        vs = sb("vs", [P, 2, T], f32)
        ekv = sb("ekv", [P, T], f32)
        EU = sb("EU", [P, 2, T], f32)
        F = sb("F", [P, 2, 2, T], f32)
        G = sb("G", [P, 2, 2, T], f32)
        Tg = sb("Tg", [P, 2, T], f32)
        gam = sb("gam", [P, C], f32)
        bet = sb("bet", [P, C], f32)
        sig = sb("sig", [P, C], bf16)
        sgn = sb("sgn", [P, C], bf16)
        onehot = sb("onehot", [P, NCH, TILES], bf16)
        ts = sb("ts", [P, TC, TILES], f32)
        comp = sb("comp", [P, TC, TILES], f32)
        cand = sb("cand", [P, TC, TILES], f32)
        cs = sb("cs", [P, TC, CLUSTERS], f32)
        rank = sb("rank", [P, TC, TILES], f32)
        best = sb("best", [P, TC], f32)
        xs = sb("xs", [P, NCH, SLICE], f32)
        tmn = sb("tmn", [P, 2, TC], f32)
        mkv = sb("mkv", [P, 2, TILES], f32)
        run = sb("run", [P, 2, TILES], f32)
        ident = sb("ident", [P, P], f32)
        identh = sb("identh", [P, P], bf16)
        decay = sb("decay", [P, 2, CT, B], f32)
        kappa = sb("kappa", [P, 2, CT, B], f32)
        cap = sb("cap", [P, 2, CT, B], f32)
        floor = sb("floor", [P, 2, CT, B], f32)
        wl = sb("wl", [P, 2, CT], f32)
        ul = sb("ul", [P, 2, CT], f32)
        tf = sb("tf", [P, 3, B], f32)
        sc = sb("sc", [P, B], f32)
        half = sb("half", [P, 1], f32)
        stat = sb("stat", [P, 9, TC], f32)
        shq = sb("shq", [P, 3], i32)
        junk = sb("junk", [P, 2, C], bf16)
        ones = sb("ones", [TILES, P], bf16)
        iota16 = sb("iota16", [P, GRID], bf16)
        lk = sb("lk", [P, NCH, 3], f32)
        knot = sb("knot", [P, NCH * SLICE], bf16)
        rng = sb("rng", [P, NCH], f32)
        lookt = sb("lookt", [TILES, 3], f32)
        lookr = sb("lookr", [TILES, 3], f32)
        look_part = sb("look_part", [TILES, 3, 3], bf16)

        z_w = z[:, TC:NCH, :].rearrange("p a b -> p (a b)")
        z_i, z_u = z_w.bitcast(i32), z_w.bitcast(u16)
        DN = (FULL + REST) * C
        gp_i = z_i[:, 0:2 * INNER]
        dp_i = z_i[:, 2 * INNER:2 * INNER + DN]
        PIECE, GP, NBUF = 1024, 4 * INNER, 3
        code = [z_u[:, o:o + PIECE] for o in (0, PIECE, 2 * PIECE + DN)]
        dn_u = z_u[:, 2 * PIECE:2 * PIECE + DN]
        dn_a = z_u[:, GP:GP + DN].bitcast(bf16)
        dn_b = z_u[:, GP + DN:GP + 2 * DN].bitcast(bf16)
        hh = h_hi[:, :, :].rearrange("p a b -> p (a b)")
        hl = h_lo[:, :, :].rearrange("p a b -> p (a b)")
        gu_u = hl[:, DN:DN + 2 * INNER].bitcast(u16)
        gu_a = hh[:, DN:DN + 2 * INNER].bitcast(bf16)
        gs_h = xf[:, :, :].rearrange("p a b -> p (a b)").bitcast(f16)[:, 0:2 * INNER]
        gu_b = gs_h.bitcast(bf16)
        ds_h = hh[:, 0:DN]
        KNOTS = SLICE * GRID
        Gf = G[:, :, :, :].rearrange("p a b c -> p (a b c)").bitcast(bf16)
        ohT = Gf[0:TILES, 0:NCH * P]
        tab = vs[:, :, :].rearrange("p a b -> p (a b)")[0:TILES, 0:2 * KNOTS]
        tab_rest = EU[:, :, :].rearrange("p a b -> p (a b)")[0:TILES, 0:2 * KNOTS]
        tab_part = ekv[:, :].bitcast(bf16)[0:TILES, 0:6 * KNOTS].rearrange("p (a b) -> p a b", a=3)
        looked = xTb[:, :, :].rearrange("p a b -> p (a b)")
        looked_s = F[:, :, :, :].rearrange("p a b c -> p (a b c)")
        gi = E[:, 0:NCH * SLICE].rearrange("p (c j) -> p c j", j=SLICE)
        gt = E[:, NCH * SLICE:2 * NCH * SLICE].rearrange("p (c j) -> p c j", j=SLICE)
        bs = E[:, 2 * NCH * SLICE:4 * NCH * SLICE].rearrange("p (i n) -> p i n", i=2)
        knot_hot = kbuf[:, :, :].rearrange("p a b -> p (a b)").bitcast(bf16)[:, 0:NCH * KNOTS]

        ps = ctx.enter_context(nc.psum_tensor("ps", [P, 8, 512], f32))
        Y0, TR0 = 4, 6

        names = ("side_loaded_0 side_loaded_1 first_rows_loaded channels_loaded rows_loaded "
                 "gate_up_codes_loaded down_codes_loaded gate_up_scales_loaded down_scales_loaded "
                 "decay_inputs_loaded late_inputs_loaded spline_tables_loaded out_stored numbers_made "
                 "half_set scales_high scales_low weights_high weights_low cond_summed cond_tanh_ready "
                 "decay_scale_ready rate_exp_ready mixing_scales_ready shifts_set words_shifted "
                 "words_packed code_placed sign_carried value_masked slopes_summed slope_signs_ready "
                 "slope_diagonal_ready slope_signs_spread slope_signs_copied ranks_ready ranges_started "
                 "identity_ready side_capped exp_ready value_scaled exp_value_ready own_exp_ready "
                 "own_exp_scaled edge_set forward_scanned backward_scanned own_value_ready "
                 "denominator_summed denominator_floored numerator_summed seed_ready denominator_seeded "
                 "numerator_seeded factor_squared first_factor_applied quotient_ready gate_tanh_ready "
                 "input_ready input_high input_low gate_up_ready silu_tanh_ready silu_ready hidden_ready "
                 "hidden_high hidden_low quotient_turned quotient_rows y_ready y_squares_summed "
                 "y_mean_square y_root x1_ready x1_tanh_ready mixed_ready residual_added mean_ready "
                 "deviations_summed variance_ready variance_root shift_ready normalised gamma_applied "
                 "beta_applied signs_ready signs_matched tile_scores_ready chain_step range_step "
                 "tile_chosen slice_selected slice_ready ranges_updated chosen_turned chosen_copied "
                 "tables_looked_up tables_copied ranges_turned ranges_reduced range_looked_up offset_ready "
                 "knot_ready knot_picked knot_summed ranges_in_parts tables_in_parts spline_ready "
                 "act_product_ready pool_product_ready dve_product_ready pool_finished dve_finished "
                 "ones_set").split()
        s = {n: sem(n) for n in names}

        SSQ, RS, SUM, NMEAN, VAR, RSTD, VAREPS, SSQEPS, NBIAS = range(9)

        def rev(ap):
            return ap[:, ::-1]

        unpack = []
        for j in range(PAIRS):
            cols = slice(2 * P * j, 2 * P * (j + 1))
            unpack.append(([(gu_u[:, cols], 4 * m) for m in range(CT)], CT, 2 * P, (gu_a, gu_b, cols),
                           (wg_hi[:, :, cols], wg_lo[:, :, cols])))
        for i in range(FULL):
            for m in (0, 2):
                cols, tiles = slice(C * i, C * (i + 1)), slice(CT * i + m, CT * i + m + 2)
                unpack.append(([(dn_u[:, cols], 4 * m), (dn_u[:, cols], 4 * m + 4)], 2, C, (dn_a, dn_b, cols),
                               (wd_hi[:, tiles, :], wd_lo[:, tiles, :])))
        for t, n in ((0, 2), (2, 1)):
            cols = slice(C * (FULL + t), C * (FULL + t + n))
            tiles = slice(CT * FULL + t, CT * FULL + t + n)
            unpack.append(([(dn_u[:, C * (FULL + t + i):C * (FULL + t + i + 1)], 0) for i in range(n)], n, C,
                           (dn_a, dn_b, cols), (wd_hi[:, tiles, :], wd_lo[:, tiles, :])))
        done = 0
        for i, u in enumerate(unpack):
            done += u[1]
            unpack[i] = (*u, done)

        def value(i):
            return code[i % NBUF][:, 0:unpack[i][1] * unpack[i][2]].bitcast(f16).rearrange("p (m n) -> p m n", m=unpack[i][1])

        def factor(i, scales):
            _, nt, n, (_, _, cols), _, _ = unpack[i]
            if i >= PAIRS + 4:
                return scales[:, cols].rearrange("p (m n) -> p m n", m=nt)
            return scales[:, cols].unsqueeze(1).broadcast_to([P, nt, n])

        def unpack_with(j):
            return list(range(5, PAIRS + 6))[sum(UNPACK[:j]):sum(UNPACK[:j + 1])]

        places = [PLACES0] + [PLACES] * (B - 2) + [()]

        def mixing(b, i):
            if i not in places[b]:
                return None, None, None
            start = 7 if b == 0 else 8 * (b + 1)
            end = 8 * (b + 2)
            k = start + places[b].index(i)
            return (k if k < end else None, k - 1 if (b == 0 or k > start) and k <= end else None,
                    k - 2 if b == 0 or k > start + 1 else None)

        def splits(b, i):
            if i < PAIRS or b == B - 1:
                return []
            ready = {m: max(PAIRS, places[b][steps.index((b + 1, m, 0)) - (7 if b == 0 else 8 * (b + 1)) + 2])
                     for m in range(CT)}
            return [m for m in range(CT) if ready[m] == i]

        by_pool = list(range(N_POOL))
        by_dve = list(range(N_POOL, NCH))
        by_act = [c for c in by_pool if c % 4 > 0]

        def chosen_bank(b):
            half_bank = ps[0:TILES, (4, 4, 5, 0)[b], :].bitcast(bf16)
            return half_bank[:, (b == 1) * TC * P:((b == 1) + 1) * TC * P]

        def table_bank(i):
            return (6, 7, 4, 5, 6, 7, 1, 2)[i]

        block = ctx.enter_context(nc.Block())

        @block.sync
        def _(sp):
            def load_k(n):
                b, m, _ = steps[first_of[n]]
                if n >= 2:
                    sp.wait_ge(s["own_exp_ready"], last_of[n - 2] + 1)
                    sp.wait_ge(s["value_scaled"], n - 1)
                    sp.wait_ge(s["side_capped"], n - 1)
                sp.dma_start(kbuf[:, n % 2, :], kT[m, :, b, :]).then_inc(s["side_loaded_%d" % (n % 2)], 16)

            def load_x(b):
                if b > 0:
                    sp.wait_ge(s["input_low"], 4 * b)
                sp.dma_start(xTb[:, :, :], xT[:, :, b, :].rearrange("m p t -> p m t")).then_inc(s["channels_loaded"], 16)

            load_k(0)
            for l, (wv, uv) in enumerate(((w0, u0), (w1, u1))):
                sp.dma_start(wl[:, l, :], wv).then_inc(s["decay_inputs_loaded"], 16)
                sp.dma_start(ul[:, l, :], uv).then_inc(s["decay_inputs_loaded"], 16)
            sp.dma_start(Tg[:, 1, :], cond.rearrange("(o b) t -> o (b t)", o=1).broadcast_to([P, B * TD])).then_inc(s["decay_inputs_loaded"], 16)
            sp.dma_start(gp_i, gu_pack).then_inc(s["gate_up_codes_loaded"], 16)
            sp.dma_start(gs_h, gu_scale).then_inc(s["gate_up_scales_loaded"], 16)
            load_k(1)
            load_x(0)
            sp.dma_start(dp_i, dn_pack).then_inc(s["down_codes_loaded"], 16)
            sp.dma_start(ds_h, dn_scale).then_inc(s["down_scales_loaded"], 16)
            sp.dma_start(Tg[0:TILES, 0, 0:SLICE * GRID], slopes.rearrange("t j g -> t (j g)")).then_inc(s["late_inputs_loaded"], 16)
            sp.dma_start(gam[:, :], gamma.rearrange("(o n) -> o n", o=1).broadcast_to([P, C])).then_inc(s["late_inputs_loaded"], 16)
            sp.dma_start(bet[:, :], beta.rearrange("(o n) -> o n", o=1).broadcast_to([P, C])).then_inc(s["late_inputs_loaded"], 16)
            sp.dma_start(z[:, 0:TC, :], x[0].rearrange("(c p) n -> p c n", p=P)).then_inc(s["first_rows_loaded"], 16)
            for n in range(2, 10):
                load_k(n)
            load_x(1)
            for n in range(10, 12):
                load_k(n)
            sp.wait_ge(s["weights_low"], PAIRS + 6)
            sp.wait_ge(s["weights_high"], PAIRS + 6)
            for b in range(1, B):
                sp.dma_start(z[:, TC * b:TC * (b + 1), :],
                             x[b].rearrange("(c p) n -> p c n", p=P)).then_inc(s["rows_loaded"], 16)
            for n in range(12, 14):
                load_k(n)
            load_x(2)
            for n in range(14, 18):
                load_k(n)
            load_x(3)
            for n in range(18, 20):
                load_k(n)
            sp.wait_ge(s["quotient_ready"], len(steps))
            sp.dma_start(tab[:, 0:KNOTS], bases.rearrange("t j g -> t (j g)")).then_inc(s["spline_tables_loaded"], 16)
            sp.dma_start(tab[:, KNOTS:], slopes.rearrange("t j g -> t (j g)")).then_inc(s["spline_tables_loaded"], 16)
            sp.dma_start(lookt[:, 2:3], oscale.rearrange("(t a) -> t a", a=1)).then_inc(s["spline_tables_loaded"], 16)
            order = sorted([(i / len(by_pool), "pool_finished", i + 1, c) for i, c in enumerate(by_pool)]
                           + [((i + len(by_dve)) / 2 / len(by_dve), "dve_finished", i + 1, c) for i, c in enumerate(by_dve)])
            for _, name, n, c in order:
                sp.wait_ge(s[name], n)
                sp.dma_start(out[c // TC, (c % TC) * P:(c % TC + 1) * P, :], z[:, c, :]).then_inc(s["out_stored"], 16)
            sp.wait_ge(s["out_stored"], 16 * NCH)

        @block.gpsimd
        def _(g):
            g.memset(ident[:, :], 0.0).then_inc(s["identity_ready"], 1)
            g.wait_ge(s["identity_ready"], 1)
            g.affine_select(out=ident[:, :], in_=ident[:, :], compare_op=ALU.not_equal, fill=1.0, base=0,
                            pattern=[[-1, P]], channel_multiplier=1).then_inc(s["identity_ready"], 1)
            g.wait_ge(s["identity_ready"], 2)
            g.tensor_copy(identh[:, :], ident[:, :]).then_inc(s["identity_ready"], 1)
            g.iota(shq[:, 0:1], pattern=[[0, 1]], base=0, channel_multiplier=1).then_inc(s["numbers_made"], 1)
            g.iota(comp[:, :, :].bitcast(i32), pattern=[[0, TC], [-256, CLUSTERS], [-1, 8]], base=0, channel_multiplier=0).then_inc(s["numbers_made"], 1)
            g.wait_ge(s["numbers_made"], 2)
            g.tensor_copy(rank[:, :, :], comp[:, :, :].bitcast(i32)).then_inc(s["ranks_ready"], 1)
            g.iota(cs[:, 0:2, :].bitcast(i32), pattern=[[1, GRID]], base=0, channel_multiplier=0).then_inc(s["numbers_made"], 1)
            g.wait_ge(s["numbers_made"], 3)
            g.tensor_copy(iota16[:, :], cs[:, 0:2, :].rearrange("p a b -> p (a b)").bitcast(i32)).then_inc(s["ranks_ready"], 1)
            g.memset(ones[:, :], 1.0).then_inc(s["ones_set"], 1)
            g.memset(half[:, :], -0.5).then_inc(s["half_set"], 1)
            g.memset(run[:, 0, :], BIG).then_inc(s["ranges_started"], 1)
            g.memset(run[:, 1, :], -BIG).then_inc(s["ranges_started"], 1)
            def exponentials(n):
                g.wait_ge(s["exp_ready"], n + 1)
                g.wait_ge(s["value_scaled"], n + 1)
                if n > 0:
                    g.wait_ge(s["forward_scanned"], 2 * last_of[n - 1] + 2)
                g.tensor_tensor(ekv[:, :], E[:, :], vs[:, n % 2, :], ALU.mult).then_inc(s["exp_value_ready"], 1)

            def seeded(k):
                i = k % 2
                g.wait_ge(s["own_value_ready"], k + 1)
                g.wait_ge(s["backward_scanned"], 2 * k + 2)
                g.tensor_tensor(G[:, i, 1, :], G[:, i, 1, :], F[:, i, 1, :], ALU.add).then_inc(s["numerator_summed"], 1)
                g.wait_ge(s["seed_ready"], k + 1)
                g.tensor_tensor(EU[:, i, :], G[:, i, 0, :], F[:, i, 0, :], ALU.mult).then_inc(s["denominator_seeded"], 1)
                g.wait_ge(s["numerator_summed"], k + 1)
                g.tensor_tensor(G[:, i, 1, :], G[:, i, 1, :], F[:, i, 0, :], ALU.mult).then_inc(s["numerator_seeded"], 1)

            def slot(k):
                if k < len(steps) and fresh[k]:
                    exponentials(shares[k])
                seeded(k - 1)

            def split_base(b, ms=range(CT)):
                for m in ms:
                    g.wait_ge(s["input_high"], 4 * b + m + 1)
                    g.tensor_tensor(base_lo[:, m, :], xTb[:, m, :], base_hi[:, m, :], ALU.subtract).then_inc(s["input_low"], 1)

            def slope_signs():
                g.wait_ge(s["slope_signs_ready"], 1)
                g.affine_select(out=sgn[0:TILES, :].rearrange("p (t j) -> p t j", j=SLICE),
                                in_=ts[0:TILES, 1, 0:SLICE].unsqueeze(1).broadcast_to([TILES, TILES, SLICE]),
                                compare_op=ALU.is_equal, fill=0.0, base=0,
                                pattern=[[-1, TILES], [0, SLICE]], channel_multiplier=1).then_inc(s["slope_diagonal_ready"], 1)

            def low_product(i):
                _, nt, n, (_, sb_, cols), (_, lo), _ = unpack[i]
                g.wait_ge(s["value_masked"], i + 1)
                g.wait_ge(s["scales_low"], 1 if i < PAIRS else 2)
                g.tensor_tensor(lo, value(i), factor(i, sb_), ALU.mult).then_inc(s["weights_low"], 1)

            exponentials(0)
            for k in range(1, 7):
                slot(k)
                if k >= 2:
                    low_product(k - 2)
                if k == 3:
                    slope_signs()
                if k == 5:
                    split_base(0)

            def rows(t, first=True, second=True, scan=None, weigh=None):
                c, c1 = t % TC, (t - 1) % TC
                if second:
                    g.wait_ge(s["variance_ready"], t)
                    g.tensor_tensor(stat[:, RSTD, c1:c1 + 1], stat[:, VAREPS, c1:c1 + 1], half[:, :], ALU.pow).then_inc(s["variance_root"], 1)
                if first:
                    g.wait_ge(s["y_mean_square"], t + 1)
                    g.tensor_tensor(stat[:, RS, c:c + 1], stat[:, SSQEPS, c:c + 1], half[:, :], ALU.pow).then_inc(s["y_root"], 1)
                if scan is not None and fresh[scan]:
                    exponentials(shares[scan])
                if second:
                    g.wait_ge(s["normalised"], t)
                    g.tensor_tensor(xf[:, c1, :], xf[:, c1, :], gam[:, :], ALU.mult).then_inc(s["gamma_applied"], 1)
                if weigh is not None:
                    seeded(weigh)
                if first:
                    g.wait_ge(s["mixed_ready"], t + 1)
                    g.tensor_tensor(z[:, t, :], z[:, t, :], xf[:, c, :], ALU.add).then_inc(s["residual_added"], 1)

            def select_slice(b, n=TC):
                g.wait_ge(s["tile_chosen"], b + 1)
                g.wait_ge(s["beta_applied"], TC * b + n)
                g.tensor_tensor(xf[:, 0:n, :].rearrange("p c (t j) -> p (c t) j", j=SLICE),
                                xf[:, 0:n, :].rearrange("p c (t j) -> p (c t) j", j=SLICE),
                                onehot[:, TC * b:TC * b + n, :].rearrange("p c t -> p (c t)").unsqueeze(2)
                                .broadcast_to([P, n * TILES, SLICE]), ALU.mult).then_inc(s["slice_selected"], 1)

            def mix(b, i):
                scan, weigh, _ = mixing(b, i)
                if scan is not None and fresh[scan] and i < PAIRS:
                    exponentials(shares[scan])
                if weigh is not None:
                    seeded(weigh)

            def iteration(b):
                mix(b, -1)
                for j in range(PAIRS):
                    e = PAIRS * b + j
                    if b > 0 and j == SELECT_AT:
                        select_slice(b - 1)
                    g.wait_ge(s["hidden_high"], e + 1)
                    g.tensor_tensor(h_lo[:, j, :], Tg[:, j % 2, :], h_hi[:, j, :], ALU.subtract).then_inc(s["hidden_low"], 1)
                    if b > 0 and j == 0:
                        rows(TC * b, first=False)
                    if b == 0:
                        for i in unpack_with(j):
                            low_product(i)
                    mix(b, j)
                for c in range(TC):
                    rows(TC * b + c, second=c > 0, scan=mixing(b, PAIRS + c)[0], weigh=mixing(b, PAIRS + c)[1])

            g.wait_ge(s["late_inputs_loaded"], 16 * 3)
            for b in range(B):
                iteration(b)
            rows(NCH, first=False)
            select_slice(B - 1, TC - 1)
            for n, c in enumerate(by_pool):
                g.wait_ge(s["spline_ready"], c // TC + 1)
                if c in by_act:
                    i = by_act.index(c)
                    g.wait_ge(s["act_product_ready"], i + 1)
                    add = Tg[:, i % 2, :]
                else:
                    add = xf[:, c % TC, :]
                    g.tensor_tensor(add.rearrange("p (t j) -> p t j", j=SLICE),
                                    onehot[:, c, :].unsqueeze(2).broadcast_to([P, TILES, SLICE]),
                                    xs[:, c, :].unsqueeze(1).broadcast_to([P, TILES, SLICE]), ALU.mult).then_inc(s["pool_product_ready"], 1)
                    g.wait_ge(s["pool_product_ready"], n - sum(a < c for a in by_act) + 1)
                g.tensor_tensor(z[:, c, :], z[:, c, :], add, ALU.add).then_inc(s["pool_finished"], 1)

        @block.scalar
        def _(a):
            a.wait_ge(s["decay_inputs_loaded"], 16 * 5)
            a.activation(wl[:, :, :], wl[:, :, :], ACT.Exp).then_inc(s["rate_exp_ready"], 1)
            a.wait_ge(s["rate_exp_ready"], 1)
            a.activation(wl[:, :, :], wl[:, :, :], ACT.Exp, scale=-1.0).then_inc(s["rate_exp_ready"], 1)
            a.wait_ge(s["cond_summed"], 1)
            a.activation(tf[:, 1, :], tf[:, 0, :], ACT.Tanh, scale=0.5).then_inc(s["cond_tanh_ready"], 1)
            def compact(n, dst, src, waits):
                a.wait_ge(s["words_shifted"], waits)
                if n == 1:
                    a.wait_ge(s["words_packed"], 1)
                a.activation(dst, src.bitcast(u16)[:, ::2], ACT.Copy).then_inc(s["words_packed"], 1)

            def sign_carry(i):
                n = unpack[i][1] * unpack[i][2]
                a.wait_ge(s["code_placed"], unpack[i][5])
                a.activation(code[i % NBUF][:, 0:n], code[i % NBUF][:, 0:n], ACT.Copy, bias=float(0x7000)).then_inc(s["sign_carried"], 1)

            def exponentials(n):
                b, m, _ = steps[first_of[n]]
                a.wait_ge(s["side_capped"], n + 1)
                a.activation(E[:, :], E[:, :], ACT.Exp).then_inc(s["exp_ready"], 1)
                if n >= 2:
                    a.wait_ge(s["own_value_ready"], last_of[n - 2] + 1)
                    a.wait_ge(s["exp_value_ready"], n - 1)
                a.activation(vs[:, n % 2, :], kbuf[:, n % 2, :], ACT.Copy, scale=sc[:, b:b + 1]).then_inc(s["value_scaled"], 1)

            def own_exp(k):
                b, m, l = steps[k]
                i = k % 2
                if not fresh[k]:
                    a.wait_ge(s["side_capped"], shares[k] + 1)
                if k >= 2:
                    a.wait_ge(s["factor_squared"], 2 * k - 2)
                a.activation(EU[:, i, :], kbuf[:, shares[k] % 2, :], ACT.Exp, bias=ul[:, l, m:m + 1]).then_inc(s["own_exp_ready"], 1)
                a.wait_ge(s["own_exp_ready"], k + 1)
                a.activation(EU[:, i, :], EU[:, i, :], ACT.Copy, scale=kappa[:, l, m, b:b + 1]).then_inc(s["own_exp_scaled"], 1)

            def seed(k):
                i = k % 2
                a.wait_ge(s["denominator_floored"], k + 1)
                a.activation(F[:, i, 0, :].bitcast(i32), G[:, i, 0, :].bitcast(i32), ACT.Copy, scale=-1.0, bias=SEED).then_inc(s["seed_ready"], 1)

            def squares(k):
                i = k % 2
                a.wait_ge(s["numerator_seeded"], k + 1)
                for (sl, tt, _), dst in zip(factors, (F[:, i, 1, :], F[:, i, 0, :])):
                    a.activation(dst, EU[:, i, :], ACT.Square, scale=-sl, bias=sl + tt).then_inc(s["factor_squared"], 1)

            def tanh_x(b, m):
                if m == 0:
                    a.wait_ge(s["channels_loaded"], 16 * (b + 1))
                a.activation(xTb[:, m, :], xTb[:, m, :], ACT.Tanh, scale=0.5).then_inc(s["gate_tanh_ready"], 1)

            def slot(k):
                if k >= 2:
                    squares(k - 2)
                if fresh[k]:
                    exponentials(shares[k])
                own_exp(k)
                if k >= 1:
                    seed(k - 1)
                if steps[k][2] == 0:
                    tanh_x(steps[k][0], steps[k][1])

            def split_base(b, ms=range(CT)):
                for m in ms:
                    a.wait_ge(s["input_ready"], 4 * b + m + 1)
                    if b > 0:
                        a.wait_ge(s["gate_up_ready"], PAIRS * b)
                    a.activation(base_hi[:, m, :], xTb[:, m, :], ACT.Copy).then_inc(s["input_high"], 1)

            a.wait_ge(s["mixing_scales_ready"], 3)
            slot(0)
            compact(0, gu_u, gp_i, 1)
            a.wait_ge(s["gate_up_scales_loaded"], 16)
            a.activation(gu_a, gs_h, ACT.Copy, scale=4096.0).then_inc(s["scales_high"], 1)
            sign_carry(0)
            slot(1)
            for k in range(2, 7):
                if fresh[k]:
                    exponentials(shares[k])
                sign_carry(k - 1)
                squares(k - 2)
                own_exp(k)
                seed(k - 1)
                if steps[k][2] == 0:
                    tanh_x(steps[k][0], steps[k][1])
                if k == 2:
                    compact(1, dn_u, dp_i, 3)
                if k == 3:
                    a.wait_ge(s["words_packed"], 2)
                    a.wait_ge(s["down_scales_loaded"], 16)
                    a.activation(dn_a, ds_h, ACT.Copy, scale=16384.0).then_inc(s["scales_high"], 1)
                    a.wait_ge(s["slopes_summed"], 1)
                    a.activation(ts[0:TILES, 1, 0:SLICE], ts[0:TILES, 0, 0:SLICE], ACT.Sign).then_inc(s["slope_signs_ready"], 1)
                if k == 5:
                    split_base(0)

            def rows(t, first=True, second=True, third=True, mixes=(None, None, None)):
                c, c1, c2 = t % TC, (t - 1) % TC, (t - 2) % TC
                if second:
                    a.wait_ge(s["mean_ready"], t)
                    a.activation(junk[:, 1, :], xf[:, c1, :], ACT.Square, bias=stat[:, NMEAN, c1:c1 + 1],
                                 accum_out=stat[:, VAR, c1:c1 + 1]).then_inc(s["deviations_summed"], 1)
                if first:
                    a.wait_ge(s["y_ready"], t + 1)
                    a.activation(junk[:, 0, :], ps[:, Y0 + c, :], ACT.Square, accum_out=stat[:, SSQ, c:c + 1]).then_inc(s["y_squares_summed"], 1)
                if third:
                    a.wait_ge(s["beta_applied"], t - 1)
                    if t > 2:
                        a.wait_ge(s["tile_scores_ready"], t - 2)
                    a.activation(sgn[:, :], xf[:, c2, :], ACT.Sign).then_inc(s["signs_ready"], 1)
                if second:
                    a.wait_ge(s["variance_root"], t)
                    a.activation(stat[:, NBIAS, c1:c1 + 1], stat[:, NMEAN, c1:c1 + 1], ACT.Copy, scale=stat[:, RSTD, c1:c1 + 1]).then_inc(s["shift_ready"], 1)
                    a.wait_ge(s["shift_ready"], t)
                    a.wait_ge(s["residual_added"], t)
                    a.activation(xf[:, c1, :], xf[:, c1, :], ACT.Identity, scale=stat[:, RSTD, c1:c1 + 1],
                                 bias=stat[:, NBIAS, c1:c1 + 1]).then_inc(s["normalised"], 1)
                if first and mixes[1] is not None:
                    seed(mixes[1])
                if first and mixes[0] is not None and fresh[mixes[0]]:
                    exponentials(shares[mixes[0]])
                if first:
                    a.wait_ge(s["x1_ready"], t + 1)
                    a.activation(Tg[:, c % 2, :], z[:, t, :], ACT.Tanh, scale=0.5).then_inc(s["x1_tanh_ready"], 1)
                    if mixes[2] is not None:
                        squares(mixes[2])
                    a.wait_ge(s["mixed_ready"], t + 1)
                    a.activation(stat[:, NMEAN, c:c + 1], stat[:, SUM, c:c + 1], ACT.Copy, scale=-1.0 / C).then_inc(s["mean_ready"], 1)

            def q1_rows(b):
                for c in range(TC):
                    t = TC * b + c
                    a.wait_ge(s["quotient_turned"], t + 1)
                    if b > 0:
                        a.wait_ge(s["slice_ready"], b)
                    a.activation(xf[:, c, :].rearrange("p (r q m) -> p m q r", q=2, m=CT),
                                 ps[:, Y0 + c, :].rearrange("p (m q r) -> p m q r", m=CT, q=2),
                                 ACT.Copy).then_inc(s["quotient_rows"], 1)

            def copy_chosen(b):
                a.wait_ge(s["chosen_turned"], TC * (b + 1))
                if b == 0:
                    a.wait_ge(s["quotient_ready"], len(steps))
                a.activation(ohT[:, TC * P * b:TC * P * (b + 1)], chosen_bank(b), ACT.Copy).then_inc(s["chosen_copied"], 1)

            def copy_tables(pairs):
                for i in pairs:
                    a.wait_ge(s["tables_looked_up"], i + 1)
                    a.wait_ge(s["input_low"], B * CT)
                    both = ps[:, table_bank(i), :].rearrange("p (c k) -> p c k", c=2)
                    for dst, cols in ((looked, slice(0, KNOTS)), (looked_s, slice(KNOTS, 2 * KNOTS))):
                        a.activation(dst[:, 2 * KNOTS * i:2 * KNOTS * (i + 1)].rearrange("p (c k) -> p c k", c=2),
                                     both[:, :, cols], ACT.Copy).then_inc(s["tables_copied"], 1)

            def mix(b, i):
                scan, weigh, _ = mixing(b, i)
                if scan is not None:
                    if fresh[scan] and i < PAIRS:
                        exponentials(shares[scan])
                    own_exp(scan)
                if weigh is not None and i < PAIRS:
                    seed(weigh)
                if weigh is not None and steps[weigh][2] == 0:
                    tanh_x(*steps[weigh][:2])

            def gate_tanh(b, j):
                e = PAIRS * b + j
                a.wait_ge(s["gate_up_ready"], e + 1)
                if j >= 2:
                    a.wait_ge(s["hidden_low"], e - 1)
                elif b > 0:
                    a.wait_ge(s["hidden_low"], PAIRS * b)
                    a.wait_ge(s["mixed_ready"], TC * b)
                a.activation(Tg[:, j % 2, :], ps[:, 2 * (j % 2), :], ACT.Tanh, scale=2.0).then_inc(s["silu_tanh_ready"], 1)

            for b in range(B):
                mix(b, -1)
                gate_tanh(b, 0)
                for j in range(PAIRS):
                    e = PAIRS * b + j
                    early = mixing(b, j) == (None, None, None) and j + 1 < PAIRS
                    if mixing(b, j)[2] is not None:
                        squares(mixing(b, j)[2])
                    if early:
                        gate_tanh(b, j + 1)
                    a.wait_ge(s["hidden_ready"], e + 1)
                    a.activation(h_hi[:, j, :], Tg[:, j % 2, :], ACT.Copy).then_inc(s["hidden_high"], 1)
                    if b == 0:
                        for i in unpack_with(j):
                            if i + 1 < len(unpack):
                                sign_carry(i + 1)
                    if b > 0 and j < 2:
                        rows(TC * b + j, first=False, second=j == 0)
                    mix(b, j)
                    if not early and j + 1 < PAIRS:
                        gate_tanh(b, j + 1)
                    if j == (4 if b == 0 else GATHER_AT + 1):
                        q1_rows(b)
                    if b == B - 1 and j == 6:
                        for i in range(B - 1):
                            copy_chosen(i)
                    if b == B - 1 and j == 8:
                        copy_tables(range(4))
                    if b == B - 1 and j == 10:
                        copy_tables(range(4, 6))
                for c in range(TC):
                    rows(TC * b + c, second=c > 0, third=c > 1, mixes=mixing(b, PAIRS + c))
                    mix(b, PAIRS + c)
                    split_base(b + 1, splits(b, PAIRS + c))
            rows(NCH, first=False)
            rows(NCH + 1, first=False, second=False)
            copy_chosen(B - 1)
            copy_tables([2 * (B - 1), 2 * B - 1])
            for i, c in enumerate(by_act):
                a.wait_ge(s["spline_ready"], c // TC + 1)
                if i >= 2:
                    a.wait_ge(s["pool_finished"], by_act[i - 2] + 1)
                for j in range(SLICE):
                    last = a.activation(Tg[:, i % 2, j::SLICE], onehot[:, c, :], ACT.Copy, scale=xs[:, c, j:j + 1])
                last.then_inc(s["act_product_ready"], 1)

        @block.tensor
        def _(pe):
            pe.wait_ge(s["slope_diagonal_ready"], 1)
            pe.wait_ge(s["ones_set"], 1)
            nc.tensor.matmul(ps[:, TR0, :], ones[:, :], sgn[0:TILES, :], start=True, stop=True).then_inc(s["slope_signs_spread"], 1)
            pe.wait_ge(s["identity_ready"], 3)
            def product(j, part, m):
                cols = slice(2 * P * j + P * part, 2 * P * j + P * (part + 1))
                dst = ps[:, 2 * (j % 2) + part, :]
                nc.tensor.matmul(dst, wg_hi[:, m, cols], base_hi[:, m, :], start=(m == 0), stop=False)
                nc.tensor.matmul(dst, wg_hi[:, m, cols], base_lo[:, m, :], start=False, stop=False)
                return nc.tensor.matmul(dst, wg_lo[:, m, cols], base_hi[:, m, :], start=False, stop=(m == CT - 1))

            def turn_chosen(b):
                pe.wait_ge(s["tile_chosen"], b + 1 + (b == B - 1))
                for c in range(TC):
                    nc.tensor.transpose(chosen_bank(b)[:, c * P:(c + 1) * P], onehot[:, TC * b + c, :], identh[:, :]).then_inc(s["chosen_turned"], 1)

            def look_up(pairs):
                for i in pairs:
                    pe.wait_ge(s["chosen_copied"], i // 2 + 1)
                    for c in range(2 * i, 2 * i + 2):
                        for part in range(3):
                            last = nc.tensor.matmul(ps[:, table_bank(i), 2 * KNOTS * (c % 2):2 * KNOTS * (c % 2 + 1)],
                                                    ohT[:, c * P:(c + 1) * P], tab_part[:, part, :], start=(part == 0), stop=(part == 2))
                    last.then_inc(s["tables_looked_up"], 1)

            for b in range(B):
                for j in range(PAIRS):
                    e = PAIRS * b + j
                    if b == 0:
                        pe.wait_ge(s["weights_low"], j + 1)
                        pe.wait_ge(s["weights_high"], j + 1)
                    if j >= 2:
                        pe.wait_ge(s["hidden_ready"], e - 1)
                    elif b > 0:
                        pe.wait_ge(s["hidden_ready"], PAIRS * b)
                    if j == 0 and b > 0:
                        for m in range(CT):
                            pe.wait_ge(s["input_low"], CT * b + m + 1)
                            for jj in range(2):
                                for part in range(2):
                                    last = product(jj, part, m)
                                if m == CT - 1:
                                    last.then_inc(s["gate_up_ready"], 1)
                    elif j > 1 or b == 0:
                        for part in range(2):
                            for m in range(CT):
                                if b == j == part == 0:
                                    pe.wait_ge(s["input_low"], m + 1)
                                last = product(j, part, m)
                        last.then_inc(s["gate_up_ready"], 1)
                    if j == (4 if b == 0 else 1):
                        pe.wait_ge(s["quotient_ready"], 8 * (b + 1))
                        for c in range(TC):
                            if b == 0:
                                pe.wait_ge(s["slope_signs_copied"], 1)
                            else:
                                pe.wait_ge(s["x1_ready"], TC * (b - 1) + c + 1)
                            for m in range(CT):
                                last = nc.tensor.transpose(ps[:, Y0 + c, P * m:P * (m + 1)],
                                                           q1[:, m, P * c:P * (c + 1)], ident[:, :])
                            last.then_inc(s["quotient_turned"], 1)
                    if b == B - 1 and j == 5:
                        pe.wait_ge(s["quotient_rows"], NCH)
                        for i in range(B - 1):
                            turn_chosen(i)
                    if b == B - 1 and j == 8:
                        pe.wait_ge(s["tables_in_parts"], 3)
                        pe.wait_ge(s["chosen_copied"], B - 1)
                        look_up(range(4))
                    if b == B - 1 and j == 10:
                        pe.wait_ge(s["tables_copied"], 4)
                        look_up(range(4, 6))
                if b == 0:
                    pe.wait_ge(s["weights_low"], PAIRS + 6)
                    pe.wait_ge(s["weights_high"], PAIRS + 6)
                for c in range(TC):
                    t = TC * b + c
                    pe.wait_ge(s["quotient_rows"], t + 1)
                    if b == B - 1:
                        pe.wait_ge(s["tables_copied"], 8 if c < 2 else 12)
                    dst = ps[:, Y0 + c, :]
                    for j in range(PAIRS):
                        if c == 0:
                            pe.wait_ge(s["hidden_low"], PAIRS * b + j + 1)
                        rows = slice(P * c, P * (c + 1))
                        nc.tensor.matmul(dst, h_hi[:, j, rows], wd_hi[:, j, :], start=(j == 0), stop=False)
                        nc.tensor.matmul(dst, h_hi[:, j, rows], wd_lo[:, j, :], start=False, stop=False)
                        last = nc.tensor.matmul(dst, h_lo[:, j, rows], wd_hi[:, j, :], start=False, stop=(j == PAIRS - 1))
                    last.then_inc(s["y_ready"], 1)
            turn_chosen(B - 1)
            look_up([2 * (B - 1), 2 * B - 1])
            pe.wait_ge(s["ranges_updated"], 2 * B)
            for i in range(2):
                nc.tensor.transpose(ps[0:TILES, 3, P * i:P * (i + 1)], run[:, i, :], ident[:, :]).then_inc(s["ranges_turned"], 1)
            pe.wait_ge(s["ranges_in_parts"], 3)
            for c in range(NCH):
                last = nc.tensor.matmul(ps[:, Y0, 9 * c:9 * (c + 1)], ohT[:, c * P:(c + 1) * P],
                                        look_part[:, :, :].rearrange("p a b -> p (a b)"), start=True, stop=True)
            last.then_inc(s["range_looked_up"], 1)

        @block.vector
        def _(v):
            count = {}

            def await_step(sem, n):
                count[sem] = count.get(sem, 0) + n
                v.wait_ge(sem, count[sem])

            def link(ins, sem=s["chain_step"]):
                ins.then_inc(sem, 1)
                await_step(sem, 1)

            def code_bits(i):
                tiles, nt, n, _, _, _ = unpack[i]
                if i >= PAIRS:
                    v.wait_ge(s["words_packed"], 2)
                if i >= NBUF:
                    v.wait_ge(s["weights_low"], i - NBUF + 1)
                    v.wait_ge(s["weights_high"], i - NBUF + 1)
                for m, (src, shift) in enumerate(tiles):
                    left = 9 - shift
                    nc.vector.tensor_scalar(code[i % NBUF][:, m * n:(m + 1) * n], src, abs(left), 0x1E00,
                                            ALU.logical_shift_left if left > 0 else ALU.logical_shift_right,
                                            ALU.bitwise_and).then_inc(s["code_placed"], 1)

            def products(i):
                _, nt, n, (sa, _, _), (hi, _), _ = unpack[i]
                v.wait_ge(s["sign_carried"], i + 1)
                bits = code[i % NBUF][:, 0:nt * n]
                nc.vector.tensor_scalar(bits, bits, 0x8FFF, None, ALU.bitwise_and).then_inc(s["value_masked"], 1)
                v.wait_ge(s["value_masked"], i + 1)
                v.wait_ge(s["scales_low"], 1 if i < PAIRS else 2)
                nc.vector.tensor_tensor(hi, value(i), factor(i, sa), ALU.mult).then_inc(s["weights_high"], 1)

            def exponentials(n):
                v.wait_ge(s["side_loaded_%d" % (n % 2)], 16 * (n // 2 + 1))
                if n > 0:
                    v.wait_ge(s["exp_value_ready"], n)
                    v.wait_ge(s["forward_scanned"], 2 * last_of[n - 1] + 2)
                nc.vector.tensor_scalar(E[:, :], kbuf[:, n % 2, :], 30.0, None, ALU.min).then_inc(s["side_capped"], 1)

            def scans(k):
                b, m, l = steps[k]
                i = k % 2
                d = decay[:, l, m, b:b + 1]
                v.wait_ge(s["exp_ready"], shares[k] + 1)
                if k >= 2:
                    v.wait_ge(s["quotient_ready"], k - 1)
                for dst, src in enumerate((E, ekv)):
                    if dst == 1:
                        v.wait_ge(s["exp_value_ready"], shares[k] + 1)
                    nc.vector.tensor_tensor_scan(F[:, i, dst, :], d.broadcast_to([P, T]), src[:, :], 0.0,
                                                 ALU.mult, ALU.add).then_inc(s["forward_scanned"], 1)
                for dst in range(2):
                    v.wait_ge(s["forward_scanned"], 2 * k + dst + 1)
                    nc.vector.tensor_scalar(G[:, i, dst, T - 1:T], F[:, i, dst, T - 1:T], kappa[:, l, m, b:b + 1], None,
                                            ALU.mult).then_inc(s["edge_set"], 1)
                for dst in range(2):
                    v.wait_ge(s["edge_set"], 2 * k + dst + 1)
                    nc.vector.tensor_tensor_scan(rev(G[:, i, dst, 0:T - 1]), d.broadcast_to([P, T - 1]),
                                                 rev(F[:, i, dst, 0:T - 1]), G[:, i, dst, T - 1:T],
                                                 ALU.mult, ALU.add).then_inc(s["backward_scanned"], 1)

            def own_weight(k):
                b, m, l = steps[k]
                i = k % 2
                v.wait_ge(s["own_exp_scaled"], k + 1)
                v.wait_ge(s["backward_scanned"], 2 * k + 2)
                nc.vector.scalar_tensor_tensor(F[:, i, 1, :], EU[:, i, :], cap[:, l, m, b:b + 1], vs[:, shares[k] % 2, :],
                                               ALU.min, ALU.mult).then_inc(s["own_value_ready"], 1)

            def add_own(k):
                if k is not None:
                    b, m, l = steps[k]
                    i = k % 2
                    nc.vector.scalar_tensor_tensor(G[:, i, 0, :], EU[:, i, :], cap[:, l, m, b:b + 1], G[:, i, 0, :],
                                                   ALU.min, ALU.add).then_inc(s["denominator_summed"], 1)

            def floor_under(k):
                if k is not None:
                    b, m, l = steps[k]
                    i = k % 2
                    v.wait_ge(s["denominator_summed"], k + 1)
                    nc.vector.tensor_scalar(G[:, i, 0, :], G[:, i, 0, :], floor[:, l, m, b:b + 1], None, ALU.max).then_inc(s["denominator_floored"], 1)

            def first_factor(k):
                if k is not None:
                    i = k % 2
                    v.wait_ge(s["numerator_seeded"], k + 1)
                    v.wait_ge(s["factor_squared"], 2 * k + 1)
                    nc.vector.scalar_tensor_tensor(G[:, i, 1, :], F[:, i, 1, :], factors[0][2], G[:, i, 1, :],
                                                   ALU.add, ALU.mult).then_inc(s["first_factor_applied"], 1)

            def second_factor(k):
                if k is not None:
                    b, m, l = steps[k]
                    i = k % 2
                    v.wait_ge(s["first_factor_applied"], k + 1)
                    v.wait_ge(s["factor_squared"], 2 * k + 2)
                    if l == 1 and b > 0:
                        v.wait_ge(s["quotient_turned"], TC * b)
                    nc.vector.scalar_tensor_tensor(q1[:, m, :] if l else G[:, i, 1, :], F[:, i, 0, :], factors[1][2],
                                                   G[:, i, 1, :], ALU.add, ALU.mult).then_inc(s["quotient_ready"], 1)

            def gate_input(k):
                if k is not None and steps[k][2] == 0:
                    b, m, _ = steps[k]
                    v.wait_ge(s["quotient_ready"], k + 1)
                    v.wait_ge(s["gate_tanh_ready"], based_at[(b, m)] + 1)
                    nc.vector.scalar_tensor_tensor(xTb[:, m, :], xTb[:, m, :], 1.0, G[:, k % 2, 1, :], ALU.add, ALU.mult).then_inc(s["input_ready"], 1)

            def weigh_and_divide(w, r):
                add_own(w)
                first_factor(r)
                floor_under(w)
                second_factor(r)
                gate_input(r)

            def slot(k):
                if fresh[k]:
                    exponentials(shares[k])
                if k >= 1:
                    own_weight(k - 1)
                weigh_and_divide(k - 1 if k >= 1 else None, k - 2 if k >= 2 else None)
                scans(k)

            v.wait_ge(s["numbers_made"], 1)
            nc.vector.tensor_scalar(shq[:, 1:2], shq[:, 0:1], 6, 4, ALU.logical_shift_right, ALU.logical_shift_left).then_inc(s["shifts_set"], 1)
            nc.vector.tensor_scalar(shq[:, 2:3], shq[:, 0:1], 4, 2, ALU.logical_shift_right, ALU.logical_shift_left).then_inc(s["shifts_set"], 1)
            v.wait_ge(s["decay_inputs_loaded"], 16 * 5)
            nc.vector.tensor_reduce(tf[:, 0, :], Tg[:, 1, :].rearrange("p (b t) -> p b t", b=B), axis=AX, op=ALU.add).then_inc(s["cond_summed"], 1)
            v.wait_ge(s["cond_tanh_ready"], 1)
            v.wait_ge(s["rate_exp_ready"], 2)
            nc.vector.tensor_scalar(tf[:, 2, :], tf[:, 1, :], 0.25, 0.75, ALU.mult, ALU.add).then_inc(s["decay_scale_ready"], 1)
            nc.vector.tensor_scalar(sc[:, :], tf[:, 1, :], 0.05, 0.45, ALU.mult, ALU.add).then_inc(s["mixing_scales_ready"], 1)
            v.wait_ge(s["decay_scale_ready"], 1)
            flat = [t[:, :, :, :].rearrange("p l m b -> p (l m b)") for t in (decay, kappa, cap, floor)]
            link(nc.vector.tensor_tensor(decay[:, :, :, :].rearrange("p l m b -> p (l m) b"),
                                         wl[:, :, :].rearrange("p l m -> p (l m)").unsqueeze(2).broadcast_to([P, 2 * CT, B]),
                                         tf[:, 2, :].unsqueeze(1).broadcast_to([P, 2 * CT, B]), ALU.mult))
            link(nc.vector.tensor_scalar(flat[0], flat[0], 1.0 - 2.0 ** -24, None, ALU.min))
            link(nc.vector.tensor_scalar(flat[1], flat[0], -1.0, 1.0, ALU.mult, ALU.add))
            link(nc.vector.scalar_tensor_tensor(flat[1], flat[0], 1.0, flat[1], ALU.add, ALU.mult))
            link(nc.vector.reciprocal(flat[1], flat[1]))
            nc.vector.tensor_scalar(flat[2], flat[1], E30, None, ALU.mult).then_inc(s["mixing_scales_ready"], 1)
            nc.vector.tensor_scalar(flat[3], flat[1], 1e-8, None, ALU.mult).then_inc(s["mixing_scales_ready"], 1)
            v.wait_ge(s["mixing_scales_ready"], 3)
            slot(0)
            v.wait_ge(s["shifts_set"], 2)
            v.wait_ge(s["gate_up_codes_loaded"], 16)
            nc.vector.tensor_scalar(gp_i, gp_i, shq[:, 1:2], None, ALU.logical_shift_right).then_inc(s["words_shifted"], 1)
            exponentials(1)
            own_weight(0)
            v.wait_ge(s["words_packed"], 1)
            code_bits(0)
            weigh_and_divide(0, None)
            scans(1)
            v.wait_ge(s["gate_up_scales_loaded"], 16)
            v.wait_ge(s["scales_high"], 1)
            nc.vector.scalar_tensor_tensor(gu_b, gs_h, 4096.0, gu_a, ALU.mult, ALU.subtract).then_inc(s["scales_low"], 1)
            v.wait_ge(s["down_codes_loaded"], 16)
            nc.vector.tensor_scalar(dp_i[:, 0:FULL * C], dp_i[:, 0:FULL * C], shq[:, 1:2], None, ALU.logical_shift_right).then_inc(s["words_shifted"], 1)
            nc.vector.tensor_scalar(dp_i[:, FULL * C:], dp_i[:, FULL * C:], shq[:, 2:3], None, ALU.logical_shift_right).then_inc(s["words_shifted"], 1)
            for k in range(2, 7):
                if fresh[k]:
                    exponentials(shares[k])
                code_bits(k - 1)
                own_weight(k - 1)
                products(k - 2)
                weigh_and_divide(k - 1, k - 2)
                scans(k)
                if k == 3:
                    v.wait_ge(s["late_inputs_loaded"], 16 * 3)
                    nc.vector.tensor_reduce(ts[0:TILES, 0, 0:SLICE], Tg[0:TILES, 0, 0:SLICE * GRID].rearrange("p (j g) -> p j g", g=GRID),
                                            axis=AX, op=ALU.add).then_inc(s["slopes_summed"], 1)
                if k == 4:
                    v.wait_ge(s["slope_signs_spread"], 1)
                    nc.vector.tensor_copy(sig[:, :], ps[:, TR0, :]).then_inc(s["slope_signs_copied"], 1)
                if k == 5:
                    v.wait_ge(s["scales_high"], 2)
                    nc.vector.scalar_tensor_tensor(dn_b, ds_h, 16384.0, dn_a, ALU.mult, ALU.subtract).then_inc(s["scales_low"], 1)

            def rows(t, first=True, second=True, third=True, mixes=(None, None, None), start=None):
                c, c1, c2 = t % TC, (t - 1) % TC, (t - 2) % TC
                scan, w, r = mixes
                if second:
                    v.wait_ge(s["deviations_summed"], t)
                    nc.vector.tensor_scalar(stat[:, VAREPS, c1:c1 + 1], stat[:, VAR, c1:c1 + 1], 1.0 / C, 1e-5,
                                            ALU.mult, ALU.add).then_inc(s["variance_ready"], 1)
                if third:
                    v.wait_ge(s["gamma_applied"], t - 1)
                    nc.vector.tensor_tensor(xf[:, c2, :], xf[:, c2, :], bet[:, :], ALU.add).then_inc(s["beta_applied"], 1)
                if first:
                    v.wait_ge(s["y_squares_summed"], t + 1)
                    nc.vector.tensor_scalar(stat[:, SSQEPS, c:c + 1], stat[:, SSQ, c:c + 1], 1.0 / C, 1e-6 / 64.0,
                                            ALU.mult, ALU.add).then_inc(s["y_mean_square"], 1)
                if start:
                    start()
                if scan is not None and fresh[scan] and w is not None:
                    own_weight(w)
                add_own(w)
                if third:
                    v.wait_ge(s["signs_ready"], t - 1)
                    nc.vector.tensor_tensor(sgn[:, :], sgn[:, :], sig[:, :], ALU.mult).then_inc(s["signs_matched"], 1)
                floor_under(w)
                if first:
                    v.wait_ge(s["y_root"], t + 1)
                    v.wait_ge(s["first_rows_loaded" if t < TC else "rows_loaded"], 16 if t < TC else 16 * (B - 1))
                    nc.vector.scalar_tensor_tensor(z[:, t, :], ps[:, Y0 + c, :], stat[:, RS, c:c + 1], z[:, t, :],
                                                   ALU.mult, ALU.add).then_inc(s["x1_ready"], 1)
                if third:
                    v.wait_ge(s["signs_matched"], t - 1)
                    nc.vector.tensor_reduce(ts[:, c2, :], sgn[:, :].rearrange("p (t j) -> p t j", j=SLICE), axis=AX, op=ALU.add).then_inc(s["tile_scores_ready"], 1)
                if not first:
                    first_factor(r)
                if first:
                    v.wait_ge(s["x1_tanh_ready"], t + 1)
                    v.wait_ge(s["quotient_rows"], t + 1)
                    nc.vector.scalar_tensor_tensor(xf[:, c, :], Tg[:, c % 2, :], 1.0, xf[:, c, :], ALU.add, ALU.mult,
                                                   accum_out=stat[:, SUM, c:c + 1]).then_inc(s["mixed_ready"], 1)
                    first_factor(r)
                second_factor(r)
                gate_input(r)
                if scan is not None:
                    scans(scan)

            def split_base(b, ms):
                for m in ms:
                    v.wait_ge(s["input_high"], CT * b + m + 1)
                    nc.vector.tensor_tensor(base_lo[:, m, :], xTb[:, m, :], base_hi[:, m, :], ALU.subtract).then_inc(s["input_low"], 1)

            def choose(b, lo=0, hi=TC):
                n = hi - lo
                oh = onehot[:, TC * b + lo:TC * b + hi, :]
                tsv = ts[:, lo:hi, :].rearrange("p c (k i) -> p (c k) i", i=8)
                cmv = comp[:, lo:hi, :].rearrange("p c (k i) -> p (c k) i", i=8)
                csv = cs[:, lo:hi, :].rearrange("p c k -> p (c k)")
                v.wait_ge(s["tile_scores_ready"], TC * b + hi)
                link(nc.vector.tensor_reduce(csv, tsv, axis=AX, op=ALU.add))
                link(nc.vector.scalar_tensor_tensor(cmv, csv.unsqueeze(2).broadcast_to([P, n * CLUSTERS, 8]), 2048.0,
                                                    rank[:, lo:hi, :].rearrange("p c (k i) -> p (c k) i", i=8), ALU.mult, ALU.add))
                link(nc.vector.scalar_tensor_tensor(comp[:, lo:hi, :], ts[:, lo:hi, :], 8.0, comp[:, lo:hi, :], ALU.mult, ALU.add))
                link(nc.vector.tensor_reduce(best[:, lo:hi], comp[:, lo:hi, :], axis=AX, op=ALU.max))
                link(nc.vector.tensor_tensor(oh, comp[:, lo:hi, :], best[:, lo:hi].unsqueeze(2).broadcast_to([P, n, TILES]), ALU.is_equal), s["tile_chosen"])

            def gather(b, lo=TC):
                oh = onehot[:, TC * b:TC * (b + 1), :]
                xb = xs[:, TC * b:TC * (b + 1), :]
                if lo < TC:
                    sel = xf[:, lo:TC, :].rearrange("p c (t j) -> p (c t) j", j=SLICE)
                    link(nc.vector.tensor_tensor(sel, sel, oh[:, lo:TC, :].rearrange("p c t -> p (c t)").unsqueeze(2)
                                                 .broadcast_to([P, (TC - lo) * TILES, SLICE]), ALU.mult))
                v.wait_ge(s["slice_selected"], b + 1)
                nc.vector.tensor_reduce(xb, xf[:, :, :].rearrange("p c (t j) -> p c j t", j=SLICE),
                                        axis=AX, op=ALU.add).then_inc(s["slice_ready"], 1)

            def ranges(b):
                oh = onehot[:, TC * b:TC * (b + 1), :]
                xb = xs[:, TC * b:TC * (b + 1), :]
                link(nc.vector.tensor_scalar(ts[:, :, :], oh, -BIG, BIG, ALU.mult, ALU.add))
                v.wait_ge(s["slice_ready"], b + 1)
                ops = (ALU.min, ALU.max)
                for i, op in enumerate(ops):
                    nc.vector.tensor_reduce(tmn[:, i, :], xb, axis=AX, op=op).then_inc(s["range_step"], 1)
                await_step(s["range_step"], 2)
                for i, buf in enumerate((comp, cand)):
                    nc.vector.tensor_tensor(buf[:, :, :], oh, tmn[:, i, :].unsqueeze(2).broadcast_to([P, TC, TILES]), ALU.mult).then_inc(s["range_step"], 1)
                await_step(s["range_step"], 2)
                for i, buf in enumerate((comp, cand)):
                    nc.vector.tensor_tensor(buf[:, :, :], buf[:, :, :], ts[:, :, :], (ALU.add, ALU.subtract)[i]).then_inc(s["range_step"], 1)
                await_step(s["range_step"], 2)
                for i, buf in enumerate((comp, cand)):
                    nc.vector.tensor_reduce(mkv[:, i, :], buf[:, :, :].rearrange("p c t -> p t c"), axis=AX, op=ops[i]).then_inc(s["range_step"], 1)
                await_step(s["range_step"], 2)
                for i in range(2):
                    nc.vector.tensor_tensor(run[:, i, :], run[:, i, :], mkv[:, i, :], ops[i]).then_inc(s["ranges_updated"], 1)
                v.wait_ge(s["ranges_updated"], 2 * (b + 1))

            def mix(b, i):
                scan, weighs, divides = mixing(b, i)
                if weighs is not None and scan is not None and fresh[scan]:
                    own_weight(weighs)
                weigh_and_divide(weighs, divides)
                if scan is not None:
                    scans(scan)

            def mix_first(b, i):
                scan, weighs, _ = mixing(b, i)
                if scan is not None and fresh[scan]:
                    exponentials(shares[scan])
                elif weighs is not None:
                    own_weight(weighs)

            def three_parts(full, rest, parts, sem):
                src = full
                for i in range(3):
                    nc.vector.tensor_copy(parts[:, i, :], src).then_inc(sem, 1)
                    if i < 2:
                        await_step(sem, 1)
                        link(nc.vector.tensor_tensor(rest, src, parts[:, i, :], ALU.subtract))
                        src = rest

            v.wait_ge(s["ranks_ready"], 2)
            v.wait_ge(s["ranges_started"], 2)
            for b in range(B):
                mix_first(b, -1)
                mix(b, -1)
                for j in range(PAIRS):
                    e = PAIRS * b + j
                    v.wait_ge(s["silu_tanh_ready"], e + 1)
                    nc.vector.scalar_tensor_tensor(Tg[:, j % 2, :], Tg[:, j % 2, :], 1.0, ps[:, 2 * (j % 2), :], ALU.add, ALU.mult).then_inc(s["silu_ready"], 1)
                    mix_first(b, j)
                    v.wait_ge(s["silu_ready"], e + 1)
                    nc.vector.tensor_tensor(Tg[:, j % 2, :], Tg[:, j % 2, :], ps[:, 2 * (j % 2) + 1, :], ALU.mult).then_inc(s["hidden_ready"], 1)
                    if b > 0 and j < 2:
                        rows(TC * b + j, first=False, second=j == 0, mixes=mixing(b, j))
                    if b > 0 and j == 2:
                        choose(b - 1)
                    if b > 0 and j == GATHER_AT:
                        gather(b - 1)
                    if b == B - 1 and 5 <= j < 5 + B - 1:
                        ranges(j - 5)
                    if b == B - 1 and j == 4:
                        v.wait_ge(s["spline_tables_loaded"], 48)
                        three_parts(tab, tab_rest, tab_part, s["tables_in_parts"])
                    if b == 0:
                        for i in unpack_with(j):
                            if i + 1 < len(unpack):
                                code_bits(i + 1)
                            products(i)
                    if b == 0 or j >= 2:
                        mix(b, j)
                for c in range(TC):
                    rows(TC * b + c, second=c > 0, third=c > 1, mixes=mixing(b, PAIRS + c),
                         start=lambda: mix_first(b, PAIRS + c))
                    if c > 0:
                        split_base(b + 1, splits(b, PAIRS + c - 1))
                    if c == TC - 1:
                        split_base(b + 1, splits(b, PAIRS + c))
            rows(NCH, first=False)
            choose(B - 1, 0, TC - 1)
            rows(NCH + 1, first=False, second=False)
            choose(B - 1, TC - 1, TC)
            gather(B - 1, TC - 1)
            ranges(B - 1)

            v.wait_ge(s["ranges_turned"], 2)
            nc.vector.tensor_reduce(lookt[:, 0:1], ps[0:TILES, 3, 0:P], axis=AX, op=ALU.min).then_inc(s["ranges_reduced"], 1)
            nc.vector.tensor_reduce(lookt[:, 1:2], ps[0:TILES, 3, P:2 * P], axis=AX, op=ALU.max).then_inc(s["ranges_reduced"], 1)
            v.wait_ge(s["ranges_reduced"], 2)
            three_parts(lookt[:, :], lookr[:, :], look_part, s["ranges_in_parts"])
            v.wait_ge(s["range_looked_up"], 1)
            lkp = ps[:, Y0, 0:9 * NCH].rearrange("p (c q i) -> p c q i", q=3, i=3)
            link(nc.vector.tensor_copy(lk[:, :, :], lkp[:, :, 0, :]))
            link(nc.vector.tensor_tensor(lk[:, :, :], lk[:, :, :], lkp[:, :, 1, :], ALU.add))
            link(nc.vector.tensor_tensor(lk[:, :, :], lk[:, :, :], lkp[:, :, 2, :], ALU.add))
            wide = [P, NCH, SLICE]
            nc.vector.tensor_tensor(xs[:, :, :], xs[:, :, :], lk[:, :, 0].unsqueeze(2).broadcast_to(wide), ALU.subtract).then_inc(s["offset_ready"], 1)
            link(nc.vector.tensor_tensor(rng[:, :], lk[:, :, 1], lk[:, :, 0], ALU.subtract))
            link(nc.vector.tensor_scalar(rng[:, :], rng[:, :], 1e-8, None, ALU.add))
            link(nc.vector.reciprocal(rng[:, :], rng[:, :]))
            v.wait_ge(s["offset_ready"], 1)
            link(nc.vector.tensor_tensor(xs[:, :, :], xs[:, :, :], rng[:, :].unsqueeze(2).broadcast_to(wide), ALU.mult))
            link(nc.vector.tensor_scalar(xs[:, :, :], xs[:, :, :], 0.0, 1.0 - 1e-6, ALU.max, ALU.min))
            link(nc.vector.tensor_scalar(xs[:, :, :], xs[:, :, :], float(GRID), None, ALU.mult))
            link(nc.vector.tensor_scalar(gi[:, :, :], xs[:, :, :], ROUND, -ROUND, ALU.add, ALU.add))
            link(nc.vector.tensor_tensor(gt[:, :, :], gi[:, :, :], xs[:, :, :], ALU.is_gt))
            link(nc.vector.tensor_tensor(gi[:, :, :], gi[:, :, :], gt[:, :, :], ALU.subtract))
            link(nc.vector.tensor_scalar(gi[:, :, :], gi[:, :, :], 0.0, float(GRID - 1), ALU.max, ALU.min))
            nc.vector.tensor_copy(knot[:, :], gi[:, :, :].rearrange("p c j -> p (c j)")).then_inc(s["knot_ready"], 1)
            link(nc.vector.tensor_tensor(xs[:, :, :], xs[:, :, :], gi[:, :, :], ALU.subtract))
            v.wait_ge(s["knot_ready"], 1)
            v.wait_ge(s["tables_copied"], 2 * NCH // 2)
            for q in range(B):
                n = slice(TC * SLICE * q, TC * SLICE * (q + 1))
                cols = slice(TC * KNOTS * q, TC * KNOTS * (q + 1))
                g3 = [P, TC * SLICE, GRID]
                link(nc.vector.tensor_tensor(knot_hot[:, cols].rearrange("p (n g) -> p n g", g=GRID),
                                             knot[:, n].unsqueeze(2).broadcast_to(g3),
                                             iota16[:, :].unsqueeze(1).broadcast_to(g3), ALU.is_equal))
                for i, tbl in enumerate((looked_s, looked)):
                    nc.vector.tensor_tensor(tbl[:, cols], tbl[:, cols], knot_hot[:, cols], ALU.mult).then_inc(s["knot_picked"], 1)
                await_step(s["knot_picked"], 2)
                for i, tbl in enumerate((looked_s, looked)):
                    nc.vector.tensor_reduce(bs[:, i, n], tbl[:, cols].rearrange("p (n g) -> p n g", g=GRID), axis=AX, op=ALU.add).then_inc(s["knot_summed"], 1)
                await_step(s["knot_summed"], 2)
                xsf = xs[:, TC * q:TC * (q + 1), :]
                link(nc.vector.tensor_tensor(xsf, xsf, bs[:, 0, n].rearrange("p (c j) -> p c j", j=SLICE), ALU.mult))
                link(nc.vector.tensor_tensor(xsf, xsf, bs[:, 1, n].rearrange("p (c j) -> p c j", j=SLICE), ALU.add))
                nc.vector.tensor_tensor(xsf, xsf, lk[:, TC * q:TC * (q + 1), 2].unsqueeze(2).broadcast_to([P, TC, SLICE]), ALU.mult).then_inc(s["spline_ready"], 1)
            v.wait_ge(s["spline_ready"], B)
            def product(i):
                c = by_dve[i]
                if i >= 2:
                    v.wait_ge(s["dve_finished"], i - 1)
                nc.vector.tensor_tensor(addend(i).rearrange("p (t j) -> p t j", j=SLICE),
                                        onehot[:, c, :].unsqueeze(2).broadcast_to([P, TILES, SLICE]),
                                        xs[:, c, :].unsqueeze(1).broadcast_to([P, TILES, SLICE]), ALU.mult).then_inc(s["dve_product_ready"], 1)

            def addend(i):
                return q1[:, i % 2, :]

            product(0)
            for i, c in enumerate(by_dve):
                if i + 1 < len(by_dve):
                    product(i + 1)
                v.wait_ge(s["dve_product_ready"], i + 1)
                nc.vector.tensor_tensor(z[:, c, :], z[:, c, :], addend(i), ALU.add).then_inc(s["dve_finished"], 1)


def kernel(x, fside_BxSxS_0, cond_512, L0_cond_w, L0_cond_u, L0_ffn_gate_up_packed, L0_ffn_gate_up_scales,
           L0_ffn_down_packed, L0_ffn_down_scales, L1_cond_w, L1_cond_u, L1_ffn_ln_gamma, L1_ffn_ln_beta,
           L1_ffn_spline_bases, L1_ffn_spline_slopes, L1_ffn_output_scale):
    import concourse.bacc as bacc
    from concourse.bass_utils import run_bass_kernel_spmd

    p = np.arange(P)
    q, r = p // 64, p % 64
    chan = np.stack([8 * r + 4 * q + m for m in range(CT)], 1)
    inner = [512 * (j // 4) + 8 * r + 4 * q + j % 4 for j in range(4 * FULL)]
    inner += [8 * (64 * FULL + 16 * t + p % 16) + p // 16 for t in range(REST)]
    order = np.concatenate([np.concatenate([i, i + INNER]) for i in inner])

    x = np.asarray(x)
    side = np.asarray(fside_BxSxS_0)
    gp = np.asarray(L0_ffn_gate_up_packed)
    gs = np.asarray(L0_ffn_gate_up_scales)
    dp = np.asarray(L0_ffn_down_packed)
    ds = np.asarray(L0_ffn_down_scales)
    xc = x.transpose(2, 0, 1)
    kc = side.transpose(2, 0, 1)
    arrays = {
        "xT": np.stack([xc[chan[:, m]] for m in range(CT)]),
        "kT": np.stack([kc[chan[:, m]] for m in range(CT)]),
        "x": x,
        "cond": np.asarray(cond_512),
        "w0": np.asarray(L0_cond_w)[chan], "w1": np.asarray(L1_cond_w)[chan],
        "u0": np.asarray(L0_cond_u)[chan], "u1": np.asarray(L1_cond_u)[chan],
        "gu_pack": gp[order].T[r],
        "gu_scale": gs[:, order][r // 16],
        "dn_pack": np.concatenate([dp.T[64 * b + r] for b in range(FULL)]
                                  + [dp.T[64 * FULL + 16 * t + p % 16] for t in range(REST)], 1),
        "dn_scale": np.concatenate([ds[4 * b + r // 16] for b in range(FULL)]
                                   + [ds[4 * FULL + t + 0 * p] for t in range(REST)], 1),
        "gamma": np.asarray(L1_ffn_ln_gamma), "beta": np.asarray(L1_ffn_ln_beta),
        "bases": np.asarray(L1_ffn_spline_bases), "slopes": np.asarray(L1_ffn_spline_slopes),
        "oscale": np.asarray(L1_ffn_output_scale),
    }
    nc = bacc.Bacc("TRN2", target_bir_lowering=False, num_devices=1)
    feed, args = {}, []
    for name, a in arrays.items():
        a = np.ascontiguousarray(a)
        feed[f"in_{name}"] = a
        args.append(nc.dram_tensor(f"in_{name}", a.shape, mybir.dt.from_np(a.dtype), kind="ExternalInput").ap())
    args.append(nc.dram_tensor("out_0", (B, T, C), mybir.dt.float32, kind="ExternalOutput").ap())
    build_program(nc, *args)
    res = run_bass_kernel_spmd(nc, [feed], core_ids=[0])
    return res.results[0]["out_0"]
```
